# Optimizing a Trainium2 kernel written in Bass

```python
import numpy as np
import jax
import jax.numpy as jnp

def _softmax(x, axis=-1):
    return jax.nn.softmax(x, axis=axis)

def _gelu(x):
    return jax.nn.gelu(x, approximate=True)

def _silu(x):
    return jax.nn.silu(x)

def _sigmoid(x):
    return jax.nn.sigmoid(x)

def _layernorm(x, axis=-1, eps=1e-05):
    m = jnp.mean(x, axis=axis, keepdims=True)
    v = jnp.var(x, axis=axis, keepdims=True)
    return (x - m) / jnp.sqrt(v + eps)

def _scatter_add(tgt, idx, src, axis=0):
    return tgt.at[idx].add(src)

def _segment_sum(src, seg, n):
    return jax.ops.segment_sum(src, seg, n)
kernel_name = 'mk_decoder_postln_d2_seqx_r8_ce7ea5'

def setup_inputs(seed: int=0):
    np.random.seed(seed)
    _w = jnp.asarray

    def _rec_inputs():
        import jax
        import jax.numpy as jnp
        _rk = jax.random.key(seed)
        x = -7.109e-05 + 0.9999 * jax.random.normal(jax.random.fold_in(_rk, 1), (4, 256, 256), jnp.float32)
        _lenS = 256 - jax.random.randint(jax.random.fold_in(_rk, 7), (4,), 0, max(1, 256 // 4) + 1, jnp.int32)
        _lenS2 = 256 - jax.random.randint(jax.random.fold_in(_rk, 8), (4,), 0, max(1, 256 // 4) + 1, jnp.int32)
        _ctx_512P = jax.random.normal(jax.random.fold_in(_rk, 11), (4, 16, 64), jnp.float32)
        _ctx_512c = jax.random.dirichlet(jax.random.fold_in(_rk, 511), 0.3 * jnp.ones((16,), jnp.float32), (4, 256))
        _ctx_512t = jnp.einsum('bsk,bkd->bsd', _ctx_512c, _ctx_512P)
        _ctx_512t = _ctx_512t * jax.lax.rsqrt(jnp.mean(jnp.square(_ctx_512t)) + 1e-12) * 0.953939
        ctx_512 = 2.81802e-05 + 1.00001 * (_ctx_512t + 0.3 * jax.random.normal(jax.random.fold_in(_rk, 611), (4, 256, 64), jnp.float32))
        return (x, ctx_512)
    x, ctx_512 = _rec_inputs()

    def _L0_attn_setup():
        import jax, jax.numpy as jnp
        import numpy as np
        NUM_HEADS = 16
        key = jax.random.key(seed)
        k1, k2, k3 = jax.random.split(key, 3)
        B, S, H = (2, 256, 256)
        x = jax.random.normal(k1, (B, S, H), dtype=jnp.float32)
        lim_qkv = (6.0 / (H + 3 * H)) ** 0.5
        lim_out = (6.0 / (H + H)) ** 0.5
        Wqkv = jax.random.uniform(k2, (3 * H, H), jnp.float32, -lim_qkv, lim_qkv)
        bqkv = jnp.zeros((3 * H,), jnp.float32)
        Wout = jax.random.uniform(k3, (H, H), jnp.float32, -lim_out, lim_out)
        bout = jnp.zeros((H,), jnp.float32)
        return {'x': x, 'Wqkv': Wqkv, 'bqkv': bqkv, 'Wout': Wout, 'bout': bout}
    _L0_attn_all = _L0_attn_setup()
    _L0_attn_in = {k: v for k, v in _L0_attn_all.items() if k in ('Wqkv', 'bqkv', 'Wout', 'bout')}
    del _L0_attn_all

    def _L0_xattn_setup():
        import jax, jax.numpy as jnp
        import numpy as np
        EPS = 1e-06
        IMAGE_DIMS = 256
        key = jax.random.key(seed)
        k1, k2, k3 = jax.random.split(key, 3)
        B, I, J, D = (16, 256, 256, 64)
        p = jax.random.normal(k1, (B, I, J), dtype=jnp.float32)
        k_v = jax.random.normal(k2, (B, J, D), dtype=jnp.float32)
        W_k = jax.random.normal(k3, (D, D), dtype=jnp.float32) * (1.0 / np.sqrt(D))
        b_k = jnp.zeros((D,), dtype=jnp.float32)
        ln_gamma = jnp.ones((J,), dtype=jnp.float32)
        ln_beta = jnp.zeros((J,), dtype=jnp.float32)
        return {'p': p, 'k_v': k_v, 'W_k': W_k, 'b_k': b_k, 'ln_gamma': ln_gamma, 'ln_beta': ln_beta}
    _L0_xattn_all = _L0_xattn_setup()
    _L0_xattn_in = {k: v for k, v in _L0_xattn_all.items() if k in ('W_k', 'b_k', 'ln_gamma', 'ln_beta')}
    del _L0_xattn_all

    def _L0_ffn_setup():
        import jax, jax.numpy as jnp
        import numpy as np
        EPS = 1e-08

        def rms_norm(x, eps=EPS):
            mean = jnp.mean(x, axis=-1, keepdims=True)
            var = jnp.var(x, axis=-1, keepdims=True)
            return (x - mean) / jnp.sqrt(var + eps)

        def activation_quant(x):
            s = 127.0 / jnp.max(jnp.abs(x), axis=-1, keepdims=True)
            return jnp.clip(jnp.round(s * x), -128, 127) / s

        def ternary_matmul(x, w):
            return jnp.matmul(x, jnp.sign(w).T)
        key = jax.random.key(seed)
        k0, k1, k2, k3 = jax.random.split(key, 4)
        B, S, D, H = (4, 256, 256, 1024)
        x = jax.random.normal(k0, (B, S, D), dtype=jnp.float32)
        W_g = jax.random.normal(k1, (H, D), dtype=jnp.float32) * 0.01
        W_u = jax.random.normal(k2, (H, D), dtype=jnp.float32) * 0.01
        W_d = jax.random.normal(k3, (D, H), dtype=jnp.float32) * 0.01
        return {'x': x, 'W_g': W_g, 'W_u': W_u, 'W_d': W_d}
    _L0_ffn_all = _L0_ffn_setup()
    _L0_ffn_in = {k: v for k, v in _L0_ffn_all.items() if k in ('W_g', 'W_u', 'W_d')}
    del _L0_ffn_all

    def _L1_attn_setup():
        import jax, jax.numpy as jnp
        import numpy as np
        import math
        B, T, E = (2, 256, 256)
        G, QPG, D = (4, 4, 128)

        def sinusoidal_pe(t, d, dtype):
            pos = jnp.arange(t, dtype=jnp.float32)[:, None]
            i = jnp.arange(0, d, 2, dtype=jnp.float32)
            inv_freq = jnp.exp(-(jnp.log(10000.0) * i / d))
            ang = pos * inv_freq
            pe = jnp.zeros((t, d), dtype=jnp.float32)
            pe = pe.at[:, 0::2].set(jnp.sin(ang)).at[:, 1::2].set(jnp.cos(ang))
            return pe.astype(dtype)
        key = jax.random.key(seed)
        ks = jax.random.split(key, 6)
        s = lambda fan_in: 1.0 / math.sqrt(fan_in)
        return {'x': jax.random.normal(ks[0], (B, T, E), dtype=jnp.float32), 'wq': jax.random.uniform(ks[1], (E, G * QPG * D), jnp.float32, -s(E), s(E)), 'bq': jax.random.uniform(ks[2], (G * QPG * D,), jnp.float32, -s(E), s(E)), 'wkv': jax.random.uniform(ks[3], (E, 2 * G * D), jnp.float32, -s(E), s(E)), 'bkv': jax.random.uniform(ks[4], (2 * G * D,), jnp.float32, -s(E), s(E)), 'wo': jax.random.uniform(ks[5], (G * QPG * D, E), jnp.float32, -s(G * QPG * D), s(G * QPG * D))}
    _L1_attn_all = _L1_attn_setup()
    _L1_attn_in = {k: v for k, v in _L1_attn_all.items() if k in ('wq', 'bq', 'wkv', 'bkv', 'wo')}
    del _L1_attn_all

    def _L1_xattn_setup():
        import jax, jax.numpy as jnp
        import numpy as np
        B, S, H, NH, L = (2, 256, 256, 16, 64)
        HD = H // NH
        key = jax.random.key(seed)
        k1, k2, k3, k4, k5 = jax.random.split(key, 5)
        scale = 0.02
        return {'q': jax.random.normal(k1, (B, S, H), dtype=jnp.float32), 'latent_kv': jax.random.normal(k2, (B, S, L), dtype=jnp.float32), 'Wq': jax.random.normal(k3, (H, H), dtype=jnp.float32) * scale, 'Wkv_expand': jax.random.normal(k4, (2 * H, L), dtype=jnp.float32) * scale, 'Wout': jax.random.normal(k5, (H, H), dtype=jnp.float32) * scale}
    _L1_xattn_all = _L1_xattn_setup()
    _L1_xattn_in = {k: v for k, v in _L1_xattn_all.items() if k in ('Wq', 'Wkv_expand', 'Wout')}
    del _L1_xattn_all

    def _L1_ffn_setup():
        import jax, jax.numpy as jnp
        import numpy as np
        from jax import lax
        TOP_K = 4
        ROUTED_SCALING = 1.0
        RENORMALIZE = True

        def _swiglu_ffn(x, wg, wu, wd):
            return jax.nn.silu(x @ wg.T) * (x @ wu.T) @ wd.T
        key = jax.random.key(seed)
        ks = jax.random.split(key, 9)
        H, I, E = (256, 128, 16)
        s = 0.02
        return {'hidden_states': jax.random.normal(ks[0], (2, 128, H), jnp.float32), 'gate_w': jax.random.normal(ks[1], (E, H), jnp.float32) * s, 'expert_bias': jax.random.normal(ks[2], (E,), jnp.float32) * s, 'w_gate': jax.random.normal(ks[3], (E, I, H), jnp.float32) * s, 'w_up': jax.random.normal(ks[4], (E, I, H), jnp.float32) * s, 'w_down': jax.random.normal(ks[5], (E, H, I), jnp.float32) * s, 'sw_gate': jax.random.normal(ks[6], (I, H), jnp.float32) * s, 'sw_up': jax.random.normal(ks[7], (I, H), jnp.float32) * s, 'sw_down': jax.random.normal(ks[8], (H, I), jnp.float32) * s}
    _L1_ffn_all = _L1_ffn_setup()
    _L1_ffn_in = {k: v for k, v in _L1_ffn_all.items() if k in ('gate_w', 'expert_bias', 'w_gate', 'w_up', 'w_down', 'sw_gate', 'sw_up', 'sw_down')}
    del _L1_ffn_all
    return {'x': x, 'ctx_512': ctx_512, 'L0_attn_Wqkv': _L0_attn_in['Wqkv'], 'L0_attn_bqkv': _L0_attn_in['bqkv'], 'L0_attn_Wout': _L0_attn_in['Wout'], 'L0_attn_bout': _L0_attn_in['bout'], 'L0_xattn_W_k': _L0_xattn_in['W_k'], 'L0_xattn_b_k': _L0_xattn_in['b_k'], 'L0_xattn_ln_gamma': _L0_xattn_in['ln_gamma'], 'L0_xattn_ln_beta': _L0_xattn_in['ln_beta'], 'L0_ffn_W_g': _L0_ffn_in['W_g'], 'L0_ffn_W_u': _L0_ffn_in['W_u'], 'L0_ffn_W_d': _L0_ffn_in['W_d'], 'L1_attn_wq': _L1_attn_in['wq'], 'L1_attn_bq': _L1_attn_in['bq'], 'L1_attn_wkv': _L1_attn_in['wkv'], 'L1_attn_bkv': _L1_attn_in['bkv'], 'L1_attn_wo': _L1_attn_in['wo'], 'L1_xattn_Wq': _L1_xattn_in['Wq'], 'L1_xattn_Wkv_expand': _L1_xattn_in['Wkv_expand'], 'L1_xattn_Wout': _L1_xattn_in['Wout'], 'L1_ffn_gate_w': _L1_ffn_in['gate_w'], 'L1_ffn_expert_bias': _L1_ffn_in['expert_bias'], 'L1_ffn_w_gate': _L1_ffn_in['w_gate'], 'L1_ffn_w_up': _L1_ffn_in['w_up'], 'L1_ffn_w_down': _L1_ffn_in['w_down'], 'L1_ffn_sw_gate': _L1_ffn_in['sw_gate'], 'L1_ffn_sw_up': _L1_ffn_in['sw_up'], 'L1_ffn_sw_down': _L1_ffn_in['sw_down']}

def reference(x, ctx_512, L0_attn_Wqkv, L0_attn_bqkv, L0_attn_Wout, L0_attn_bout, L0_xattn_W_k, L0_xattn_b_k, L0_xattn_ln_gamma, L0_xattn_ln_beta, L0_ffn_W_g, L0_ffn_W_u, L0_ffn_W_d, L1_attn_wq, L1_attn_bq, L1_attn_wkv, L1_attn_bkv, L1_attn_wo, L1_xattn_Wq, L1_xattn_Wkv_expand, L1_xattn_Wout, L1_ffn_gate_w, L1_ffn_expert_bias, L1_ffn_w_gate, L1_ffn_w_up, L1_ffn_w_down, L1_ffn_sw_gate, L1_ffn_sw_up, L1_ffn_sw_down):
    import jax
    import jax.numpy as jnp

    def _L0_attn_ref(x, Wqkv, bqkv, Wout, bout):
        import jax, jax.numpy as jnp
        import numpy as np
        NUM_HEADS = 16
        B, S, H = x.shape
        nh = NUM_HEADS
        hd = H // nh
        qkv = jnp.einsum('bsh,oh->bso', x, Wqkv) + bqkv
        q, k, v = jnp.split(qkv, 3, axis=-1)
        q = q.reshape(B, S, nh, hd).transpose(0, 2, 1, 3)
        k = k.reshape(B, S, nh, hd).transpose(0, 2, 1, 3)
        v = v.reshape(B, S, nh, hd).transpose(0, 2, 1, 3)
        scale = hd ** (-0.5)
        scores = jnp.einsum('bhqd,bhkd->bhqk', q, k) * scale
        causal = jnp.triu(jnp.ones((S, S), dtype=bool), k=1)
        scores = jnp.where(causal, -jnp.inf, scores)
        attn = jax.nn.softmax(scores, axis=-1)
        out = jnp.einsum('bhqk,bhkd->bhqd', attn, v)
        out = out.transpose(0, 2, 1, 3).reshape(B, S, H)
        return jnp.einsum('bsh,oh->bso', out, Wout) + bout

    def _L0_xattn_ref(p, k_v, W_k, b_k, ln_gamma, ln_beta):
        import jax, jax.numpy as jnp
        import numpy as np
        EPS = 1e-06
        IMAGE_DIMS = 256
        kv = k_v @ W_k.T + b_k
        out = jnp.einsum('bij,bjd->bid', p, kv)
        scale = IMAGE_DIMS ** (-0.5)
        sim = jnp.einsum('bid,bjd->bij', out, kv) * scale
        mu = jnp.mean(sim, axis=-1, keepdims=True)
        var = jnp.var(sim, axis=-1, keepdims=True)
        sim = (sim - mu) * jax.lax.rsqrt(var + EPS) * ln_gamma + ln_beta
        attn = jax.nn.softmax(sim, axis=-1)
        return attn

    def _L0_ffn_ref(x, W_g, W_u, W_d):
        import jax, jax.numpy as jnp
        import numpy as np
        EPS = 1e-08

        def rms_norm(x, eps=EPS):
            mean = jnp.mean(x, axis=-1, keepdims=True)
            var = jnp.var(x, axis=-1, keepdims=True)
            return (x - mean) / jnp.sqrt(var + eps)

        def activation_quant(x):
            s = 127.0 / jnp.max(jnp.abs(x), axis=-1, keepdims=True)
            return jnp.clip(jnp.round(s * x), -128, 127) / s

        def ternary_matmul(x, w):
            return jnp.matmul(x, jnp.sign(w).T)
        xq = activation_quant(rms_norm(x))
        g = jax.nn.silu(ternary_matmul(xq, W_g))
        u = ternary_matmul(xq, W_u)
        p = g * u
        return ternary_matmul(p, W_d)

    def _L1_attn_ref(x, wq, bq, wkv, bkv, wo):
        import jax, jax.numpy as jnp
        import numpy as np
        import math
        B, T, E = (2, 256, 256)
        G, QPG, D = (4, 4, 128)

        def sinusoidal_pe(t, d, dtype):
            pos = jnp.arange(t, dtype=jnp.float32)[:, None]
            i = jnp.arange(0, d, 2, dtype=jnp.float32)
            inv_freq = jnp.exp(-(jnp.log(10000.0) * i / d))
            ang = pos * inv_freq
            pe = jnp.zeros((t, d), dtype=jnp.float32)
            pe = pe.at[:, 0::2].set(jnp.sin(ang)).at[:, 1::2].set(jnp.cos(ang))
            return pe.astype(dtype)
        b, t, e = x.shape
        q = (x @ wq + bq).reshape(b, t, G, QPG, D).transpose(0, 2, 3, 1, 4)
        kv = (x @ wkv + bkv).reshape(b, t, G, 1, 2 * D).transpose(0, 2, 3, 1, 4)
        k, v = (kv[..., :D], kv[..., D:])
        pe = sinusoidal_pe(t, D, x.dtype)
        q = q + pe
        k = k + pe
        scores = jnp.einsum('bgqtd,bgksd->bgqts', q, k) / math.sqrt(D)
        causal = jnp.tril(jnp.ones((t, t), dtype=bool))
        scores = jnp.where(causal, scores, -jnp.inf)
        probs = jax.nn.softmax(scores, axis=-1)
        out = jnp.einsum('bgqts,bgksd->btgqd', probs, v).reshape(b, t, G * QPG * D)
        return out @ wo

    def _L1_xattn_ref(q, latent_kv, Wq, Wkv_expand, Wout):
        import jax, jax.numpy as jnp
        import numpy as np
        B, S, H, NH, L = (2, 256, 256, 16, 64)
        HD = H // NH
        b, sq, _ = q.shape
        sk = latent_kv.shape[1]
        qp = q @ Wq.T
        kv = latent_kv @ Wkv_expand.T
        k, v = jnp.split(kv, 2, axis=-1)
        qh = qp.reshape(b, sq, NH, HD).transpose(0, 2, 1, 3)
        kh = k.reshape(b, sk, NH, HD).transpose(0, 2, 1, 3)
        vh = v.reshape(b, sk, NH, HD).transpose(0, 2, 1, 3)
        inv_sqrt_d = 1.0 / jnp.sqrt(jnp.float32(HD))
        scores = jnp.einsum('bhqd,bhkd->bhqk', qh, kh) * inv_sqrt_d
        causal = jnp.tril(jnp.ones((sq, sk), dtype=bool))
        scores = jnp.where(causal, scores, jnp.finfo(scores.dtype).min)
        attn = jax.nn.softmax(scores, axis=-1)
        out = jnp.einsum('bhqk,bhkd->bhqd', attn, vh)
        out = out.transpose(0, 2, 1, 3).reshape(b, sq, H)
        return out @ Wout.T

    def _L1_ffn_ref(hidden_states, gate_w, expert_bias, w_gate, w_up, w_down, sw_gate, sw_up, sw_down):
        import jax, jax.numpy as jnp
        import numpy as np
        from jax import lax
        TOP_K = 4
        ROUTED_SCALING = 1.0
        RENORMALIZE = True

        def _swiglu_ffn(x, wg, wu, wd):
            return jax.nn.silu(x @ wg.T) * (x @ wu.T) @ wd.T
        orig_shape = hidden_states.shape
        H = orig_shape[-1]
        x = hidden_states.reshape(-1, H)
        T = x.shape[0]
        logits = x.astype(jnp.float32) @ gate_w.T
        scores = jax.nn.sigmoid(logits)
        _, topk_idx = lax.top_k(scores + expert_bias[None, :], TOP_K)
        topk_w = jnp.take_along_axis(scores, topk_idx, axis=-1)
        if RENORMALIZE:
            topk_w = topk_w / jnp.sum(topk_w, axis=-1, keepdims=True)
        topk_w = topk_w * ROUTED_SCALING
        E = gate_w.shape[0]
        combine = jnp.zeros((T, E), dtype=x.dtype).at[jnp.arange(T)[:, None], topk_idx].set(topk_w.astype(x.dtype))

        def step(acc, ws):
            wg, wu, wd, cw = ws
            return (acc + cw[:, None] * _swiglu_ffn(x, wg, wu, wd), None)
        routed, _ = lax.scan(step, jnp.zeros_like(x), (w_gate, w_up, w_down, combine.T))
        shared = _swiglu_ffn(x, sw_gate, sw_up, sw_down)
        return (routed + shared).reshape(orig_shape)
    x = _layernorm(x + _L0_attn_ref(x, L0_attn_Wqkv, L0_attn_bqkv, L0_attn_Wout, L0_attn_bout), axis=-1)
    x = _layernorm(x + _L0_xattn_ref(x, ctx_512, L0_xattn_W_k, L0_xattn_b_k, L0_xattn_ln_gamma, L0_xattn_ln_beta), axis=-1)
    x = _layernorm(x + _L0_ffn_ref(x, L0_ffn_W_g, L0_ffn_W_u, L0_ffn_W_d), axis=-1)
    x = _layernorm(x + _L1_attn_ref(x, L1_attn_wq, L1_attn_bq, L1_attn_wkv, L1_attn_bkv, L1_attn_wo), axis=-1)
    x = _layernorm(x + _L1_xattn_ref(x, ctx_512, L1_xattn_Wq, L1_xattn_Wkv_expand, L1_xattn_Wout), axis=-1)
    x = _layernorm(x + _L1_ffn_ref(x, L1_ffn_gate_w, L1_ffn_expert_bias, L1_ffn_w_gate, L1_ffn_w_up, L1_ffn_w_down, L1_ffn_sw_gate, L1_ffn_sw_up, L1_ffn_sw_down), axis=-1)
    return x

_drawn_inputs = setup_inputs


def setup_inputs(seed=0):
    import zlib

    import numpy as np

    out = dict(_drawn_inputs(seed))
    spreads = {'L0_attn_bqkv': (0.0, 0.1),
     'L0_attn_bout': (0.0, 0.1),
     'L0_xattn_b_k': (0.0, 0.8),
     'L0_xattn_ln_gamma': (1.0, 0.6),
     'L0_xattn_ln_beta': (0.0, 0.8)}
    factors = {'L0_xattn_W_k': 7.692,
     'L1_attn_bq': 8.0,
     'L1_attn_bkv': 2.868,
     'L1_xattn_Wq': 8.0,
     'L1_ffn_gate_w': 8.0,
     'L1_ffn_expert_bias': 8.0,
     'L1_ffn_w_gate': 8.0,
     'L1_ffn_w_up': 8.0,
     'L1_ffn_w_down': 8.0,
     'L1_ffn_sw_gate': 4.831,
     'L1_ffn_sw_up': 4.818,
     'L1_ffn_sw_down': 4.8}
    for name, (base, spread) in spreads.items():
        noise = np.random.default_rng([zlib.crc32(name.encode()), seed]).standard_normal(out[name].shape)
        drawn = base * np.exp(spread * noise) if base else spread * noise
        out[name] = jnp.asarray(drawn.astype(out[name].dtype))
    for name, factor in factors.items():
        out[name] = (out[name] * factor).astype(out[name].dtype)
    return out
```

```python
from contextlib import ExitStack

import numpy as np
import concourse.bass as bass
from concourse import mybir

F32 = mybir.dt.float32
BF16 = mybir.dt.bfloat16
U32 = mybir.dt.uint32
ACT = mybir.ActivationFunctionType
ALU = mybir.AluOpType
AX = mybir.AxisListType

P = 128
B, S, D = 4, 256, 256
TILES = B * S // P
C = D // P
PAIRS = B // 2
PT_ = 2 * S
NH, HD = 16, 16
G, QPG, DW = 4, 4, 128
L = 64
FF = 1024
E, I, TOPK = 16, 128, 4
EPS_LN, EPS_X, EPS_F = 1e-5, 1e-6, 1e-8
NEG = -1e30
ROUND = 1.5 * 2.0 ** 23
AHEAD = 4
START = 1

UN = 24
UW = 12
N_P, N_PT = 4, 3


class Steps:

    def __init__(self, sem):
        self.sem = sem

    def done(self, u):
        return u + (1 + AHEAD)

    def free(self, u, ring):
        return u + (1 + AHEAD - ring)


def build(nc, t, stop=6):
    ctx = ExitStack()
    with ctx:
        def sb(name, shape, dt=F32):
            return ctx.enter_context(nc.sbuf_tensor(name, shape, dt))

        def sem(name):
            return ctx.enter_context(nc.semaphore(name))

        X = sb("X", [P, TILES, D])
        xs = sb("xs", [P, 4, D])
        XT = sb("XT", [P, C, B * S])
        ident = sb("ident", [P, P])
        identb = sb("identb", [P, P], BF16)
        tri = sb("tri", [P, 4, P], BF16)
        r = sb("r", [P, 2, 2, D])
        stat = sb("stat", [P, 2, 2, 6])
        mv = sb("mv", [P, 2, 2, 2])
        veps = sb("veps", [P, 2, 2])
        rstd = sb("rstd", [P, 2, 2])
        mhalf = sb("mhalf", [P, 8])
        wqkv = sb("wqkv", [P, C, 3 * D])
        wout = sb("wout", [P, C, D])
        bqk = sb("bqk", [P, 4])
        bqs = sb("bqs", [P, 2])
        bv = sb("bv", [P, D])
        bout = sb("bout", [P, D])
        qk = sb("qk", [P, 4, PT_])
        kbd = sb("kbd", [P, C, 8, PT_])
        vn = sb("vn", [P, 4, NH, 32])
        an = sb("an", [P, C, PT_])
        prob = sb("prob", [P, N_P, 512])
        probT = sb("probT", [P, N_PT, 512])
        nmax = sb("nmax", [P, N_P, 4])
        rsum = sb("rsum", [P, N_P, 4])
        rinv = sb("rinv", [P, N_P, 4])
        cx = sb("cx", [L, PT_])
        wk = sb("wk", [L, L])
        bk = sb("bk", [L, 1])
        bkb = sb("bkb", [P, L])
        gam = sb("gam", [P, D])
        bet = sb("bet", [P, D])
        kvT = sb("kvT", [L, PT_])
        kv = sb("kv", [P, 4, L])
        oT = sb("oT", [L, PT_])
        z = sb("z", [P, 2, 2, D])
        xst = sb("xst", [P, 2, 2, 6])
        xmv = sb("xmv", [P, 2, 2, 2])
        xve = sb("xve", [P, 2, 2])
        xrs = sb("xrs", [P, 2, 2])
        xnm = sb("xnm", [P, 2, 2])
        xsm = sb("xsm", [P, 2, 2])
        xri = sb("xri", [P, 2, 2])
        sgu = sb("sgu", [P, 2, C, FF], BF16)
        wd = sb("wd", [P, FF // P, D])
        qT = sb("qT", [P, C, PT_], BF16)
        xn = z[:, :, :, :].rearrange("p a t d -> p (a t) d")
        fst = sb("fst", [P, 4, 6])
        fmv = sb("fmv", [P, 4, 2])
        fve = sb("fve", [P, 4])
        frs = sb("frs", [P, 4])
        amax = sb("amax", [P, 4])
        fsc = sb("fsc", [P, 4])
        finv = sb("finv", [P, 4])
        sg = sb("sg", [P, 2, 512])
        pr = sb("pr", [P, 2, 512])
        prT = sb("prT", [P, 2, 512])
        ww = sb("ww", [P, 2560])
        bw = sb("bw", [P, 8])
        bws = sb("bws", [P, 8])
        bvw = sb("bvw", [P, P])
        pes = sb("pes", [P, 2, S])
        peb = sb("peb", [P, 5, S])
        qw = sb("qw", [P, QPG, B * S])
        kw = sb("kw", [P, B * S])
        vw = sb("vw", [P, TILES, DW])
        aw = sb("aw", [P, 2, QPG, S])
        xq = sb("xq", [P, C, D])
        xkv = sb("xkv", [L, 2 * D])
        xo = sb("xo", [P, C, D])
        gw = sb("gw", [P, C, E])
        eb = sb("eb", [P, E])
        we = wqkv[:, :, :]
        sc_ = sb("sc_", [P, TILES, E])
        sel = sb("sel", [P, TILES, E])
        top = sb("top", [P, TILES, 8])
        topi = sb("topi", [P, TILES, 8], U32)
        topf = sb("topf", [P, TILES, 8])
        iota = sb("iota", [P, E])
        eq = sb("eq", [P, TILES, TOPK, E])
        pick = sb("pick", [P, TILES, E])
        cws = sb("cws", [P, TILES, E])
        csum = sb("csum", [P, TILES])
        cinv = sb("cinv", [P, TILES])
        cw = sb("cw", [P, TILES, E])
        cwe = sb("cwe", [P, 2, TILES])
        raw = qw[:, :, :].rearrange("p (u c) n -> p u c n", u=2)
        hid = aw[:, :, :, :].rearrange("p a h n -> p (a h n)").rearrange("p (s n) -> p s n", s=4)

        def bank(name):
            return ctx.enter_context(nc.psum_tensor(name, [P, 512], F32))

        pS = [bank("pS0"), bank("pS1")]
        pT = [bank("pT0"), bank("pT1")]
        pO = [bank("pO0"), bank("pO1")]
        pG = [bank("pG0"), bank("pG1")]

        ld = {k: sem("loaded_" + k) for k in ("a0", "x1", "f", "w", "x2", "e", "xs", "ctx", "wide", "wo", "exp0", "exp1")}
        consts = sem("consts")
        zeroed = sem("zeroed")
        gfull = [sem("general0_full"), sem("general1_full")]
        gread = [sem("general0_read"), sem("general1_read")]
        k_spread = [sem("keys0_spread"), sem("keys1_spread")]
        passed = {e: sem("passed_" + e) for e in ("dve", "pe", "sp")}
        score = Steps(sem("score_done"))
        maxed = Steps(sem("max_done"))
        exped = Steps(sem("exp_done"))
        recip = Steps(sem("recip_done"))
        normed = Steps(sem("norm_done"))
        transp = Steps(sem("transpose_done"))
        copied = Steps(sem("probT_done"))
        pved = Steps(sem("pv_done"))
        oread = Steps(sem("out_read"))
        bias_q = sem("bias_q")
        ln_step = sem("ln_step")
        ln_rstd = sem("ln_rstd")
        x_done = sem("x_done")
        x1_step = sem("x1_step")
        x1_rstd = sem("x1_rstd")
        x1_exp = sem("x1_exp")
        signs = sem("signs")
        f_step = sem("f_step")
        f_rstd = sem("f_rstd")
        f_gu = Steps(sem("f_gate_up"))
        f_silu = Steps(sem("f_silu"))
        f_pr = Steps(sem("f_product"))
        f_tr = Steps(sem("f_transposed"))
        f_prT = Steps(sem("f_productT"))
        w_bias = sem("w_bias")
        e_sig = sem("e_sigmoid")
        e_step = sem("e_step")
        e_gu = Steps(sem("e_gate_up"))
        e_silu = Steps(sem("e_silu"))
        e_h = Steps(sem("e_hidden"))
        e_cw = sem("e_cw")
        stored = sem("stored")

        GEN = [(0, 10, PAIRS), (0, 8, PAIRS), (0, 4, PAIRS), (4, 16, G), (0, 10, PAIRS), (6, 8, E // 2)]
        g_at = [0]
        for first, per, count in GEN:
            g_at.append(g_at[-1] + first + per * count)

        def gk(sub, i, n):
            first, per, _ = GEN[sub]
            return i * (per // 2) + (START + (g_at[sub] + first + n) // 2)

        def gk0(sub, n):
            return START + (g_at[sub] + n) // 2

        def g_take(pe, k, n):
            pe.wait_ge(gread[n % 2], k)
            return pG[n % 2]

        def g_wait(eng, k, n):
            eng.wait_ge(gfull[n % 2], k + 1)
            return pG[n % 2]

        def g_result(eng, k, n):
            eng.wait_ge(gread[n % 2], k + 1)

        narrow_units = [(j, 4 * hg + o, kind) for j in range(2) for hg in range(4)
                        for kind, o in (("first", 0), ("second", 0), ("second", 2))]
        wide_units = [(b, o, kind) for b in range(B)
                      for kind, o in (("first", 0), ("second", 0), ("second", 2))]
        UNITS_AT = {0: 0, 3: PAIRS * UN, 4: PAIRS * UN + G * UW}
        OUTS_AT = {0: 0, 3: PAIRS * 4, 4: PAIRS * 4 + G * 8}

        def units_of(sub, i):
            if sub == 3:
                return wide_units, i * UW + UNITS_AT[3], i * 8 + OUTS_AT[3]
            return narrow_units, i * UN + UNITS_AT[sub], i * 4 + OUTS_AT[sub]

        def out_of(sub, u):
            if sub == 3:
                return 2 * (u // 3) + (u % 3 > 0), u % 3 < 2, u % 3 != 1
            return u // 6, u % 6 == 0, u % 6 == 5

        def slot_end(sub, u):
            per = 3 if sub == 3 else 12
            return u // per if u >= 0 and u % per == per - 1 else None

        def by_head(ap, kind):
            return ap.rearrange("p (h k) -> p h k", h=4 if kind == "first" else 2)

        XS_AT = {0: 0, 1: 1, 2: 2, 4: 3}
        CTX_AT = {1: 0, 4: 1}

        def call_of(sub, i, j):
            return i * 2 + (4 * sub + j)

        def ln_at(sub, i, j):
            return i * 8 + 4 * j if sub == 0 else i * 6 + (16 + 12 * (sub - 1) + 3 * j)

        block = ctx.enter_context(nc.Block())

        @block.sync
        def _(sp):
            def load(dst, src, key):
                sp.dma_start(dst, src).then_inc(ld[key], 16)

            def load_pair(sub, i):
                if sub == 0:
                    sp.wait_ge(x_done, i * 2 + START)
                    load(xs[:, :, :], t["x"][bass.ds(i * PT_, PT_), :].rearrange("(t p) d -> p t d", p=P), "xs")
                else:
                    sp.wait_ge(x_done, i * 2 + (START + 4 * sub))
                    load(xs[:, :, :], X[:, bass.ds(i * 4, 4), :], "xs")
                if sub in CTX_AT:
                    load(cx[:, :], t["ctxT"][:, bass.ds(i * PT_, PT_)], "ctx")

            def spread_keys(sub, i):
                _, u0, _ = units_of(sub, i)
                sp.wait_ge(score.sem, score.done(u0 - 1))
                sp.wait_ge(zeroed, 2)
                for tl in range(C):
                    g_result(sp, gk(sub, i, 4 + tl), 4 + tl)
                    for g in range(8):
                        sp.dma_start(kbd[16 * g:16 * g + 16, tl, g, :],
                                     qk[16 * g:16 * g + 16, 2 + tl, :]).then_inc(k_spread[tl], 16)

            for tl in range(C):
                sp.sem_inc(k_spread[tl], 16)
            load(wqkv[:, :, :], t["wqkvT"].rearrange("(c p) n -> p c n", p=P), "a0")
            load(bqk[:, :], t["bqk"], "a0")
            load(bv[:, :], t["bv"].partition_broadcast(P), "a0")
            load(bout[:, :], t["bout"].partition_broadcast(P), "a0")
            load(wout[:, :, :], t["woutT"].rearrange("(c p) n -> p c n", p=P), "a0")
            with sp.Fori(0, PAIRS) as i:
                load_pair(0, i)
                spread_keys(0, i)
            load(wk[:, :], t["wkT"], "x1")
            load(bk[:, :], t["bk"].rearrange("(l o) -> l o", o=1), "x1")
            load(bkb[:, :], t["bk"].partition_broadcast(P), "x1")
            load(gam[:, :], t["gamma"].partition_broadcast(P), "x1")
            load(bet[:, :], t["beta"].partition_broadcast(P), "x1")
            load(raw[:, 0, :, :], t["wgT"].rearrange("(c p) n -> p c n", p=P), "f")
            load(raw[:, 1, :, :], t["wuT"].rearrange("(c p) n -> p c n", p=P), "f")
            load(wd[:, :, :], t["wdT"].rearrange("(c p) n -> p c n", p=P), "f")
            load(pes[:, :, :], t["pe"], "w")
            load(xq[:, :, :], t["xqT"].rearrange("(c p) n -> p c n", p=P), "x2")
            load(xkv[:, :], t["xkvT"], "x2")
            load(xo[:, :, :], t["xoT"].rearrange("(c p) n -> p c n", p=P), "x2")
            load(gw[:, :, :], t["gateT"].rearrange("(c p) n -> p c n", p=P), "e")
            load(eb[:, :], t["ebias"].partition_broadcast(P), "e")
            for sub in (1, 2):
                if stop > sub:
                    with sp.Fori(0, PAIRS) as i:
                        load_pair(sub, i)
            if stop > 3:
                with sp.Fori(0, G) as g:
                    sp.wait_ge(gfull[1], gk(3, g, 11) - 7)
                    sp.wait_ge(gread[1], gk(3, g, 11) - 7)
                    sp.sem_inc(passed["sp"], 1)
                    sp.wait_ge(w_bias, g * 2 + START)
                    load(ww[:, 0:1536], t["wwide"][bass.ds(g, 1), :, 0:1536].rearrange("o p n -> p (o n)"), "wide")
                    load(bw[:, :], t["bwide"][bass.ds(g, 1), :, :].rearrange("o p n -> p (o n)"), "wide")
                    load(bvw[:, :], t["bvwide"][bass.ds(g, 1), :].rearrange("o n -> (o n)").partition_broadcast(P), "wide")
                    sp.wait_ge(gfull[1], gk(3, g, 15) - 7)
                    load(ww[:, 1536:2560], t["wwide"][bass.ds(g, 1), :, 1536:2560].rearrange("o p n -> p (o n)"), "wo")
            if stop > 4:
                with sp.Fori(0, PAIRS) as i:
                    load_pair(4, i)
                    spread_keys(4, i)
            if stop > 5:
                with sp.Fori(0, E // 2) as i:
                    for s in range(2):
                        sp.wait_ge(gfull[1], gk(5, i, 4 * s + 3) - 3)
                        load(we[:, s, :], t["wexp"][bass.ds(i * 2 + s, 1), :, :].rearrange("o p n -> p (o n)"), f"exp{s}")
                sp.wait_ge(gfull[1], gk(5, E // 2, 3) - 3)
                load(we[:, 0, :], t["wexp"][E, :, :], "exp0")
            sp.wait_ge(x_done, START + 4 * stop)
            sp.dma_start(t["out"].rearrange("(t p) d -> p t d", p=P), X[:, :, :]).then_inc(stored, 16)
            sp.wait_ge(stored, 16)

        @block.gpsimd
        def _(pool):
            pool.sem_inc(normed.sem, AHEAD)
            pool.memset(ident[:, :], 0.0).then_inc(consts, 1)
            pool.memset(tri[:, :, :], 0.0).then_inc(consts, 1)
            pool.memset(mhalf[:, :], -0.5).then_inc(consts, 1)
            pool.iota(iota[:, :], pattern=[[1, E]], base=0, channel_multiplier=0,
                      allow_small_or_imprecise_dtypes=True).then_inc(consts, 1)
            pool.wait_ge(consts, 2)
            pool.affine_select(out=ident[:, :], in_=ident[:, :], compare_op=ALU.not_equal, fill=1.0,
                               base=0, pattern=[[-1, P]], channel_multiplier=1).then_inc(consts, 1)
            pool.affine_select(out=tri[:, :, :], in_=tri[:, :, :], compare_op=ALU.is_ge, fill=NEG,
                               base=0, pattern=[[0, 4], [-1, P]], channel_multiplier=1).then_inc(consts, 1)
            pool.wait_ge(consts, 5)
            pool.tensor_copy(identb[:, :], ident[:, :]).then_inc(consts, 1)
            pool.memset(kbd[:, :, :, :], 0.0).then_inc(zeroed, 1)

            def norm(u0, u, kind):
                pool.wait_ge(recip.sem, recip.done(u0 + u))
                v = by_head(prob[:, u % N_P, :], kind)
                n = v.shape[1]
                pool.tensor_tensor(v, v, rinv[:, u % N_P, 0:n].unsqueeze(2).broadcast_to(list(v.shape)),
                                   ALU.mult).then_inc(normed.sem, 1)

            def ln_root(sub, i, j):
                pool.wait_ge(ln_step, ln_at(sub, i, j) + (4 if sub == 0 else 3))
                pool.tensor_tensor(rstd[:, j, :], veps[:, j, :], mhalf[:, 0:2], ALU.pow).then_inc(ln_rstd, 1)

            def attention(sub, i):
                units, u0, _ = units_of(sub, i)
                for s in range(len(units) + 8):
                    if 0 <= s - 1 < len(units):
                        norm(u0, s - 1, units[s - 1][2])
                    j = slot_end(sub, s - 7)
                    if j is not None and sub != 3:
                        ln_root(sub, i, j)

            with pool.Fori(0, PAIRS) as i:
                attention(0, i)
            if stop > 1:
                with pool.Fori(0, PAIRS) as i:
                    for j in range(2):
                        pool.wait_ge(x1_step, i * 16 + (8 * j + 3))
                        pool.tensor_tensor(xrs[:, j, :], xve[:, j, :], mhalf[:, 0:2], ALU.pow).then_inc(x1_rstd, 1)
                        ln_root(1, i, j)
            if stop > 2:
                with pool.Fori(0, PAIRS) as i:
                    pool.wait_ge(f_step, i * 11 + 3)
                    pool.tensor_tensor(frs[:, :], fve[:, :], mhalf[:, 0:4], ALU.pow).then_inc(f_rstd, 1)
                    for j in range(2):
                        ln_root(2, i, j)
            if stop > 3:
                with pool.Fori(0, G) as g:
                    attention(3, g)
                for b in range(B):
                    ln_root(3, b // 2, b % 2)
            if stop > 4:
                with pool.Fori(0, PAIRS) as i:
                    attention(4, i)
            if stop > 5:
                for b in range(B):
                    ln_root(5, b // 2, b % 2)

        @block.scalar
        def _(act):
            act.sem_inc(exped.sem, AHEAD)
            act.sem_inc(oread.sem, AHEAD)
            act.sem_inc(f_silu.sem, AHEAD)
            act.sem_inc(f_prT.sem, AHEAD)
            act.sem_inc(e_silu.sem, AHEAD)
            act.sem_inc(w_bias, START)

            def exp_unit(u0, u, kind):
                act.wait_ge(maxed.sem, maxed.done(u0 + u))
                act.wait_ge(transp.sem, transp.free(u0 + u, N_P))
                src, dst = by_head(pS[u % 2][:, :], kind), by_head(prob[:, u % N_P, :], kind)
                for h in range(src.shape[1]):
                    e = act.activation(dst[:, h, :], src[:, h, :], ACT.Exp, bias=nmax[:, u % N_P, h:h + 1],
                                       accum_out=rsum[:, u % N_P, h:h + 1])
                e.then_inc(exped.sem, 1)

            def attention(sub, i):
                units, u0, o0 = units_of(sub, i)
                for s in range(len(units) + 6):
                    if s < len(units):
                        exp_unit(u0, s, units[s][2])
                    u = s - 5
                    if 0 <= u < len(units):
                        o, _, last = out_of(sub, u)
                        if last:
                            act.wait_ge(pved.sem, pved.done(u0 + u))
                            if sub == 3:
                                b, half = o // 2, o % 2
                                n = 12 + (b - 2) % 4
                                act.wait_ge(gfull[n % 2], gk(3, i, n) + (1 if b >= 2 else -7))
                                act.activation(aw[:, b % 2, :, half * P:half * P + P],
                                               pO[o % 2][:, :].rearrange("p (h q) -> p h q", h=QPG),
                                               ACT.Copy).then_inc(oread.sem, 1)
                            else:
                                j, tl = o // 2, o % 2
                                act.wait_ge(gfull[j], gk(sub, i, 8 + j) - 4)
                                act.activation(an[:, tl, j * S:(j + 1) * S], pO[o % 2][:, 0:S],
                                               ACT.Copy).then_inc(oread.sem, 1)

            def query_key_tiles(sub, i):
                _, u0, _ = units_of(sub, i)
                act.wait_ge(score.sem, score.done(u0 - 1))
                for m in range(4):
                    if m == 2:
                        for tl in range(C):
                            act.wait_ge(k_spread[tl], (i + (PAIRS if sub == 4 else 0)) * (8 * NH) + 16)
                    bank = g_wait(act, gk(sub, i, 2 + m), 2 + m)
                    scale = HD ** -0.5 if m < 2 else 1.0
                    if sub == 0:
                        bias = bqs[:, m:m + 1] if m < 2 else bqk[:, m:m + 1]
                        act.activation(qk[:, m, :], bank[:, :], ACT.Identity, bias=bias, scale=scale).then_inc(gread[m % 2], 1)
                    else:
                        act.activation(qk[:, m, :], bank[:, :], ACT.Copy, scale=scale).then_inc(gread[m % 2], 1)

            act.wait_ge(ld["a0"], 80)
            act.activation(bqs[:, :], bqk[:, 0:2], ACT.Copy, scale=HD ** -0.5).then_inc(bias_q, 1)
            act.wait_ge(bias_q, 1)
            with act.Fori(0, PAIRS) as i:
                query_key_tiles(0, i)
                attention(0, i)
            if stop > 1:
                act.wait_ge(ld["x1"], 80)
                with act.Fori(0, PAIRS) as i:
                    bank = g_wait(act, gk(1, i, 2), 2)
                    act.wait_ge(gfull[1], gk(1, i, 7) - 3)
                    act.activation(kvT[:, :], bank[0:L, :], ACT.Identity, bias=bk[:, 0:1]).then_inc(gread[0], 1)
                    for j in range(2):
                        bank = g_wait(act, gk(1, i, 4 + j), 4 + j)
                        act.activation(oT[:, j * S:(j + 1) * S], bank[0:L, 0:S], ACT.Copy,
                                       scale=D ** -0.5).then_inc(gread[j], 1)
                    for j in range(2):
                        act.wait_ge(x1_step, i * 16 + (8 * j + 6))
                        for q in range(2):
                            e = act.activation(z[:, j, q, :], z[:, j, q, :], ACT.Exp, bias=xnm[:, j, q:q + 1],
                                               accum_out=xsm[:, j, q:q + 1])
                        e.then_inc(x1_exp, 1)
            if stop > 2:
                act.wait_ge(ld["f"], 48)
                act.activation(sgu[:, :, :, :], raw[:, :, :, :], ACT.Sign).then_inc(signs, 1)
                act.activation(wd[:, :, :], wd[:, :, :], ACT.Sign).then_inc(signs, 1)
                with act.Fori(0, PAIRS) as i:
                    for s in range(8 + 1):
                        if s < 8:
                            v = i * 8 + s
                            act.wait_ge(f_gu.sem, f_gu.done(v))
                            act.wait_ge(f_pr.sem, f_pr.free(v, 2))
                            act.activation(sg[:, s % 2, :], pS[s % 2][:, :], ACT.Silu,
                                           scale=finv[:, s // 2:s // 2 + 1]).then_inc(f_silu.sem, 1)
                        if s >= 1:
                            v = i * 8 + (s - 1)
                            act.wait_ge(f_tr.sem, f_tr.done(v))
                            act.activation(prT[:, (s - 1) % 2, :], pO[(s - 1) % 2][:, :], ACT.Copy).then_inc(f_prT.sem, 1)
            if stop > 3:
                act.wait_ge(ld["w"], 16)
                with act.Fori(0, G) as g:
                    act.wait_ge(ld["wide"], (g + 1) * 48)
                    act.wait_ge(gread[1], gk(3, g, 9) - 7)
                    act.wait_ge(gread[0], gk(3, g, 8) - 7)
                    act.activation(bws[:, :], bw[:, :], ACT.Copy, scale=DW ** -0.5).then_inc(w_bias, 1)
                    act.wait_ge(w_bias, g * 2 + (START + 1))
                    for h in range(QPG + 1):
                        bias = bws[:, h:h + 1] if h < QPG else bw[:, h:h + 1]
                        a = act.activation(peb[:, h, :], pes[:, h // QPG, :], ACT.Identity, bias=bias)
                    a.then_inc(w_bias, 1)
                    attention(3, g)
            if stop > 4:
                with act.Fori(0, PAIRS) as i:
                    query_key_tiles(4, i)
                    attention(4, i)
            if stop > 5:
                for n in (4, 5):
                    bank = g_wait(act, gk0(5, n), n)
                    act.activation(sc_[:, 4 * (n - 4):4 * (n - 3), :], bank[:, 0:4 * E].rearrange("p (t e) -> p t e", e=E),
                                   ACT.Sigmoid).then_inc(gread[n % 2], 1)

                def silu_unit(v, q):
                    act.wait_ge(e_gu.sem, e_gu.done(v))
                    act.wait_ge(e_h.sem, e_h.free(v, 2))
                    act.activation(sg[:, q % 2, :], pS[q % 2][:, :], ACT.Silu).then_inc(e_silu.sem, 1)

                with act.Fori(0, E // 2) as i:
                    for q in range(4):
                        silu_unit(i * 4 + q, q)
                for q in range(2):
                    silu_unit(2 * E + q, q)

        @block.vector
        def _(dve):
            for st in (maxed, recip, copied, f_pr, e_h):
                dve.sem_inc(st.sem, AHEAD)
            for st in (*gread, x_done):
                dve.sem_inc(st, START)
            dve.memset(vn[:, :, :, :], 0.0).then_inc(zeroed, 1)

            def max_unit(u0, u, kind):
                dve.wait_ge(score.sem, score.done(u0 + u))
                v = by_head(pS[u % 2][:, :], kind)
                dve.reduce_max(nmax[:, u % N_P, 0:v.shape[1]], v, AX.X, negate=True).then_inc(maxed.sem, 1)

            def recip_unit(u0, u, kind):
                dve.wait_ge(exped.sem, exped.done(u0 + u))
                dve.wait_ge(normed.sem, normed.free(u0 + u, N_P))
                n = 4 if kind == "first" else 2
                dve.reciprocal(rinv[:, u % N_P, 0:n], rsum[:, u % N_P, 0:n]).then_inc(recip.sem, 1)

            def copy_unit(u0, u):
                dve.wait_ge(transp.sem, transp.done(u0 + u))
                dve.wait_ge(pved.sem, pved.free(u0 + u, N_PT))
                dve.tensor_copy(probT[:, u % N_PT, :], pT[u % 2][:, :]).then_inc(copied.sem, 1)

            def layernorm(sub, i, j, src, dst):
                at = ln_at(sub, i, j) + (1 if sub == 0 else 0)
                dve.wait_ge(ln_step, at)
                dve.wait_ge(x_done, call_of(sub, i, j) + START)
                for q in range(2):
                    a = dve.bn_stats(stat[:, j, q, :], src[:, q, :])
                a.then_inc(ln_step, 1)
                dve.wait_ge(ln_step, at + 1)
                dve.sem_inc(passed["dve"], 1)
                for q in range(2):
                    a = dve.bn_aggr(mv[:, j, q, :], stat[:, j, q, :])
                a.then_inc(ln_step, 1)
                dve.wait_ge(ln_step, at + 2)
                dve.tensor_scalar(veps[:, j, :], mv[:, j, :, 1], EPS_LN, None, ALU.add).then_inc(ln_step, 1)
                dve.wait_ge(ln_rstd, call_of(sub, i, j) + 1)
                for q in range(2):
                    a = dve.tensor_scalar(dst(q), src[:, q, :], mv[:, j, q, 0:1], rstd[:, j, q:q + 1],
                                          ALU.subtract, ALU.mult)
                a.then_inc(x_done, 1)

            def in_x(i, j):
                return lambda q: X[:, bass.ds(i * 4 + (2 * j + q), 1), :].rearrange("p o n -> p (o n)")

            def add_and_norm(sub, i, j, n):
                k = gk(sub, i, n)
                bank = g_wait(dve, k, n)
                dve.wait_ge(x_done, call_of(sub, i, j) + START)
                dve.tensor_tensor(r[:, j, :, :], bank[:, :].rearrange("p (t d) -> p t d", t=2),
                                  xs[:, 2 * j:2 * j + 2, :], ALU.add).then_inc(gread[n % 2], 1)
                g_result(dve, k, n)
                if sub == 0:
                    dve.tensor_tensor(r[:, j, :, :], r[:, j, :, :], bout[:, :].unsqueeze(1).broadcast_to([P, 2, D]),
                                      ALU.add).then_inc(ln_step, 1)
                layernorm(sub, i, j, r[:, j, :, :], in_x(i, j))

            def copy_xT(sub, i):
                for c in range(C):
                    bank = g_wait(dve, gk(sub, i, c), c)
                    dve.tensor_copy(XT[:, c, 0:PT_], bank[:, :]).then_inc(gread[c], 1)

            def attention(sub, i):
                units, u0, _ = units_of(sub, i)
                for s in range(len(units) + 8):
                    if s < len(units):
                        max_unit(u0, s, units[s][2])
                    if 0 <= s - 1 < len(units):
                        recip_unit(u0, s - 1, units[s - 1][2])
                    if 0 <= s - 3 < len(units):
                        copy_unit(u0, s - 3)
                    j = slot_end(sub, s - 7)
                    if j is not None:
                        if sub == 3:
                            n = 12 + j
                            k = gk(3, i, n)
                            bank = g_wait(dve, k, n)
                            dve.wait_ge(gread[n % 2], k)
                            dve.tensor_tensor(X[:, 2 * j:2 * j + 2, :], bank[:, :].rearrange("p (t d) -> p t d", t=2),
                                              X[:, 2 * j:2 * j + 2, :], ALU.add).then_inc(gread[n % 2], 1)
                        else:
                            add_and_norm(sub, i, j, 8 + j)

            def values(sub, i):
                _, u0, _ = units_of(sub, i)
                dve.wait_ge(pved.sem, pved.done(u0 - 1))
                dve.wait_ge(zeroed, 2)
                for n in (6, 7):
                    bank = g_wait(dve, gk(sub, i, n), n)
                    for q in range(2):
                        src = bank[:, q * D:(q + 1) * D].rearrange("p (s e d) -> p s e d", e=2, d=HD)
                        for e in range(2):
                            dst = vn[:, 2 * (n - 6) + q, e::2, e * HD:(e + 1) * HD]
                            if sub == 0:
                                b = bv[:, :].rearrange("p (s e d) -> p s e d", e=2, d=HD)[:, :, e, :]
                                a = dve.tensor_tensor(dst, src[:, :, e, :], b, ALU.add)
                            else:
                                a = dve.tensor_copy(dst, src[:, :, e, :])
                    a.then_inc(gread[n % 2], 1)

            dve.wait_ge(ld["a0"], 80)
            with dve.Fori(0, PAIRS) as i:
                copy_xT(0, i)
                values(0, i)
                attention(0, i)
            if stop > 1:
                dve.wait_ge(ld["x1"], 80)
                with dve.Fori(0, PAIRS) as i:
                    copy_xT(1, i)
                    bank = g_wait(dve, gk(1, i, 3), 3)
                    dve.tensor_tensor(kv[:, :, :], bank[:, 0:4 * L].rearrange("p (t d) -> p t d", d=L),
                                      bkb[:, :].unsqueeze(1).broadcast_to([P, 4, L]), ALU.add).then_inc(gread[1], 1)
                    for j in range(2):
                        at = i * 16 + 8 * j
                        k = gk(1, i, 6 + j)
                        bank = g_wait(dve, k, 6 + j)
                        dve.wait_ge(x_done, call_of(1, i, j) + START)
                        sim = bank[:, :].rearrange("p (t d) -> p t d", t=2)
                        for q in range(2):
                            a = dve.bn_stats(xst[:, j, q, :], sim[:, q, :])
                        a.then_inc(x1_step, 1)
                        dve.wait_ge(x1_step, at + 1)
                        dve.sem_inc(passed["dve"], 1)
                        for q in range(2):
                            a = dve.bn_aggr(xmv[:, j, q, :], xst[:, j, q, :])
                        a.then_inc(x1_step, 1)
                        dve.wait_ge(x1_step, at + 2)
                        dve.tensor_scalar(xve[:, j, :], xmv[:, j, :, 1], EPS_X, None, ALU.add).then_inc(x1_step, 1)
                        dve.wait_ge(x1_rstd, i * 2 + (j + 1))
                        for q in range(2):
                            a = dve.tensor_scalar(z[:, j, q, :], sim[:, q, :], xmv[:, j, q, 0:1], xrs[:, j, q:q + 1],
                                                  ALU.subtract, ALU.mult)
                        a.then_inc(gread[j], 1)
                        g_result(dve, k, 6 + j)
                        dve.tensor_tensor(z[:, j, :, :], z[:, j, :, :], gam[:, :].unsqueeze(1).broadcast_to([P, 2, D]),
                                          ALU.mult).then_inc(x1_step, 1)
                        dve.wait_ge(x1_step, at + 4)
                        dve.tensor_tensor(z[:, j, :, :], z[:, j, :, :], bet[:, :].unsqueeze(1).broadcast_to([P, 2, D]),
                                          ALU.add).then_inc(x1_step, 1)
                        dve.wait_ge(x1_step, at + 5)
                        dve.reduce_max(xnm[:, j, :], z[:, j, :, :], AX.X, negate=True).then_inc(x1_step, 1)
                        dve.wait_ge(x1_exp, i * 2 + (j + 1))
                        dve.reciprocal(xri[:, j, :], xsm[:, j, :]).then_inc(x1_step, 1)
                        dve.wait_ge(x1_step, at + 7)
                        for q in range(2):
                            a = dve.scalar_tensor_tensor(r[:, j, q, :], z[:, j, q, :], xri[:, j, q:q + 1],
                                                         xs[:, 2 * j + q, :], ALU.mult, ALU.add)
                        a.then_inc(x1_step, 1)
                        dve.wait_ge(x1_step, at + 8)
                        layernorm(1, i, j, r[:, j, :, :], in_x(i, j))
            if stop > 2:
                with dve.Fori(0, PAIRS) as i:
                    at = i * 11
                    dve.wait_ge(ld["xs"], (i + (2 * PAIRS + 1)) * 16)
                    for q in range(4):
                        a = dve.bn_stats(fst[:, q, :], xs[:, q, :])
                    a.then_inc(f_step, 1)
                    dve.wait_ge(f_step, at + 1)
                    dve.sem_inc(passed["dve"], 1)
                    for q in range(4):
                        a = dve.bn_aggr(fmv[:, q, :], fst[:, q, :])
                    a.then_inc(f_step, 1)
                    dve.wait_ge(f_step, at + 2)
                    dve.tensor_scalar(fve[:, :], fmv[:, :, 1], EPS_F, None, ALU.add).then_inc(f_step, 1)
                    dve.wait_ge(f_rstd, i + 1)
                    for q in range(4):
                        a = dve.tensor_scalar(xn[:, q, :], xs[:, q, :], fmv[:, q, 0:1], frs[:, q:q + 1],
                                              ALU.subtract, ALU.mult)
                    a.then_inc(f_step, 1)
                    dve.wait_ge(f_step, at + 4)
                    dve.reduce_max(amax[:, :], xn[:, :, :], AX.X, apply_absolute_value=True).then_inc(f_step, 1)
                    dve.wait_ge(f_step, at + 5)
                    dve.reciprocal(fsc[:, :], amax[:, :]).then_inc(f_step, 1)
                    dve.wait_ge(f_step, at + 6)
                    dve.tensor_scalar(fsc[:, :], fsc[:, :], 127.0, None, ALU.mult).then_inc(f_step, 1)
                    dve.tensor_scalar(finv[:, :], amax[:, :], 1.0 / 127.0, None, ALU.mult).then_inc(f_step, 1)
                    dve.wait_ge(f_step, at + 8)
                    for q in range(4):
                        a = dve.tensor_scalar(xn[:, q, :], xn[:, q, :], fsc[:, q:q + 1], ROUND, ALU.mult, ALU.add)
                    a.then_inc(f_step, 1)
                    dve.wait_ge(f_step, at + 9)
                    dve.tensor_scalar(xn[:, :, :], xn[:, :, :], ROUND, 127.0, ALU.subtract, ALU.min).then_inc(f_step, 1)
                    dve.wait_ge(f_step, at + 10)
                    dve.tensor_scalar(xn[:, :, :], xn[:, :, :], -128.0, None, ALU.max).then_inc(f_step, 1)
                    for c in range(C):
                        bank = g_wait(dve, gk(2, i, c), c)
                        dve.tensor_copy(qT[:, c, :], bank[:, :]).then_inc(gread[c], 1)
                    for s in range(8):
                        v = i * 8 + s
                        dve.wait_ge(f_silu.sem, f_silu.done(v))
                        dve.wait_ge(f_tr.sem, f_tr.free(v, 2))
                        dve.scalar_tensor_tensor(pr[:, s % 2, :], pT[s % 2][:, :], finv[:, s // 2:s // 2 + 1],
                                                 sg[:, s % 2, :], ALU.mult, ALU.mult).then_inc(f_pr.sem, 1)
                        if s == 7:
                            add_and_norm(2, i, 0, 2)
                    add_and_norm(2, i, 1, 3)
            if stop > 3:
                def copy_all_xT(sub):
                    for c in range(C):
                        for half in range(2):
                            n = 2 * c + half
                            bank = g_wait(dve, gk0(sub, n), n)
                            dve.tensor_copy(XT[:, c, half * 512:(half + 1) * 512], bank[:, :]).then_inc(gread[n % 2], 1)

                copy_all_xT(3)
                with dve.Fori(0, G) as g:
                    _, u0, _ = units_of(3, g)
                    dve.wait_ge(w_bias, g * 2 + (START + 2))
                    dve.wait_ge(score.sem, score.done(u0 - 1))
                    for h in range(QPG):
                        for half in range(2):
                            n = 2 * h + half
                            bank = g_wait(dve, gk(3, g, n), n)
                            dve.scalar_tensor_tensor(
                                qw[:, h, half * 512:(half + 1) * 512].rearrange("p (b s) -> p b s", b=2),
                                bank[:, :].rearrange("p (b s) -> p b s", b=2), DW ** -0.5,
                                peb[:, h, :].unsqueeze(1).broadcast_to([P, 2, S]), ALU.mult, ALU.add).then_inc(gread[n % 2], 1)
                    for half in range(2):
                        n = 8 + half
                        bank = g_wait(dve, gk(3, g, n), n)
                        dve.tensor_tensor(kw[:, half * 512:(half + 1) * 512].rearrange("p (b s) -> p b s", b=2),
                                          bank[:, :].rearrange("p (b s) -> p b s", b=2),
                                          peb[:, QPG, :].unsqueeze(1).broadcast_to([P, 2, S]), ALU.add).then_inc(gread[n % 2], 1)
                    dve.wait_ge(pved.sem, pved.done(u0 - 1))
                    for half in range(2):
                        n = 10 + half
                        bank = g_wait(dve, gk(3, g, n), n)
                        dve.tensor_tensor(vw[:, 4 * half:4 * half + 4, :], bank[:, :].rearrange("p (t d) -> p t d", t=4),
                                          bvw[:, :].unsqueeze(1).broadcast_to([P, 4, DW]), ALU.add).then_inc(gread[n % 2], 1)
                    attention(3, g)
                for b in range(B):
                    dve.wait_ge(gread[b % 2], gk(3, G - 1, 12 + b) + 1)
                    layernorm(3, b // 2, b % 2, X[:, 2 * b:2 * b + 2, :], lambda q, b=b: X[:, 2 * b + q, :])
            if stop > 4:
                with dve.Fori(0, PAIRS) as i:
                    copy_xT(4, i)
                    values(4, i)
                    attention(4, i)
            if stop > 5:
                copy_all_xT(5)
                dve.wait_ge(ld["e"], 32)
                for n in (4, 5):
                    g_result(dve, gk0(5, n), n)
                wide = [P, TILES, E]
                dve.tensor_tensor(sel[:, :, :], sc_[:, :, :], eb[:, :].unsqueeze(1).broadcast_to(wide), ALU.add).then_inc(e_step, 1)
                dve.wait_ge(e_step, 1)
                for q in range(TILES):
                    a = dve.max(top[:, q, :], sel[:, q, :])
                a.then_inc(e_step, 1)
                dve.wait_ge(e_step, 2)
                for q in range(TILES):
                    a = dve.max_index(topi[:, q, :], top[:, q, :], sel[:, q, :])
                a.then_inc(e_step, 1)
                dve.wait_ge(e_step, 3)
                dve.tensor_copy(topf[:, :, :], topi[:, :, :]).then_inc(e_step, 1)
                dve.wait_ge(e_step, 4)
                dve.wait_ge(consts, 4)
                for q in range(TOPK):
                    a = dve.tensor_tensor(eq[:, :, q, :], iota[:, :].unsqueeze(1).broadcast_to(wide),
                                          topf[:, :, q:q + 1].broadcast_to(wide), ALU.is_equal)
                a.then_inc(e_step, 1)
                dve.wait_ge(e_step, 5)
                dve.tensor_reduce(pick[:, :, :], eq[:, :, :, :].rearrange("p t k e -> p t e k"), AX.X, ALU.add).then_inc(e_step, 1)
                dve.wait_ge(e_step, 6)
                dve.tensor_tensor(cws[:, :, :], pick[:, :, :], sc_[:, :, :], ALU.mult).then_inc(e_step, 1)
                dve.wait_ge(e_step, 7)
                dve.tensor_reduce(csum[:, :], cws[:, :, :], AX.X, ALU.add).then_inc(e_step, 1)
                dve.wait_ge(e_step, 8)
                dve.reciprocal(cinv[:, :], csum[:, :]).then_inc(e_step, 1)
                dve.wait_ge(e_step, 9)
                dve.tensor_tensor(cw[:, :, :], cws[:, :, :], cinv[:, :].unsqueeze(2).broadcast_to(wide), ALU.mult).then_inc(e_step, 1)
                dve.wait_ge(e_step, 10)

                def hidden(v, q):
                    dve.wait_ge(e_silu.sem, e_silu.done(v))
                    dve.tensor_tensor(hid[:, q % 4, :], pT[q % 2][:, :], sg[:, q % 2, :], ALU.mult).then_inc(e_h.sem, 1)

                def combine(i, q):
                    for n in (2 * q, 2 * q + 1):
                        k = gk(5, i, n)
                        bank = g_wait(dve, k, n)
                        dve.wait_ge(gread[n % 2], k)
                        for w in range(2):
                            tile = 4 * (q % 2) + 2 * (n % 2) + w
                            a = dve.scalar_tensor_tensor(X[:, tile, :], bank[:, w * D:(w + 1) * D],
                                                         cwe[:, (q // 2) % 2, tile:tile + 1], X[:, tile, :],
                                                         ALU.mult, ALU.add)
                        a.then_inc(gread[n % 2], 1)

                with dve.Fori(0, E // 2) as i:
                    dve.wait_ge(gread[1], gk(5, i, 1))
                    for s in range(2):
                        a = dve.tensor_copy(cwe[:, s, :], cw[:, :, bass.ds(i * 2 + s, 1)].rearrange("p t o -> p (t o)"))
                    a.then_inc(e_cw, 1)
                    dve.wait_ge(e_cw, i + 1)
                    for q in range(4 + 1):
                        if q < 4:
                            hidden(i * 4 + q, q)
                        if q >= 1:
                            combine(i, q - 1)
                dve.wait_ge(gread[1], gk(5, E // 2, 1))
                dve.memset(cwe[:, 0, :], 1.0).then_inc(e_cw, 1)
                dve.wait_ge(e_cw, E // 2 + 1)
                for q in range(2 + 1):
                    if q < 2:
                        hidden(2 * E + q, q)
                    if q >= 1:
                        combine(E // 2, q - 1)
                for n in (2, 3):
                    g_result(dve, gk(5, E // 2, n), n)
                for b in range(B):
                    layernorm(5, b // 2, b % 2, X[:, 2 * b:2 * b + 2, :], lambda q, b=b: X[:, 2 * b + q, :])

        @block.tensor
        def _(pe):
            for st in (score, transp, pved, f_gu, f_tr, e_gu):
                pe.sem_inc(st.sem, AHEAD)
            for st in gfull:
                pe.sem_inc(st, START)

            def transpose_pair(sub, i, src):
                for c in range(C):
                    bank = g_take(pe, gk(sub, i, c), c)
                    for q in range(4):
                        a = pe.transpose(bank[:, q * P:(q + 1) * P], src[:, q, c * P:(c + 1) * P], ident[:, :])
                    a.then_inc(gfull[c], 1)

            def transpose_all(sub):
                for c in range(C):
                    for half in range(2):
                        n = 2 * c + half
                        bank = g_take(pe, gk0(sub, n), n)
                        for q in range(4):
                            a = pe.transpose(bank[:, q * P:(q + 1) * P], X[:, 4 * half + q, c * P:(c + 1) * P], ident[:, :])
                        a.then_inc(gfull[n % 2], 1)

            def score_unit(sub, u0, u, unit):
                b, h0, kind = unit
                pe.wait_ge(exped.sem, exped.free(u0 + u, 2))
                bank = pS[u % 2]
                v = by_head(bank[:, :], kind)
                if kind == "first":
                    pe.matmul(v, identb[:, :], tri[:, :, :], start=True, stop=False, skip_group_check=True)
                    q0, nk, nh = b * S, P, 4
                else:
                    pe.matmul(v[:, :, P:S], identb[:, :], tri[:, 0:2, :], start=True, stop=False, skip_group_check=True)
                    q0, nk, nh = b * S + P, S, 2
                if sub == 3:
                    for h in range(nh):
                        a = pe.matmul(v[:, h, :], qw[:, h0 + h, q0:q0 + P], kw[:, b * S:b * S + nk],
                                      start=False, stop=True, skip_group_check=True)
                else:
                    tl, g = h0 // 8, h0 % 8
                    a = pe.matmul(v, qk[:, tl, q0:q0 + P], kbd[:, tl, g:g + nh, b * S:b * S + nk],
                                  start=False, stop=True, skip_group_check=True)
                a.then_inc(score.sem, 1)

            def transpose_unit(u0, u):
                pe.wait_ge(normed.sem, normed.done(u0 + u))
                pe.wait_ge(copied.sem, copied.free(u0 + u, 2))
                for q in range(4):
                    a = pe.transpose(pT[u % 2][:, q * P:(q + 1) * P], prob[:, u % N_P, q * P:(q + 1) * P], ident[:, :])
                a.then_inc(transp.sem, 1)

            def value_unit(sub, u0, o0, u, unit):
                b, h0, kind = unit
                o, first, _ = out_of(sub, u)
                if first:
                    pe.wait_ge(oread.sem, oread.free(o0 + o, 2))
                pe.wait_ge(copied.sem, copied.done(u0 + u))
                bank = pO[o % 2]
                for q in range(4):
                    h, kt = (h0 + q, 0) if kind == "first" else (h0 + q // 2, q % 2)
                    src = probT[:, u % N_PT, q * P:(q + 1) * P]
                    if sub == 3:
                        a = pe.matmul(bank[:, h * P:(h + 1) * P], vw[:, 2 * b + kt, :], src, start=kt == 0,
                                      stop=kind == "first" or kt == 1, skip_group_check=True)
                    else:
                        s, q0 = (h % 8) // 2, 0 if kind == "first" else P
                        a = pe.matmul(bank[32 * s:32 * s + 32, q0:q0 + P], vn[:, 2 * b + kt, h, :], src,
                                      start=kind == "first" and h % 2 == 0,
                                      stop=h % 2 == 1 and (kind == "first" or kt == 1), skip_group_check=True)
                a.then_inc(pved.sem, 1)

            def attention(sub, i, wo):
                units, u0, o0 = units_of(sub, i)
                for s in range(len(units) + 7):
                    if s < len(units):
                        if sub != 3 and s in (0, 6):
                            pe.wait_ge(k_spread[s // 6], (i + (PAIRS if sub == 4 else 0)) * (8 * NH) + (8 * NH + 16))
                        score_unit(sub, u0, s, units[s])
                    if 0 <= s - 3 < len(units):
                        transpose_unit(u0, s - 3)
                    if 0 <= s - 4 < len(units):
                        value_unit(sub, u0, o0, s - 4, units[s - 4])
                    j = slot_end(sub, s - 6)
                    if j is not None:
                        n = (12 if sub == 3 else 8) + j
                        pe.wait_ge(oread.sem, oread.done(o0 + (2 * j + 1)))
                        bank = g_take(pe, gk(sub, i, n), n)
                        for q in range(2):
                            for c in range(QPG if sub == 3 else C):
                                if sub == 3:
                                    x, w = aw[:, j % 2, c, q * P:(q + 1) * P], wo[:, c * D:(c + 1) * D]
                                else:
                                    x, w = an[:, c, (2 * j + q) * P:(2 * j + q + 1) * P], wo[:, c, :]
                                a = pe.matmul(bank[:, q * D:(q + 1) * D], x, w, start=c == 0,
                                              stop=c == (QPG if sub == 3 else C) - 1)
                        a.then_inc(gfull[n % 2], 1)

            def narrow_projections(sub, i):
                for n in range(2):
                    g_result(pe, gk(sub, i, n), n)
                for m in range(4):
                    n = 2 + m
                    bank = g_take(pe, gk(sub, i, n), n)
                    if sub == 4 and m >= 2:
                        a = pe.matmul(bank[:, :], xkv[:, (m - 2) * P:(m - 1) * P], cx[:, :], start=True, stop=True)
                    else:
                        w = wqkv if sub == 0 else xq
                        for c in range(C):
                            a = pe.matmul(bank[:, :], w[:, c, m * P:(m + 1) * P], XT[:, c, 0:PT_], start=c == 0, stop=c == 1)
                    a.then_inc(gfull[n % 2], 1)
                for n in (6, 7):
                    bank = g_take(pe, gk(sub, i, n), n)
                    for q in range(2):
                        tok = (2 * (n - 6) + q) * P
                        if sub == 4:
                            a = pe.matmul(bank[:, q * D:(q + 1) * D], cx[:, tok:tok + P], xkv[:, D:2 * D], start=True, stop=True)
                        else:
                            for c in range(C):
                                a = pe.matmul(bank[:, q * D:(q + 1) * D], XT[:, c, tok:tok + P], wqkv[:, c, 2 * D:3 * D],
                                              start=c == 0, stop=c == 1)
                    a.then_inc(gfull[n % 2], 1)

            def pair_loaded(sub, i):
                pe.wait_ge(ld["xs"], (i + (PAIRS * XS_AT[sub] + 1)) * 16)
                if sub in CTX_AT:
                    pe.wait_ge(ld["ctx"], (i + (PAIRS * CTX_AT[sub] + 1)) * 16)

            pe.wait_ge(consts, 7)
            pe.wait_ge(ld["a0"], 80)
            with pe.Fori(0, PAIRS) as i:
                pair_loaded(0, i)
                transpose_pair(0, i, xs)
                narrow_projections(0, i)
                for n in (2, 3, 6, 7):
                    g_result(pe, gk(0, i, n), n)
                attention(0, i, wout)
            if stop > 1:
                pe.wait_ge(ld["x1"], 80)
                with pe.Fori(0, PAIRS) as i:
                    pair_loaded(1, i)
                    transpose_pair(1, i, xs)
                    bank = g_take(pe, gk(1, i, 2), 2)
                    pe.sem_inc(passed["pe"], 1)
                    pe.matmul(bank[0:L, :], wk[:, :], cx[:, :], start=True, stop=True).then_inc(gfull[0], 1)
                    bank = g_take(pe, gk(1, i, 3), 3)
                    for q in range(4):
                        a = pe.matmul(bank[:, q * L:(q + 1) * L], cx[:, q * P:(q + 1) * P], wk[:, :], start=True, stop=True)
                    a.then_inc(gfull[1], 1)
                    g_result(pe, gk(1, i, 3), 3)
                    for j in range(2):
                        bank = g_take(pe, gk(1, i, 4 + j), 4 + j)
                        pe.sem_inc(passed["pe"], 1)
                        for c in range(C):
                            a = pe.matmul(bank[0:L, 0:S], kv[:, 2 * j + c, :], XT[:, c, j * S:(j + 1) * S], start=c == 0, stop=c == 1)
                        a.then_inc(gfull[j], 1)
                    for j in range(2):
                        g_result(pe, gk(1, i, 4 + j), 4 + j)
                        bank = g_take(pe, gk(1, i, 6 + j), 6 + j)
                        for q in range(2):
                            a = pe.matmul(bank[:, q * D:(q + 1) * D], oT[:, j * S + q * P:j * S + (q + 1) * P],
                                          kvT[:, j * S:(j + 1) * S], start=True, stop=True)
                        a.then_inc(gfull[j], 1)
            if stop > 2:
                pe.wait_ge(signs, 2)
                with pe.Fori(0, PAIRS) as i:
                    pe.wait_ge(f_step, i * 11 + 11)
                    transpose_pair(2, i, xn)
                    for n in range(2):
                        g_result(pe, gk(2, i, n), n)
                    for s in range(8 + 2):
                        if s < 8:
                            v, q, hh = i * 8 + s, s // 2, s % 2
                            pe.wait_ge(f_silu.sem, f_silu.free(v, 2))
                            pe.wait_ge(f_pr.sem, f_pr.free(v, 2))
                            for u, bank in ((0, pS[hh]), (1, pT[hh])):
                                for c in range(C):
                                    a = pe.matmul(bank[:, :], qT[:, c, q * P:(q + 1) * P], sgu[:, u, c, hh * 512:(hh + 1) * 512],
                                                  start=c == 0, stop=c == 1)
                            a.then_inc(f_gu.sem, 1)
                        if 0 <= s - 1 < 8:
                            v, hh = i * 8 + (s - 1), (s - 1) % 2
                            pe.wait_ge(f_pr.sem, f_pr.done(v))
                            pe.wait_ge(f_prT.sem, f_prT.free(v, 2))
                            for w in range(4):
                                a = pe.transpose(pO[hh][:, w * P:(w + 1) * P], pr[:, hh, w * P:(w + 1) * P], ident[:, :])
                            a.then_inc(f_tr.sem, 1)
                        if s - 2 >= 0:
                            v, q, hh = i * 8 + (s - 2), (s - 2) // 2, (s - 2) % 2
                            pe.wait_ge(f_prT.sem, f_prT.done(v))
                            n = 2 + q // 2
                            if q % 2 == 0 and hh == 0:
                                g_take(pe, gk(2, i, n), n)
                            for w in range(4):
                                a = pe.matmul(pG[n % 2][:, (q % 2) * D:(q % 2 + 1) * D], prT[:, hh, w * P:(w + 1) * P],
                                              wd[:, 4 * hh + w, :], start=hh == 0 and w == 0, stop=hh == 1 and w == 3)
                            if q % 2 == 1 and hh == 1:
                                a.then_inc(gfull[n % 2], 1)
            if stop > 3:
                pe.wait_ge(x_done, START + 12)
                transpose_all(3)
                with pe.Fori(0, G) as g:
                    pe.wait_ge(ld["wide"], (g + 1) * 48)
                    for n in range(2, 4):
                        pe.wait_ge(gread[n % 2], gk0(3, n) + 1)
                    for h in range(QPG + 1):
                        for half in range(2):
                            n = 2 * h + half
                            bank = g_take(pe, gk(3, g, n), n)
                            for c in range(C):
                                w = ww[:, c * 512 + h * P:c * 512 + (h + 1) * P] if h < QPG else ww[:, 1024 + c * 256:1024 + c * 256 + P]
                                a = pe.matmul(bank[:, :], w, XT[:, c, half * 512:(half + 1) * 512], start=c == 0, stop=c == 1)
                            a.then_inc(gfull[n % 2], 1)
                    for half in range(2):
                        n = 10 + half
                        bank = g_take(pe, gk(3, g, n), n)
                        for q in range(4):
                            for c in range(C):
                                a = pe.matmul(bank[:, q * P:(q + 1) * P], XT[:, c, (4 * half + q) * P:(4 * half + q + 1) * P],
                                              ww[:, 1024 + c * 256 + P:1024 + (c + 1) * 256], start=c == 0, stop=c == 1)
                        a.then_inc(gfull[n % 2], 1)
                    for n in (10, 11):
                        g_result(pe, gk(3, g, n), n)
                    pe.wait_ge(ld["wo"], (g + 1) * 16)
                    attention(3, g, ww[:, 1536:2560])
            if stop > 4:
                pe.wait_ge(ld["x2"], 48)
                with pe.Fori(0, PAIRS) as i:
                    pair_loaded(4, i)
                    transpose_pair(4, i, xs)
                    narrow_projections(4, i)
                    for n in (2, 3, 6, 7):
                        g_result(pe, gk(4, i, n), n)
                    attention(4, i, xo)
            if stop > 5:
                pe.wait_ge(ld["e"], 32)
                pe.wait_ge(x_done, START + 20)
                transpose_all(5)
                for n in (2, 3):
                    g_result(pe, gk0(5, n), n)
                for n in (4, 5):
                    bank = g_take(pe, gk0(5, n), n)
                    for q in range(4):
                        for c in range(C):
                            tile = 4 * (n - 4) + q
                            a = pe.matmul(bank[:, q * E:(q + 1) * E], XT[:, c, tile * P:(tile + 1) * P], gw[:, c, :],
                                          start=c == 0, stop=c == 1)
                    a.then_inc(gfull[n % 2], 1)

                def gate_up(v, q):
                    s, half = (q // 2) % 2, q % 2
                    pe.wait_ge(e_silu.sem, e_silu.free(v, 2))
                    pe.wait_ge(e_h.sem, e_h.free(v, 2))
                    for u, bank in ((0, pS[half]), (1, pT[half])):
                        for c in range(C):
                            o = u * D + c * P
                            a = pe.matmul(bank[:, :], we[:, s, o:o + P], XT[:, c, half * 512:(half + 1) * 512], start=c == 0, stop=c == 1)
                    a.then_inc(e_gu.sem, 1)

                def down(i, v, q):
                    pe.wait_ge(e_h.sem, e_h.done(v))
                    for n in (2 * q, 2 * q + 1):
                        bank = g_take(pe, gk(5, i, n), n)
                        for w in range(2):
                            o = (2 * (n % 2) + w) * P
                            a = pe.matmul(bank[:, w * D:(w + 1) * D], hid[:, q % 4, o:o + P], we[:, (q // 2) % 2, 2 * D:3 * D],
                                          start=True, stop=True)
                        a.then_inc(gfull[n % 2], 1)

                with pe.Fori(0, E // 2) as i:
                    for q in range(4 + 1):
                        if q < 4:
                            if q % 2 == 0:
                                pe.wait_ge(ld[f"exp{q // 2}"], (i + 1) * 16)
                            gate_up(i * 4 + q, q)
                        if q >= 1:
                            down(i, i * 4 + (q - 1), q - 1)
                pe.wait_ge(ld["exp0"], (E // 2 + 1) * 16)
                for q in range(2 + 1):
                    if q < 2:
                        gate_up(2 * E + q, q)
                    if q >= 1:
                        down(E // 2, 2 * E + q - 1, q - 1)


def position_table():
    pos = np.arange(S, dtype=np.float32)[:, None]
    i = np.arange(0, DW, 2, dtype=np.float32)
    ang = pos * np.exp(-(np.log(np.float32(10000.0)) * i / np.float32(DW))).astype(np.float32)
    pe = np.zeros((S, DW), np.float32)
    pe[:, 0::2] = np.sin(ang)
    pe[:, 1::2] = np.cos(ang)
    return np.ascontiguousarray(np.stack([pe.T * np.float32(DW ** -0.5), pe.T], axis=1))


def layouts(a):
    wq = a["L1_attn_wq"].reshape(C, P, G, 512).transpose(2, 1, 0, 3).reshape(G, P, 1024)
    wkv = a["L1_attn_wkv"].reshape(C, P, G, 256).transpose(2, 1, 0, 3).reshape(G, P, 512)
    wo = a["L1_attn_wo"].reshape(G, QPG, P, D).transpose(0, 2, 1, 3).reshape(G, P, 1024)
    bkv = a["L1_attn_bkv"].reshape(G, 2, P)
    bq = a["L1_attn_bq"].reshape(G, QPG, P).transpose(0, 2, 1)

    def expert(wg, wu, wd):
        n = wg.shape[0]
        up = [w.reshape(n, I, C, P).transpose(0, 3, 2, 1).reshape(n, P, C * I) for w in (wg, wu)]
        return np.concatenate([*up, wd.transpose(0, 2, 1)], axis=2)

    shared = expert(a["L1_ffn_sw_gate"][None], a["L1_ffn_sw_up"][None], a["L1_ffn_sw_down"][None])
    out = {
        "x": a["x"].reshape(B * S, D),
        "ctxT": a["ctx_512"].reshape(B * S, L).T,
        "wqkvT": a["L0_attn_Wqkv"].T,
        "bqk": a["L0_attn_bqkv"][:2 * D].reshape(4, P).T,
        "bv": a["L0_attn_bqkv"][2 * D:],
        "woutT": a["L0_attn_Wout"].T,
        "bout": a["L0_attn_bout"],
        "wkT": a["L0_xattn_W_k"].T,
        "bk": a["L0_xattn_b_k"],
        "gamma": a["L0_xattn_ln_gamma"],
        "beta": a["L0_xattn_ln_beta"],
        "wgT": a["L0_ffn_W_g"].T,
        "wuT": a["L0_ffn_W_u"].T,
        "wdT": a["L0_ffn_W_d"].T,
        "wwide": np.concatenate([wq, wkv, wo], axis=2),
        "bwide": np.concatenate([bq, bkv[:, 0, :, None], np.zeros((G, P, 3), np.float32)], axis=2),
        "bvwide": bkv[:, 1, :],
        "pe": position_table(),
        "xqT": a["L1_xattn_Wq"].T,
        "xkvT": a["L1_xattn_Wkv_expand"].T,
        "xoT": a["L1_xattn_Wout"].T,
        "gateT": a["L1_ffn_gate_w"].T,
        "ebias": a["L1_ffn_expert_bias"],
        "wexp": np.concatenate([expert(a["L1_ffn_w_gate"], a["L1_ffn_w_up"], a["L1_ffn_w_down"]), shared]),
    }
    return {k: np.ascontiguousarray(v) for k, v in out.items()}


def kernel(**inputs):
    from concourse import bacc
    from concourse.bass_utils import run_bass_kernel_spmd as run

    arrays = layouts({k: np.asarray(v) for k, v in inputs.items()})
    nc = bacc.Bacc("TRN2", target_bir_lowering=False, num_devices=1)
    t = {k: nc.dram_tensor(f"in_{k}", v.shape, mybir.dt.from_np(v.dtype), kind="ExternalInput").ap()
         for k, v in arrays.items()}
    t["out"] = nc.dram_tensor("out", (B * S, D), F32, kind="ExternalOutput").ap()
    build(nc, t)
    res = run(nc, [{f"in_{k}": v for k, v in arrays.items()}], core_ids=[0])
    return res.results[0]["out"].reshape(B, S, D)
```

```python
from contextlib import ExitStack

import numpy as np
import concourse.bass as bass
from concourse import mybir

F32 = mybir.dt.float32
BF16 = mybir.dt.bfloat16
U32 = mybir.dt.uint32
ACT = mybir.ActivationFunctionType
ALU = mybir.AluOpType
AX = mybir.AxisListType

P = 128
B, S, D = 4, 256, 256
TILES = B * S // P
C = D // P
NH, HD = 16, 16
G, QPG, DW = 4, 4, 128
L = 64
FF = 1024
E, I, TOPK = 16, 128, 4
EPS_LN, EPS_X, EPS_F = 1e-5, 1e-6, 1e-8
NEG = -1e30
ROUND = 1.5 * 2.0 ** 23
AHEAD = 4
START = 1

UN = 12
UW = 12
N_P, N_PT = 4, 3


class Steps:

    def __init__(self, sem):
        self.sem = sem

    def done(self, u):
        return u + (1 + AHEAD)

    def free(self, u, ring):
        return u + (1 + AHEAD - ring)


class BankUses:

    def __init__(self):
        self.count = [START, START, START]
        self.turn = 0
        self.of = {}

    def take(self, key):
        n = self.turn
        self.of[key] = (n, self.count[n])
        self.count[n] += 1
        self.turn = (n + 1) % 3
        return self.of[key]


def build(nc, t, stop=6):
    ctx = ExitStack()
    with ctx:
        def sb(name, shape, dt=F32):
            return ctx.enter_context(nc.sbuf_tensor(name, shape, dt))

        def sem(name):
            return ctx.enter_context(nc.semaphore(name))

        X = sb("X", [P, TILES, D])
        XT = sb("XT", [P, C, B * S])
        ident = sb("ident", [P, P])
        identb = sb("identb", [P, P], BF16)
        tri = sb("tri", [P, 4, P], BF16)
        stat = sb("stat", [P, B, 2, 6])
        mv = sb("mv", [P, B, 2, 2])
        veps = sb("veps", [P, B, 2])
        rstd = sb("rstd", [P, B, 2])
        mhalf = sb("mhalf", [P, 8])
        wqkv = sb("wqkv", [P, C, 3 * D])
        wout = sb("wout", [P, C, D])
        bqk = sb("bqk", [P, 4])
        bqs = sb("bqs", [P, 2])
        bv = sb("bv", [P, D])
        bout = sb("bout", [P, D])
        qk = sb("qk", [P, 2, 4, S])
        kbd = sb("kbd", [P, 2, C, 8, S])
        vn = sb("vn", [P, 2, 2, NH, 32])
        an = sb("an", [P, 2, C, S])
        prob = sb("prob", [P, N_P, 512])
        probT = sb("probT", [P, N_PT, 512])
        nmax = sb("nmax", [P, N_P, 4])
        rsum = sb("rsum", [P, N_P, 4])
        rinv = sb("rinv", [P, N_P, 4])
        cx = sb("cx", [L, B * S])
        wk = sb("wk", [L, L])
        bk = sb("bk", [L, 1])
        bkb = sb("bkb", [P, L])
        gam = sb("gam", [P, D])
        bet = sb("bet", [P, D])
        kvT = sb("kvT", [L, S])
        kv = sb("kv", [P, 2, L])
        oT = sb("oT", [L, S])
        z = sb("z", [P, 2, D])
        xst = sb("xst", [P, 2, 6])
        xmv = sb("xmv", [P, 2, 2])
        xve = sb("xve", [P, 2])
        xrs = sb("xrs", [P, 2])
        xnm = sb("xnm", [P, 2])
        xsm = sb("xsm", [P, 2])
        xri = sb("xri", [P, 2])
        sgu = sb("sgu", [P, 2, C, FF], BF16)
        wd = sb("wd", [P, FF // P, D])
        qT = sb("qT", [P, C, S], BF16)
        xn = sb("xn", [P, 2, D])
        fst = sb("fst", [P, 2, 6])
        fmv = sb("fmv", [P, 2, 2])
        fve = sb("fve", [P, 2])
        frs = sb("frs", [P, 2])
        amax = sb("amax", [P, 2])
        fsc = sb("fsc", [P, 2])
        finv = sb("finv", [P, 2])
        sg = sb("sg", [P, 2, 512])
        pr = sb("pr", [P, 2, 512])
        prT = sb("prT", [P, 4, 512])
        ww = sb("ww", [P, 2560])
        bw = sb("bw", [P, 8])
        bws = sb("bws", [P, 8])
        bvw = sb("bvw", [P, P])
        pes = sb("pes", [P, 2, S])
        peb = sb("peb", [P, 5, S])
        qw = sb("qw", [P, QPG, B * S])
        kw = sb("kw", [P, B * S])
        vw = sb("vw", [P, TILES, DW])
        aw = sb("aw", [P, 2, QPG, S])
        xq = sb("xq", [P, C, D])
        xkv = sb("xkv", [L, 2 * D])
        xo = sb("xo", [P, C, D])
        gw = sb("gw", [P, C, E])
        eb = sb("eb", [P, E])
        we = wqkv[:, :, :]
        sc_ = sb("sc_", [P, TILES, E])
        sel = sb("sel", [P, TILES, E])
        top = sb("top", [P, TILES, 8])
        topi = sb("topi", [P, TILES, 8], U32)
        topf = sb("topf", [P, TILES, 8])
        iota = sb("iota", [P, E])
        eq = sb("eq", [P, TILES, TOPK, E])
        pick = sb("pick", [P, TILES, E])
        cws = sb("cws", [P, TILES, E])
        csum = sb("csum", [P, TILES])
        cinv = sb("cinv", [P, TILES])
        cw = sb("cw", [P, TILES, E])
        cwe = sb("cwe", [P, 2, TILES])
        raw = qw[:, :, :].rearrange("p (u c) n -> p u c n", u=2)
        hid = aw[:, :, :, :].rearrange("p a h n -> p (a h n)").rearrange("p (s n) -> p s n", s=4)

        def bank(name):
            return ctx.enter_context(nc.psum_tensor(name, [P, 512], F32))

        pS = [bank("pS0"), bank("pS1")]
        pT = bank("pT")
        pO = [bank("pO0"), bank("pO1")]
        pG = [bank("pG0"), bank("pG1"), bank("pG2")]

        ld = {k: sem("loaded_" + k) for k in ("x0", "x", "qkv", "a0", "x1", "ctx", "f", "w", "x2", "e",
                                              "wide", "wo", "exp0", "exp1")}
        consts = sem("consts")
        zeroed = sem("zeroed")
        gfull = [sem(f"general{n}_full") for n in range(3)]
        gread = [sem(f"general{n}_read") for n in range(3)]
        k_spread = [[sem(f"keys{j}{tl}_spread") for tl in range(C)] for j in range(2)]
        passed = {e: sem("passed_" + e) for e in ("dve", "pe", "sp")}
        score = Steps(sem("score_done"))
        maxed = Steps(sem("max_done"))
        exped = Steps(sem("exp_done"))
        recip = Steps(sem("recip_done"))
        normed = Steps(sem("norm_done"))
        transp = Steps(sem("transpose_done"))
        copied = Steps(sem("probT_done"))
        pved = Steps(sem("pv_done"))
        oread = Steps(sem("out_read"))
        bias_q = sem("bias_q")
        ln_step = [sem(f"ln{q}_step") for q in range(6)]
        ln_rstd = [sem(f"ln{q}_rstd") for q in range(6)]
        x_done = [sem(f"x{q}_done") for q in range(6)]
        x1_step = sem("x1_step")
        x1_rstd = sem("x1_rstd")
        x1_exp = sem("x1_exp")
        signs = sem("signs")
        f_step = sem("f_step")
        f_rstd = sem("f_rstd")
        w_bias = sem("w_bias")
        e_step = sem("e_step")
        e_gu = Steps(sem("e_gate_up"))
        e_silu = Steps(sem("e_silu"))
        e_h = Steps(sem("e_hidden"))
        e_cw = sem("e_cw")
        stored = sem("stored")

        uses = BankUses()
        LOOP_USES = {3: (0, 16, G), 5: (2, 8, E // 2)}
        base = {}

        def loop_uses(sub, extra=0):
            first, per, count = LOOP_USES[sub]
            base[sub] = list(uses.count)
            for n in range(2):
                uses.count[n] += (first + per * count + extra) // 2

        def gk(sub, i, n):
            first, per, _ = LOOP_USES[sub]
            return i * (per // 2) + (base[sub][n % 2] + (first + n) // 2)

        def g_take(pe, k, n):
            pe.wait_ge(gread[n], k)
            return pG[n]

        def g_wait(eng, k, n):
            eng.wait_ge(gfull[n], k + 1)
            return pG[n]

        def g_result(eng, k, n):
            eng.wait_ge(gread[n], k + 1)

        def full(eng, *key):
            n, k = uses.of[key]
            return g_wait(eng, k, n), n

        def result(eng, *key):
            n, k = uses.of[key]
            g_result(eng, k, n)

        KINDS = (("first", 0), ("second", 0), ("second", 2))
        narrow_units = [(4 * hg + o, kind) for hg in range(4) for kind, o in KINDS]
        wide_units = [(o, kind) for b in range(B) for kind, o in KINDS]
        UNITS_AT = {0: 0, 3: B * UN, 4: B * UN + G * UW}
        OUTS_AT = {0: 0, 3: B * 2, 4: B * 2 + G * 8}

        def by_head(ap, kind):
            return ap.rearrange("p (h k) -> p h k", h=4 if kind == "first" else 2)

        FIRST_STEP = -13
        STEPS_END = {0: (B - 1) * UN + 53, 4: (B - 1) * UN + 22}
        LAST_AT = {0: 50, 4: 20}
        LAST_AT = {0: 50, 4: 20}
        LAST_AT = {0: 50, 4: 20}
        SPREADS = {0: 0, 4: B // 2}

        def tasks(sub, s):
            return [(b, s - UN * b) for b in range(B)]

        def unit(sub, s):
            if 0 <= s < B * UN:
                return s // UN, s % UN, UNITS_AT[sub] + s
            return None

        def f_unit(o, at):
            return (o - at) // 2 if 0 <= o - at < 8 and (o - at) % 2 == 0 else None

        LN_STEPS = [4, 3, 3, 3, 3, 3]

        block = ctx.enter_context(nc.Block())

        @block.tensor
        def _(pe):
            for st in (score, transp, pved, e_gu):
                pe.sem_inc(st.sem, AHEAD)
            for st in gfull:
                pe.sem_inc(st, START)

            def take(*key):
                n, k = uses.take(key)
                return g_take(pe, k, n), n

            def score_unit(sub, u0, u, b, h0, kind):
                pe.wait_ge(exped.sem, exped.free(u0 + u, 2))
                bank = pS[u % 2]
                v = by_head(bank[:, :], kind)
                if kind == "first":
                    pe.matmul(v, identb[:, :], tri[:, :, :], start=True, stop=False, skip_group_check=True)
                    q0, nk, nh = 0, P, 4
                else:
                    pe.matmul(v[:, :, P:S], identb[:, :], tri[:, 0:2, :], start=True, stop=False, skip_group_check=True)
                    q0, nk, nh = P, S, 2
                if sub == 3:
                    for h in range(nh):
                        a = pe.matmul(v[:, h, :], qw[:, h0 + h, b * S + q0:b * S + q0 + P], kw[:, b * S:b * S + nk],
                                      start=False, stop=True, skip_group_check=True)
                else:
                    tl, g = h0 // 8, h0 % 8
                    a = pe.matmul(v, qk[:, b % 2, tl, q0:q0 + P], kbd[:, b % 2, tl, g:g + nh, 0:nk],
                                  start=False, stop=True, skip_group_check=True)
                a.then_inc(score.sem, 1)

            def transpose_unit(u0, u):
                pe.wait_ge(normed.sem, normed.done(u0 + u))
                pe.wait_ge(copied.sem, copied.free(u0 + u, 1))
                for q in range(4):
                    a = pe.transpose(pT[:, q * P:(q + 1) * P], prob[:, u % N_P, q * P:(q + 1) * P], ident[:, :])
                a.then_inc(transp.sem, 1)

            def value_unit(sub, u0, o, o0, u, first, b, h0, kind):
                if first:
                    pe.wait_ge(oread.sem, oread.free(o0 + o, 2))
                pe.wait_ge(copied.sem, copied.done(u0 + u))
                bank = pO[o % 2]
                for q in range(4):
                    h, kt = (h0 + q, 0) if kind == "first" else (h0 + q // 2, q % 2)
                    src = probT[:, u % N_PT, q * P:(q + 1) * P]
                    if sub == 3:
                        a = pe.matmul(bank[:, h * P:(h + 1) * P], vw[:, 2 * b + kt, :], src, start=kt == 0,
                                      stop=kind == "first" or kt == 1, skip_group_check=True)
                    else:
                        r, q0 = (h % 8) // 2, 0 if kind == "first" else P
                        a = pe.matmul(bank[32 * r:32 * r + 32, q0:q0 + P], vn[:, b % 2, kt, h, :], src,
                                      start=kind == "first" and h % 2 == 0,
                                      stop=h % 2 == 1 and (kind == "first" or kt == 1), skip_group_check=True)
                a.then_inc(pved.sem, 1)

            def transpose_batch(src, *key):
                bank, n = take(*key)
                for c in range(C):
                    for q in range(2):
                        a = pe.transpose(bank[:, c * S + q * P:c * S + (q + 1) * P], src[:, q, c * P:(c + 1) * P], ident[:, :])
                a.then_inc(gfull[n], 1)

            def project(sub, b, what):
                if what == "q":
                    result(pe, "xT", sub, b)
                bank, n = take(what, sub, b)
                for m in range(2):
                    if sub == 4 and what == "k":
                        a = pe.matmul(bank[:, m * S:(m + 1) * S], xkv[:, m * P:(m + 1) * P], cx[:, b * S:(b + 1) * S],
                                      start=True, stop=True)
                        continue
                    w, w0 = (wqkv, (m if what == "q" else 2 + m) * P) if sub == 0 else (xq, m * P)
                    for c in range(C):
                        a = pe.matmul(bank[:, m * S:(m + 1) * S], w[:, c, w0:w0 + P], XT[:, c, b * S:(b + 1) * S],
                                      start=c == 0, stop=c == 1)
                a.then_inc(gfull[n], 1)

            def project_values(sub, b):
                bank, n = take("v", sub, b)
                for q in range(2):
                    tok = b * S + q * P
                    if sub == 4:
                        a = pe.matmul(bank[:, q * D:(q + 1) * D], cx[:, tok:tok + P], xkv[:, D:2 * D], start=True, stop=True)
                    else:
                        for c in range(C):
                            a = pe.matmul(bank[:, q * D:(q + 1) * D], XT[:, c, tok:tok + P], wqkv[:, c, 2 * D:3 * D],
                                          start=c == 0, stop=c == 1)
                a.then_inc(gfull[n], 1)

            def out_projection(sub, b, wo):
                if sub == 0 and b == 0:
                    pe.wait_ge(ld["a0"], 64)
                pe.wait_ge(oread.sem, oread.done(OUTS_AT[sub] + 2 * b + 1))
                bank, n = take("out", sub, b)
                for q in range(2):
                    for c in range(C):
                        a = pe.matmul(bank[:, q * D:(q + 1) * D], an[:, b % 2, c, q * P:(q + 1) * P], wo[:, c, :],
                                      start=c == 0, stop=c == 1)
                a.then_inc(gfull[n], 1)

            def gated_softmax(b, o):
                bs = slice(b * S, (b + 1) * S)
                if o == 18:
                    bank, n = take("kvT", b)
                    pe.matmul(bank[0:L, 0:S], wk[:, :], cx[:, bs], start=True, stop=True).then_inc(gfull[n], 1)
                    bank, n = take("kv", b)
                    for q in range(2):
                        a = pe.matmul(bank[:, q * L:(q + 1) * L], cx[:, b * S + q * P:b * S + (q + 1) * P], wk[:, :],
                                      start=True, stop=True)
                    a.then_inc(gfull[n], 1)
                if o == 20:
                    pe.wait_ge(x_done[0], b + 1)
                    transpose_batch(X[:, 2 * b:2 * b + 2, :], "x1T", b)
                if o == 22:
                    result(pe, "x1T", b)
                    result(pe, "kv", b)
                    bank, n = take("ctx", b)
                    for c in range(C):
                        a = pe.matmul(bank[0:L, 0:S], kv[:, c, :], XT[:, c, bs], start=c == 0, stop=c == 1)
                    a.then_inc(gfull[n], 1)
                if o == 24:
                    result(pe, "ctx", b)
                    result(pe, "kvT", b)
                    bank, n = take("sim", b)
                    for q in range(2):
                        a = pe.matmul(bank[:, q * D:(q + 1) * D], oT[:, q * P:(q + 1) * P], kvT[:, :], start=True, stop=True)
                    a.then_inc(gfull[n], 1)

            def feed_forward(b, o):
                if o == 34:
                    pe.wait_ge(f_step, 11 * b + 11)
                    transpose_batch(xn, "qT", b)
                for at, which in ((36, "gate"), (37, "up")):
                    k = f_unit(o, at)
                    if k is not None:
                        if k == 0:
                            result(pe, "qT", b)
                        if b == 0 and k == 0:
                            pe.wait_ge(signs, 4)
                        bank, n = take(which, b, k)
                        for c in range(C):
                            a = pe.matmul(bank[:, :], qT[:, c, (k // 2) * P:(k // 2 + 1) * P],
                                          sgu[:, 0 if which == "gate" else 1, c, (k % 2) * 512:(k % 2 + 1) * 512],
                                          start=c == 0, stop=c == 1)
                        a.then_inc(gfull[n], 1)
                k = f_unit(o, 39)
                if k is not None:
                    result(pe, "up", b, k)
                    bank, n = take("prT", b, k)
                    for w in range(4):
                        a = pe.transpose(bank[:, w * P:(w + 1) * P], pr[:, k % 2, w * P:(w + 1) * P], ident[:, :])
                    a.then_inc(gfull[n], 1)
                if o in (43, 47):
                    q = (o - 43) // 4
                    pe.wait_ge(signs, 6)
                    for k in (2 * q, 2 * q + 1):
                        result(pe, "prT", b, k)
                    bank, n = take("down", b, q)
                    for w in range(8):
                        a = pe.matmul(bank[:, 0:D], prT[:, 2 * q + w // 4, (w % 4) * P:(w % 4 + 1) * P], wd[:, w, :],
                                      start=w == 0, stop=w == 7)
                    a.then_inc(gfull[n], 1)

            def stream(sub, wo):
                for s in range(FIRST_STEP, STEPS_END[sub]):
                    at = unit(sub, s)
                    if at is not None:
                        b, k, _ = at
                        if k == 0:
                            result(pe, "q", sub, b)
                            result(pe, "v", sub, b)
                        if k in (0, 6):
                            pe.wait_ge(k_spread[b % 2][k // 6], 8 * 16 * (SPREADS[sub] + b // 2 + 1))
                        score_unit(sub, UNITS_AT[sub], s, b, *narrow_units[k])
                    if unit(sub, s - 3) is not None:
                        transpose_unit(UNITS_AT[sub], s - 3)
                    at = unit(sub, s - 4)
                    if at is not None:
                        b, k, _ = at
                        value_unit(sub, UNITS_AT[sub], 2 * b + k // 6, OUTS_AT[sub], s - 4, k % 6 == 0, b, *narrow_units[k])
                    for b, o in tasks(sub, s):
                        if o == -11:
                            if sub == 0:
                                pe.wait_ge(ld["x" if b else "x0"], 16)
                            else:
                                pe.wait_ge(x_done[3], b + 1)
                            transpose_batch(X[:, 2 * b:2 * b + 2, :], "xT", sub, b)
                        if o == -10:
                            project(sub, b, "q")
                        if o == -9:
                            project(sub, b, "k")
                        if o == -8:
                            project_values(sub, b)
                        if o == 17:
                            out_projection(sub, b, wo)
                        if sub == 0 and stop > 1:
                            gated_softmax(b, o)
                        if sub == 0 and stop > 2:
                            feed_forward(b, o)
                        if o == LAST_AT[sub] and stop > (3 if sub == 0 else 5):
                            pe.wait_ge(x_done[2 if sub == 0 else 4], b + 1)
                            transpose_batch(X[:, 2 * b:2 * b + 2, :], "last", sub, b)

            def wide_attention(g, wo):
                u0, o0 = g * UW + UNITS_AT[3], g * 8 + OUTS_AT[3]
                for s in range(UW + 7):
                    if s < UW:
                        score_unit(3, u0, s, s // 3, *wide_units[s])
                    if 0 <= s - 3 < UW:
                        transpose_unit(u0, s - 3)
                    u = s - 4
                    if 0 <= u < UW:
                        value_unit(3, u0, 2 * (u // 3) + (u % 3 > 0), o0, u, u % 3 < 2, u // 3, *wide_units[u])
                    j, ends = divmod(s - 6, 3)
                    if 0 <= j < B and ends == 2:
                        n = 12 + j
                        pe.wait_ge(oread.sem, oread.done(o0 + (2 * j + 1)))
                        bank = g_take(pe, gk(3, g, n), n % 2)
                        for q in range(2):
                            for c in range(QPG):
                                a = pe.matmul(bank[:, q * D:(q + 1) * D], aw[:, j % 2, c, q * P:(q + 1) * P],
                                              wo[:, c * D:(c + 1) * D], start=c == 0, stop=c == QPG - 1)
                        a.then_inc(gfull[n % 2], 1)

            pe.wait_ge(consts, 7)
            pe.wait_ge(ld["qkv"], 48)
            pe.wait_ge(ld["ctx"], 16)
            stream(0, wout)
            if stop > 3:
                loop_uses(3)
                for b in range(B):
                    result(pe, "last", 0, b)
                with pe.Fori(0, G) as g:
                    pe.wait_ge(ld["wide"], (g + 1) * 48)
                    for h in range(QPG + 1):
                        for half in range(2):
                            n = 2 * h + half
                            bank = g_take(pe, gk(3, g, n), n % 2)
                            for c in range(C):
                                w = ww[:, c * 512 + h * P:c * 512 + (h + 1) * P] if h < QPG else ww[:, 1024 + c * 256:1024 + c * 256 + P]
                                a = pe.matmul(bank[:, :], w, XT[:, c, half * 512:(half + 1) * 512], start=c == 0, stop=c == 1)
                            a.then_inc(gfull[n % 2], 1)
                    for half in range(2):
                        n = 10 + half
                        bank = g_take(pe, gk(3, g, n), n % 2)
                        for q in range(4):
                            for c in range(C):
                                a = pe.matmul(bank[:, q * P:(q + 1) * P], XT[:, c, (4 * half + q) * P:(4 * half + q + 1) * P],
                                              ww[:, 1024 + c * 256 + P:1024 + (c + 1) * 256], start=c == 0, stop=c == 1)
                        a.then_inc(gfull[n % 2], 1)
                    for n in (10, 11):
                        g_result(pe, gk(3, g, n), n % 2)
                    pe.wait_ge(ld["wo"], (g + 1) * 16)
                    wide_attention(g, ww[:, 1536:2560])
            if stop > 4:
                pe.wait_ge(ld["x2"], 48)
                stream(4, xo)
            if stop > 5:
                pe.wait_ge(ld["e"], 32)
                loop_uses(5, extra=4)
                for b in range(B):
                    result(pe, "last", 4, b)
                for n in (0, 1):
                    bank = g_take(pe, base[5][n], n)
                    for q in range(4):
                        for c in range(C):
                            tile = 4 * n + q
                            a = pe.matmul(bank[:, q * E:(q + 1) * E], XT[:, c, tile * P:(tile + 1) * P], gw[:, c, :],
                                          start=c == 0, stop=c == 1)
                    a.then_inc(gfull[n % 2], 1)

                def gate_up(v, q):
                    s, half = (q // 2) % 2, q % 2
                    pe.wait_ge(e_silu.sem, e_silu.free(v, 2))
                    pe.wait_ge(e_h.sem, e_h.free(v, 2))
                    for u, bank in ((0, pS[half]), (1, (pT, pG[2])[half])):
                        for c in range(C):
                            o = u * D + c * P
                            a = pe.matmul(bank[:, :], we[:, s, o:o + P], XT[:, c, half * 512:(half + 1) * 512], start=c == 0, stop=c == 1)
                    a.then_inc(e_gu.sem, 1)

                def down(i, v, q):
                    pe.wait_ge(e_h.sem, e_h.done(v))
                    for n in (2 * q, 2 * q + 1):
                        bank = g_take(pe, gk(5, i, n), n % 2)
                        for w in range(2):
                            o = (2 * (n % 2) + w) * P
                            a = pe.matmul(bank[:, w * D:(w + 1) * D], hid[:, q % 4, o:o + P], we[:, (q // 2) % 2, 2 * D:3 * D],
                                          start=True, stop=True)
                        a.then_inc(gfull[n % 2], 1)

                with pe.Fori(0, E // 2) as i:
                    for q in range(4 + 1):
                        if q < 4:
                            if q % 2 == 0:
                                pe.wait_ge(ld[f"exp{q // 2}"], (i + 1) * 16)
                            gate_up(i * 4 + q, q)
                        if q >= 1:
                            down(i, i * 4 + (q - 1), q - 1)
                pe.wait_ge(ld["exp0"], (E // 2 + 1) * 16)
                for q in range(2 + 1):
                    if q < 2:
                        gate_up(2 * E + q, q)
                    if q >= 1:
                        down(E // 2, 2 * E + q - 1, q - 1)
        @block.sync
        def _(sp):
            def load(dst, src, key):
                sp.dma_start(dst, src).then_inc(ld[key], 16)

            def spread_keys(sub, b):
                if sub == 4 or b >= 2:
                    last = UNITS_AT[4] + (b - 2) * UN + UN - 1 if sub == 4 and b >= 2 else (
                        B * UN - 1 if sub == 4 else (b - 2) * UN + UN - 1)
                    sp.wait_ge(score.sem, score.done(last))
                sp.wait_ge(zeroed, 2)
                result(sp, "k", sub, b)
                for tl in range(C):
                    for g in range(8):
                        sp.dma_start(kbd[16 * g:16 * g + 16, b % 2, tl, g, :],
                                     qk[16 * g:16 * g + 16, b % 2, 2 + tl, :]).then_inc(k_spread[b % 2][tl], 16)

            def load_group(g):
                load(ww[:, 0:1536], t["wwide"][g, :, 0:1536].rearrange("o p n -> p (o n)"), "wide")
                load(bw[:, :], t["bwide"][g, :, :].rearrange("o p n -> p (o n)"), "wide")
                load(bvw[:, :], t["bvwide"][g, :].rearrange("o n -> (o n)").partition_broadcast(P), "wide")

            def load_group_out(g):
                load(ww[:, 1536:2560], t["wwide"][g, :, 1536:2560].rearrange("o p n -> p (o n)"), "wo")

            x = t["x"].rearrange("(t p) d -> p t d", p=P)
            load(X[:, 0:2, :], x[:, 0:2, :], "x0")
            load(wqkv[:, :, :], t["wqkvT"].rearrange("(c p) n -> p c n", p=P), "qkv")
            load(bqk[:, :], t["bqk"], "qkv")
            load(bv[:, :], t["bv"].partition_broadcast(P), "qkv")
            load(X[:, 2:TILES, :], x[:, 2:TILES, :], "x")
            load(cx[:, :], t["ctxT"], "ctx")
            spread_keys(0, 0)
            load(bout[:, :], t["bout"].partition_broadcast(P), "a0")
            load(wout[:, :, :], t["woutT"].rearrange("(c p) n -> p c n", p=P), "a0")
            load(wk[:, :], t["wkT"], "a0")
            load(bk[:, :], t["bk"].rearrange("(l o) -> l o", o=1), "a0")
            load(bkb[:, :], t["bk"].partition_broadcast(P), "x1")
            load(gam[:, :], t["gamma"].partition_broadcast(P), "x1")
            load(bet[:, :], t["beta"].partition_broadcast(P), "x1")
            load(raw[:, 0, :, :], t["wgT"].rearrange("(c p) n -> p c n", p=P), "f")
            load(raw[:, 1, :, :], t["wuT"].rearrange("(c p) n -> p c n", p=P), "f")
            load(wd[:, :, :], t["wdT"].rearrange("(c p) n -> p c n", p=P), "f")
            spread_keys(0, 1)
            load(pes[:, :, :], t["pe"], "w")
            load(xq[:, :, :], t["xqT"].rearrange("(c p) n -> p c n", p=P), "x2")
            load(xkv[:, :], t["xkvT"], "x2")
            load(xo[:, :, :], t["xoT"].rearrange("(c p) n -> p c n", p=P), "x2")
            load(gw[:, :, :], t["gateT"].rearrange("(c p) n -> p c n", p=P), "e")
            load(eb[:, :], t["ebias"].partition_broadcast(P), "e")
            load_group(slice(0, 1))
            load_group_out(slice(0, 1))
            for b in range(2, B):
                spread_keys(0, b)
            if stop > 3:
                with sp.Fori(1, G) as g:
                    sp.wait_ge(gfull[1], gk(3, g, 11) - 7)
                    sp.wait_ge(gread[1], gk(3, g, 11) - 7)
                    sp.sem_inc(passed["sp"], 1)
                    sp.wait_ge(w_bias, g * 2 + START)
                    load_group(bass.ds(g, 1))
                    sp.wait_ge(gfull[1], gk(3, g, 15) - 7)
                    load_group_out(bass.ds(g, 1))
            if stop > 5:
                for s in range(2):
                    load(we[:, s, :], t["wexp"][s, :, :], f"exp{s}")
            if stop > 4:
                for b in range(B):
                    spread_keys(4, b)
            if stop > 5:
                with sp.Fori(1, E // 2) as i:
                    for s in range(2):
                        sp.wait_ge(gfull[1], gk(5, i, 4 * s + 3) - 3)
                        load(we[:, s, :], t["wexp"][bass.ds(i * 2 + s, 1), :, :].rearrange("o p n -> p (o n)"), f"exp{s}")
                sp.wait_ge(gfull[1], gk(5, E // 2, 3) - 3)
                load(we[:, 0, :], t["wexp"][E, :, :], "exp0")
            sp.wait_ge(x_done[stop - 1], B)
            sp.dma_start(t["out"].rearrange("(t p) d -> p t d", p=P), X[:, :, :]).then_inc(stored, 16)
            sp.wait_ge(stored, 16)

        @block.gpsimd
        def _(pool):
            pool.sem_inc(normed.sem, AHEAD)
            pool.memset(ident[:, :], 0.0).then_inc(consts, 1)
            pool.memset(tri[:, :, :], 0.0).then_inc(consts, 1)
            pool.memset(mhalf[:, :], -0.5).then_inc(consts, 1)
            pool.iota(iota[:, :], pattern=[[1, E]], base=0, channel_multiplier=0,
                      allow_small_or_imprecise_dtypes=True).then_inc(consts, 1)
            pool.wait_ge(consts, 2)
            pool.affine_select(out=ident[:, :], in_=ident[:, :], compare_op=ALU.not_equal, fill=1.0,
                               base=0, pattern=[[-1, P]], channel_multiplier=1).then_inc(consts, 1)
            pool.affine_select(out=tri[:, :, :], in_=tri[:, :, :], compare_op=ALU.is_ge, fill=NEG,
                               base=0, pattern=[[0, 4], [-1, P]], channel_multiplier=1).then_inc(consts, 1)
            pool.wait_ge(consts, 5)
            pool.tensor_copy(identb[:, :], ident[:, :]).then_inc(consts, 1)
            pool.memset(kbd[:, :, :, :, :], 0.0).then_inc(zeroed, 1)

            def norm(u0, u, kind):
                pool.wait_ge(recip.sem, recip.done(u0 + u))
                v = by_head(prob[:, u % N_P, :], kind)
                n = v.shape[1]
                pool.tensor_tensor(v, v, rinv[:, u % N_P, 0:n].unsqueeze(2).broadcast_to(list(v.shape)),
                                   ALU.mult).then_inc(normed.sem, 1)

            def ln_root(sub, b):
                pool.wait_ge(ln_step[sub], (b + 1) * LN_STEPS[sub])
                pool.tensor_tensor(rstd[:, b, :], veps[:, b, :], mhalf[:, 0:2], ALU.pow).then_inc(ln_rstd[sub], 1)

            def stream(sub):
                for s in range(FIRST_STEP, STEPS_END[sub]):
                    for b, o in tasks(sub, s):
                        if sub == 4 and o == -13:
                            ln_root(3, b)
                        if o == 18:
                            ln_root(sub, b)
                        if sub == 0 and stop > 1:
                            if o == 26:
                                pool.wait_ge(x1_step, 9 * b + 3)
                                pool.tensor_tensor(xrs[:, :], xve[:, :], mhalf[:, 0:2], ALU.pow).then_inc(x1_rstd, 1)
                            if o == 29:
                                ln_root(1, b)
                        if sub == 0 and stop > 2:
                            if o == 31:
                                pool.wait_ge(f_step, 11 * b + 3)
                                pool.tensor_tensor(frs[:, :], fve[:, :], mhalf[:, 0:2], ALU.pow).then_inc(f_rstd, 1)
                            if o == 48:
                                ln_root(2, b)
                    at = unit(sub, s - 1)
                    if at is not None:
                        norm(UNITS_AT[sub], s - 1, narrow_units[at[1]][1])

            stream(0)
            if stop > 3:
                with pool.Fori(0, G) as g:
                    for u in range(UW):
                        norm(g * UW + UNITS_AT[3], u, wide_units[u][1])
            if stop == 4:
                for b in range(B):
                    ln_root(3, b)
            if stop > 4:
                stream(4)
            if stop > 5:
                for b in range(B):
                    ln_root(5, b)

        @block.scalar
        def _(act):
            act.sem_inc(exped.sem, AHEAD)
            act.sem_inc(oread.sem, AHEAD)
            act.sem_inc(e_silu.sem, AHEAD)
            act.sem_inc(w_bias, START)

            def exp_unit(u0, u, kind):
                act.wait_ge(maxed.sem, maxed.done(u0 + u))
                act.wait_ge(transp.sem, transp.free(u0 + u, N_P))
                src, dst = by_head(pS[u % 2][:, :], kind), by_head(prob[:, u % N_P, :], kind)
                for h in range(src.shape[1]):
                    e = act.activation(dst[:, h, :], src[:, h, :], ACT.Exp, bias=nmax[:, u % N_P, h:h + 1],
                                       accum_out=rsum[:, u % N_P, h:h + 1])
                e.then_inc(exped.sem, 1)

            def evacuate_out(sub, s):
                at = unit(sub, s)
                if at is None or at[1] % 6 != 5:
                    return
                b, k, u = at
                act.wait_ge(pved.sem, pved.done(u))
                if b >= 2:
                    full(act, "out", sub, b - 2)
                elif sub == 4:
                    full(act, "out", 0, b + 2)
                act.activation(an[:, b % 2, k // 6, :], pO[k // 6][:, 0:S], ACT.Copy).then_inc(oread.sem, 1)

            def query_tiles(sub, b):
                if b >= 2:
                    act.wait_ge(score.sem, score.done(UNITS_AT[sub] + (b - 1) * UN - 1))
                elif sub == 4:
                    act.wait_ge(score.sem, score.done(B * UN - 1))
                bank, n = full(act, "q", sub, b)
                if sub == 0:
                    for m in range(2):
                        a = act.activation(qk[:, b % 2, m, :], bank[:, m * S:(m + 1) * S], ACT.Identity,
                                           bias=bqs[:, m:m + 1], scale=HD ** -0.5)
                else:
                    a = act.activation(qk[:, b % 2, 0:2, :], bank[:, :].rearrange("p (m s) -> p m s", m=2), ACT.Copy,
                                       scale=HD ** -0.5)
                a.then_inc(gread[n], 1)

            def key_tiles(sub, b):
                if sub == 4 or b >= 2:
                    for tl in range(C):
                        act.wait_ge(k_spread[b % 2][tl], 8 * 16 * (SPREADS[sub] + b // 2))
                bank, n = full(act, "k", sub, b)
                if sub == 0:
                    for m in range(2):
                        a = act.activation(qk[:, b % 2, 2 + m, :], bank[:, m * S:(m + 1) * S], ACT.Identity,
                                           bias=bqk[:, 2 + m:3 + m])
                else:
                    a = act.activation(qk[:, b % 2, 2:4, :], bank[:, :].rearrange("p (m s) -> p m s", m=2), ACT.Copy)
                a.then_inc(gread[n], 1)

            def gated_softmax(b, o):
                if o == 19:
                    if b == 0:
                        act.wait_ge(ld["a0"], 64)
                    if b > 0:
                        full(act, "sim", b - 1)
                    bank, n = full(act, "kvT", b)
                    act.activation(kvT[:, :], bank[0:L, 0:S], ACT.Identity, bias=bk[:, 0:1]).then_inc(gread[n], 1)
                if o == 23:
                    bank, n = full(act, "ctx", b)
                    act.activation(oT[:, :], bank[0:L, 0:S], ACT.Copy, scale=D ** -0.5).then_inc(gread[n], 1)
                if o == 25:
                    if b > 0:
                        act.wait_ge(x1_step, 9 * b)
                    bank, n = full(act, "sim", b)
                    act.activation(z[:, :, :], bank[:, :].rearrange("p (t d) -> p t d", t=2), ACT.Copy).then_inc(gread[n], 1)
                if o == 28:
                    act.wait_ge(x1_step, 9 * b + 7)
                    for q in range(2):
                        e = act.activation(z[:, q, :], z[:, q, :], ACT.Exp, bias=xnm[:, q:q + 1],
                                           accum_out=xsm[:, q:q + 1])
                    e.then_inc(x1_exp, 1)

            def feed_forward(b, o):
                k = f_unit(o, 37)
                if k is not None:
                    v = 4 * b + k
                    if v >= 2:
                        result(act, "up", (v - 2) // 4, (v - 2) % 4)
                    bank, n = full(act, "gate", b, k)
                    act.activation(sg[:, k % 2, :], bank[:, :], ACT.Silu, scale=finv[:, k // 2:k // 2 + 1]).then_inc(gread[n], 1)
                k = f_unit(o, 40)
                if k is not None:
                    if b > 0:
                        full(act, "down", b - 1, k // 2)
                    bank, n = full(act, "prT", b, k)
                    act.activation(prT[:, k, :], bank[:, :], ACT.Copy).then_inc(gread[n], 1)

            def sign_weights(s):
                if s == 0:
                    act.wait_ge(ld["f"], 48)
                if s < 4:
                    act.activation(sgu[:, s // 2, s % 2, :], raw[:, s // 2, s % 2, :], ACT.Sign).then_inc(signs, 1)
                else:
                    part = slice(4 * (s - 4), 4 * (s - 3))
                    act.activation(wd[:, part, :], wd[:, part, :], ACT.Sign).then_inc(signs, 1)

            def stream(sub):
                for s in range(FIRST_STEP, STEPS_END[sub]):
                    for b, o in tasks(sub, s):
                        if o == -9:
                            query_tiles(sub, b)
                        if o == -8:
                            key_tiles(sub, b)
                        if sub == 0 and stop > 1:
                            gated_softmax(b, o)
                        if sub == 0 and stop > 2:
                            feed_forward(b, o)
                    if sub == 0 and stop > 2 and 12 <= s < 18:
                        sign_weights(s - 12)
                    at = unit(sub, s)
                    if at is not None:
                        exp_unit(UNITS_AT[sub], s, narrow_units[at[1]][1])
                    evacuate_out(sub, s - 5)

            def wide_attention(g):
                u0, o0 = g * UW + UNITS_AT[3], g * 8 + OUTS_AT[3]
                for s in range(UW + 6):
                    if s < UW:
                        exp_unit(u0, s, wide_units[s][1])
                    u = s - 5
                    if 0 <= u < UW and u % 3 != 1:
                        o = 2 * (u // 3) + (u % 3 > 0)
                        act.wait_ge(pved.sem, pved.done(u0 + u))
                        b, half = o // 2, o % 2
                        n = 12 + (b - 2) % 4
                        act.wait_ge(gfull[n % 2], gk(3, g, n) + (1 if b >= 2 else -7))
                        act.activation(aw[:, b % 2, :, half * P:half * P + P],
                                       pO[o % 2][:, :].rearrange("p (h q) -> p h q", h=QPG),
                                       ACT.Copy).then_inc(oread.sem, 1)

            act.wait_ge(ld["qkv"], 48)
            act.activation(bqs[:, :], bqk[:, 0:2], ACT.Copy, scale=HD ** -0.5).then_inc(bias_q, 1)
            act.wait_ge(bias_q, 1)
            stream(0)
            if stop > 3:
                act.wait_ge(ld["w"], 16)
                with act.Fori(0, G) as g:
                    act.wait_ge(ld["wide"], (g + 1) * 48)
                    act.wait_ge(gread[1], gk(3, g, 9) - 7)
                    act.wait_ge(gread[0], gk(3, g, 8) - 7)
                    act.activation(bws[:, :], bw[:, :], ACT.Copy, scale=DW ** -0.5).then_inc(w_bias, 1)
                    act.wait_ge(w_bias, g * 2 + (START + 1))
                    for h in range(QPG + 1):
                        bias = bws[:, h:h + 1] if h < QPG else bw[:, h:h + 1]
                        a = act.activation(peb[:, h, :], pes[:, h // QPG, :], ACT.Identity, bias=bias)
                    a.then_inc(w_bias, 1)
                    wide_attention(g)
            if stop > 4:
                stream(4)
            if stop > 5:
                for n in (0, 1):
                    bank = g_wait(act, base[5][n], n)
                    act.activation(sc_[:, 4 * n:4 * (n + 1), :], bank[:, 0:4 * E].rearrange("p (t e) -> p t e", e=E),
                                   ACT.Sigmoid).then_inc(gread[n % 2], 1)

                def silu_unit(v, q):
                    act.wait_ge(e_gu.sem, e_gu.done(v))
                    act.wait_ge(e_h.sem, e_h.free(v, 2))
                    act.activation(sg[:, q % 2, :], pS[q % 2][:, :], ACT.Silu).then_inc(e_silu.sem, 1)

                with act.Fori(0, E // 2) as i:
                    for q in range(4):
                        silu_unit(i * 4 + q, q)
                for q in range(2):
                    silu_unit(2 * E + q, q)

        @block.vector
        def _(dve):
            for st in (maxed, recip, copied, e_h):
                dve.sem_inc(st.sem, AHEAD)
            for st in gread:
                dve.sem_inc(st, START)
            dve.memset(vn[:, :, :, :, :], 0.0).then_inc(zeroed, 1)

            def max_unit(u0, u, kind):
                dve.wait_ge(score.sem, score.done(u0 + u))
                v = by_head(pS[u % 2][:, :], kind)
                dve.reduce_max(nmax[:, u % N_P, 0:v.shape[1]], v, AX.X, negate=True).then_inc(maxed.sem, 1)

            def recip_unit(u0, u, kind):
                dve.wait_ge(exped.sem, exped.done(u0 + u))
                dve.wait_ge(normed.sem, normed.free(u0 + u, N_P))
                n = 4 if kind == "first" else 2
                dve.reciprocal(rinv[:, u % N_P, 0:n], rsum[:, u % N_P, 0:n]).then_inc(recip.sem, 1)

            def copy_unit(u0, u):
                dve.wait_ge(transp.sem, transp.done(u0 + u))
                dve.wait_ge(pved.sem, pved.free(u0 + u, N_PT))
                dve.tensor_copy(probT[:, u % N_PT, :], pT[:, :]).then_inc(copied.sem, 1)

            def ln_stats(sub, b):
                at = b * LN_STEPS[sub] + LN_STEPS[sub] - 3
                if sub > 0:
                    dve.wait_ge(x_done[sub - 1], b + 1)
                if at > 0:
                    dve.wait_ge(ln_step[sub], at)
                for q in range(2):
                    a = dve.bn_stats(stat[:, b, q, :], X[:, 2 * b + q, :])
                a.then_inc(ln_step[sub], 1)
                dve.wait_ge(ln_step[sub], at + 1)
                for q in range(2):
                    a = dve.bn_aggr(mv[:, b, q, :], stat[:, b, q, :])
                a.then_inc(ln_step[sub], 1)
                dve.wait_ge(ln_step[sub], at + 2)
                dve.tensor_scalar(veps[:, b, :], mv[:, b, :, 1], EPS_LN, None, ALU.add).then_inc(ln_step[sub], 1)

            def ln_apply(sub, b):
                dve.wait_ge(ln_rstd[sub], b + 1)
                for q in range(2):
                    a = dve.tensor_scalar(X[:, 2 * b + q, :], X[:, 2 * b + q, :], mv[:, b, q, 0:1], rstd[:, b, q:q + 1],
                                          ALU.subtract, ALU.mult)
                a.then_inc(x_done[sub], 1)

            def add_out(sub, b):
                if sub == 0 and b == 0:
                    dve.wait_ge(ld["a0"], 64)
                    dve.wait_ge(ld["x1"], 48)
                bank, n = full(dve, "out", sub, b)
                xb = X[:, 2 * b:2 * b + 2, :]
                dve.tensor_tensor(xb, bank[:, :].rearrange("p (t d) -> p t d", t=2), xb, ALU.add).then_inc(gread[n], 1)
                result(dve, "out", sub, b)
                if sub == 0:
                    dve.tensor_tensor(xb, xb, bout[:, :].unsqueeze(1).broadcast_to([P, 2, D]), ALU.add).then_inc(ln_step[0], 1)
                ln_stats(sub, b)

            def copy_xT(b, *key):
                bank, n = full(dve, *key)
                dve.tensor_copy(XT[:, :, b * S:(b + 1) * S], bank[:, :].rearrange("p (c s) -> p c s", c=C)).then_inc(gread[n], 1)

            def values(sub, b):
                if b >= 2:
                    dve.wait_ge(pved.sem, pved.done(UNITS_AT[sub] + (b - 1) * UN - 1))
                elif sub == 4:
                    dve.wait_ge(pved.sem, pved.done(B * UN - 1))
                dve.wait_ge(zeroed, 2)
                bank, n = full(dve, "v", sub, b)
                src = bank[:, :].rearrange("p (t s e d) -> p t s e d", t=2, e=2, d=HD)
                for q in range(2):
                    for e in range(2):
                        dst = vn[:, b % 2, q, e::2, e * HD:(e + 1) * HD]
                        if sub == 0:
                            bias = bv[:, :].rearrange("p (s e d) -> p s e d", e=2, d=HD)[:, :, e, :]
                            a = dve.tensor_tensor(dst, src[:, q, :, e, :], bias, ALU.add)
                        else:
                            a = dve.tensor_copy(dst, src[:, q, :, e, :])
                a.then_inc(gread[n], 1)

            def gated_softmax(b, o):
                at = 9 * b
                if o == 19:
                    if b > 0:
                        full(dve, "ctx", b - 1)
                    bank, n = full(dve, "kv", b)
                    dve.tensor_tensor(kv[:, :, :], bank[:, 0:2 * L].rearrange("p (t d) -> p t d", d=L),
                                      bkb[:, :].unsqueeze(1).broadcast_to([P, 2, L]), ALU.add).then_inc(gread[n], 1)
                if o == 21:
                    copy_xT(b, "x1T", b)
                if o == 26:
                    result(dve, "sim", b)
                    if b > 0:
                        dve.wait_ge(x1_step, at)
                    for q in range(2):
                        a = dve.bn_stats(xst[:, q, :], z[:, q, :])
                    a.then_inc(x1_step, 1)
                    dve.wait_ge(x1_step, at + 1)
                    for q in range(2):
                        a = dve.bn_aggr(xmv[:, q, :], xst[:, q, :])
                    a.then_inc(x1_step, 1)
                    dve.wait_ge(x1_step, at + 2)
                    dve.tensor_scalar(xve[:, :], xmv[:, :, 1], EPS_X, None, ALU.add).then_inc(x1_step, 1)
                if o == 27:
                    dve.wait_ge(x1_rstd, b + 1)
                    for q in range(2):
                        a = dve.tensor_scalar(z[:, q, :], z[:, q, :], xmv[:, q, 0:1], xrs[:, q:q + 1],
                                              ALU.subtract, ALU.mult)
                    a.then_inc(x1_step, 1)
                    dve.wait_ge(x1_step, at + 4)
                    dve.tensor_tensor(z[:, :, :], z[:, :, :], gam[:, :].unsqueeze(1).broadcast_to([P, 2, D]),
                                      ALU.mult).then_inc(x1_step, 1)
                    dve.wait_ge(x1_step, at + 5)
                    dve.tensor_tensor(z[:, :, :], z[:, :, :], bet[:, :].unsqueeze(1).broadcast_to([P, 2, D]),
                                      ALU.add).then_inc(x1_step, 1)
                    dve.wait_ge(x1_step, at + 6)
                    dve.reduce_max(xnm[:, :], z[:, :, :], AX.X, negate=True).then_inc(x1_step, 1)
                if o == 29:
                    dve.wait_ge(x1_exp, b + 1)
                    dve.reciprocal(xri[:, :], xsm[:, :]).then_inc(x1_step, 1)
                    dve.wait_ge(x1_step, at + 8)
                    for q in range(2):
                        a = dve.scalar_tensor_tensor(X[:, 2 * b + q, :], z[:, q, :], xri[:, q:q + 1],
                                                     X[:, 2 * b + q, :], ALU.mult, ALU.add)
                    a.then_inc(x1_step, 1)
                    dve.wait_ge(x1_step, at + 9)
                    ln_stats(1, b)
                if o == 30:
                    ln_apply(1, b)

            def feed_forward(b, o):
                at = 11 * b
                if o == 31:
                    dve.wait_ge(x_done[1], b + 1)
                    if b > 0:
                        dve.wait_ge(f_step, at)
                    for q in range(2):
                        a = dve.bn_stats(fst[:, q, :], X[:, 2 * b + q, :])
                    a.then_inc(f_step, 1)
                    dve.wait_ge(f_step, at + 1)
                    for q in range(2):
                        a = dve.bn_aggr(fmv[:, q, :], fst[:, q, :])
                    a.then_inc(f_step, 1)
                    dve.wait_ge(f_step, at + 2)
                    dve.tensor_scalar(fve[:, :], fmv[:, :, 1], EPS_F, None, ALU.add).then_inc(f_step, 1)
                if o == 32:
                    dve.wait_ge(f_rstd, b + 1)
                    for q in range(2):
                        a = dve.tensor_scalar(xn[:, q, :], X[:, 2 * b + q, :], fmv[:, q, 0:1], frs[:, q:q + 1],
                                              ALU.subtract, ALU.mult)
                    a.then_inc(f_step, 1)
                    dve.wait_ge(f_step, at + 4)
                    dve.reduce_max(amax[:, :], xn[:, :, :], AX.X, apply_absolute_value=True).then_inc(f_step, 1)
                    dve.wait_ge(f_step, at + 5)
                    dve.reciprocal(fsc[:, :], amax[:, :]).then_inc(f_step, 1)
                    if b > 0:
                        result(dve, "up", b - 1, 3)
                    dve.tensor_scalar(finv[:, :], amax[:, :], 1.0 / 127.0, None, ALU.mult).then_inc(f_step, 1)
                    dve.wait_ge(f_step, at + 7)
                    dve.tensor_scalar(fsc[:, :], fsc[:, :], 127.0, None, ALU.mult).then_inc(f_step, 1)
                if o == 33:
                    dve.wait_ge(f_step, at + 8)
                    for q in range(2):
                        a = dve.tensor_scalar(xn[:, q, :], xn[:, q, :], fsc[:, q:q + 1], ROUND, ALU.mult, ALU.add)
                    a.then_inc(f_step, 1)
                    dve.wait_ge(f_step, at + 9)
                    dve.tensor_scalar(xn[:, :, :], xn[:, :, :], ROUND, 127.0, ALU.subtract, ALU.min).then_inc(f_step, 1)
                    dve.wait_ge(f_step, at + 10)
                    dve.tensor_scalar(xn[:, :, :], xn[:, :, :], -128.0, None, ALU.max).then_inc(f_step, 1)
                if o == 35:
                    bank, n = full(dve, "qT", b)
                    dve.tensor_copy(qT[:, :, :], bank[:, :].rearrange("p (c s) -> p c s", c=C)).then_inc(gread[n], 1)
                k = f_unit(o, 38)
                if k is not None:
                    v = 4 * b + k
                    result(dve, "gate", b, k)
                    if v >= 2:
                        full(dve, "prT", (v - 2) // 4, (v - 2) % 4)
                    bank, n = full(dve, "up", b, k)
                    dve.scalar_tensor_tensor(pr[:, k % 2, :], bank[:, :], finv[:, k // 2:k // 2 + 1],
                                             sg[:, k % 2, :], ALU.mult, ALU.mult).then_inc(gread[n], 1)
                if o in (44, 48):
                    q = (o - 44) // 4
                    bank, n = full(dve, "down", b, q)
                    dve.tensor_tensor(X[:, 2 * b + q, :], bank[:, 0:D], X[:, 2 * b + q, :], ALU.add).then_inc(gread[n], 1)
                    if q == 1:
                        for w in range(2):
                            result(dve, "down", b, w)
                        ln_stats(2, b)
                if o == 49:
                    ln_apply(2, b)

            def stream(sub):
                for s in range(FIRST_STEP, STEPS_END[sub]):
                    for b, o in tasks(sub, s):
                        if sub == 4 and o == -13:
                            dve.wait_ge(gread[b % 2], gk(3, G - 1, 12 + b) + 1)
                            ln_stats(3, b)
                        if sub == 4 and o == -12:
                            ln_apply(3, b)
                        if o == -10:
                            copy_xT(b, "xT", sub, b)
                        if o == -7:
                            values(sub, b)
                        if o == 18:
                            add_out(sub, b)
                        if o == 19:
                            ln_apply(sub, b)
                        if sub == 0 and stop > 1:
                            gated_softmax(b, o)
                        if sub == 0 and stop > 2:
                            feed_forward(b, o)
                        if o == LAST_AT[sub] + 1 and stop > (3 if sub == 0 else 5):
                            copy_xT(b, "last", sub, b)
                    at = unit(sub, s)
                    if at is not None:
                        max_unit(UNITS_AT[sub], s, narrow_units[at[1]][1])
                    at = unit(sub, s - 1)
                    if at is not None:
                        recip_unit(UNITS_AT[sub], s - 1, narrow_units[at[1]][1])
                    if unit(sub, s - 3) is not None:
                        copy_unit(UNITS_AT[sub], s - 3)

            def wide_attention(g):
                u0 = g * UW + UNITS_AT[3]
                for s in range(UW + 8):
                    if s < UW:
                        max_unit(u0, s, wide_units[s][1])
                    if 0 <= s - 1 < UW:
                        recip_unit(u0, s - 1, wide_units[s - 1][1])
                    if 0 <= s - 3 < UW:
                        copy_unit(u0, s - 3)
                    j, ends = divmod(s - 7, 3)
                    if 0 <= j < B and ends == 2:
                        n = 12 + j
                        k = gk(3, g, n)
                        bank = g_wait(dve, k, n % 2)
                        dve.wait_ge(gread[n % 2], k)
                        dve.tensor_tensor(X[:, 2 * j:2 * j + 2, :], bank[:, :].rearrange("p (t d) -> p t d", t=2),
                                          X[:, 2 * j:2 * j + 2, :], ALU.add).then_inc(gread[n % 2], 1)

            dve.wait_ge(ld["qkv"], 48)
            stream(0)
            if stop > 3:
                with dve.Fori(0, G) as g:
                    u0 = g * UW + UNITS_AT[3]
                    dve.wait_ge(w_bias, g * 2 + (START + 2))
                    dve.wait_ge(score.sem, score.done(u0 - 1))
                    for h in range(QPG):
                        for half in range(2):
                            n = 2 * h + half
                            bank = g_wait(dve, gk(3, g, n), n % 2)
                            dve.scalar_tensor_tensor(
                                qw[:, h, half * 512:(half + 1) * 512].rearrange("p (b s) -> p b s", b=2),
                                bank[:, :].rearrange("p (b s) -> p b s", b=2), DW ** -0.5,
                                peb[:, h, :].unsqueeze(1).broadcast_to([P, 2, S]), ALU.mult, ALU.add).then_inc(gread[n % 2], 1)
                    for half in range(2):
                        n = 8 + half
                        bank = g_wait(dve, gk(3, g, n), n % 2)
                        dve.tensor_tensor(kw[:, half * 512:(half + 1) * 512].rearrange("p (b s) -> p b s", b=2),
                                          bank[:, :].rearrange("p (b s) -> p b s", b=2),
                                          peb[:, QPG, :].unsqueeze(1).broadcast_to([P, 2, S]), ALU.add).then_inc(gread[n % 2], 1)
                    dve.wait_ge(pved.sem, pved.done(u0 - 1))
                    for half in range(2):
                        n = 10 + half
                        bank = g_wait(dve, gk(3, g, n), n % 2)
                        dve.tensor_tensor(vw[:, 4 * half:4 * half + 4, :], bank[:, :].rearrange("p (t d) -> p t d", t=4),
                                          bvw[:, :].unsqueeze(1).broadcast_to([P, 4, DW]), ALU.add).then_inc(gread[n % 2], 1)
                    wide_attention(g)
            if stop == 4:
                for b in range(B):
                    dve.wait_ge(gread[b % 2], gk(3, G - 1, 12 + b) + 1)
                    ln_stats(3, b)
                    ln_apply(3, b)
            if stop > 4:
                stream(4)
            if stop > 5:
                dve.wait_ge(ld["e"], 32)
                for n in (0, 1):
                    g_result(dve, base[5][n], n)
                wide = [P, TILES, E]
                dve.tensor_tensor(sel[:, :, :], sc_[:, :, :], eb[:, :].unsqueeze(1).broadcast_to(wide), ALU.add).then_inc(e_step, 1)
                dve.wait_ge(e_step, 1)
                for q in range(TILES):
                    a = dve.max(top[:, q, :], sel[:, q, :])
                a.then_inc(e_step, 1)
                dve.wait_ge(e_step, 2)
                for q in range(TILES):
                    a = dve.max_index(topi[:, q, :], top[:, q, :], sel[:, q, :])
                a.then_inc(e_step, 1)
                dve.wait_ge(e_step, 3)
                dve.tensor_copy(topf[:, :, :], topi[:, :, :]).then_inc(e_step, 1)
                dve.wait_ge(e_step, 4)
                dve.wait_ge(consts, 4)
                for q in range(TOPK):
                    a = dve.tensor_tensor(eq[:, :, q, :], iota[:, :].unsqueeze(1).broadcast_to(wide),
                                          topf[:, :, q:q + 1].broadcast_to(wide), ALU.is_equal)
                a.then_inc(e_step, 1)
                dve.wait_ge(e_step, 5)
                dve.tensor_reduce(pick[:, :, :], eq[:, :, :, :].rearrange("p t k e -> p t e k"), AX.X, ALU.add).then_inc(e_step, 1)
                dve.wait_ge(e_step, 6)
                dve.tensor_tensor(cws[:, :, :], pick[:, :, :], sc_[:, :, :], ALU.mult).then_inc(e_step, 1)
                dve.wait_ge(e_step, 7)
                dve.tensor_reduce(csum[:, :], cws[:, :, :], AX.X, ALU.add).then_inc(e_step, 1)
                dve.wait_ge(e_step, 8)
                dve.reciprocal(cinv[:, :], csum[:, :]).then_inc(e_step, 1)
                dve.wait_ge(e_step, 9)
                dve.tensor_tensor(cw[:, :, :], cws[:, :, :], cinv[:, :].unsqueeze(2).broadcast_to(wide), ALU.mult).then_inc(e_step, 1)
                dve.wait_ge(e_step, 10)

                def hidden(v, q):
                    dve.wait_ge(e_silu.sem, e_silu.done(v))
                    dve.tensor_tensor(hid[:, q % 4, :], (pT, pG[2])[q % 2][:, :], sg[:, q % 2, :], ALU.mult).then_inc(e_h.sem, 1)

                def combine(i, q):
                    for n in (2 * q, 2 * q + 1):
                        k = gk(5, i, n)
                        bank = g_wait(dve, k, n % 2)
                        dve.wait_ge(gread[n % 2], k)
                        for w in range(2):
                            tile = 4 * (q % 2) + 2 * (n % 2) + w
                            a = dve.scalar_tensor_tensor(X[:, tile, :], bank[:, w * D:(w + 1) * D],
                                                         cwe[:, (q // 2) % 2, tile:tile + 1], X[:, tile, :],
                                                         ALU.mult, ALU.add)
                        a.then_inc(gread[n % 2], 1)

                with dve.Fori(0, E // 2) as i:
                    dve.wait_ge(gread[1], gk(5, i, 1))
                    for s in range(2):
                        a = dve.tensor_copy(cwe[:, s, :], cw[:, :, bass.ds(i * 2 + s, 1)].rearrange("p t o -> p (t o)"))
                    a.then_inc(e_cw, 1)
                    dve.wait_ge(e_cw, i + 1)
                    for q in range(4 + 1):
                        if q < 4:
                            hidden(i * 4 + q, q)
                        if q >= 1:
                            combine(i, q - 1)
                dve.wait_ge(gread[1], gk(5, E // 2, 1))
                dve.memset(cwe[:, 0, :], 1.0).then_inc(e_cw, 1)
                dve.wait_ge(e_cw, E // 2 + 1)
                for q in range(2 + 1):
                    if q < 2:
                        hidden(2 * E + q, q)
                    if q >= 1:
                        combine(E // 2, q - 1)
                for n in (2, 3):
                    g_result(dve, gk(5, E // 2, n), n % 2)
                for b in range(B):
                    ln_stats(5, b)
                for b in range(B):
                    ln_apply(5, b)


def position_table():
    pos = np.arange(S, dtype=np.float32)[:, None]
    i = np.arange(0, DW, 2, dtype=np.float32)
    ang = pos * np.exp(-(np.log(np.float32(10000.0)) * i / np.float32(DW))).astype(np.float32)
    pe = np.zeros((S, DW), np.float32)
    pe[:, 0::2] = np.sin(ang)
    pe[:, 1::2] = np.cos(ang)
    return np.ascontiguousarray(np.stack([pe.T * np.float32(DW ** -0.5), pe.T], axis=1))


def layouts(a):
    wq = a["L1_attn_wq"].reshape(C, P, G, 512).transpose(2, 1, 0, 3).reshape(G, P, 1024)
    wkv = a["L1_attn_wkv"].reshape(C, P, G, 256).transpose(2, 1, 0, 3).reshape(G, P, 512)
    wo = a["L1_attn_wo"].reshape(G, QPG, P, D).transpose(0, 2, 1, 3).reshape(G, P, 1024)
    bkv = a["L1_attn_bkv"].reshape(G, 2, P)
    bq = a["L1_attn_bq"].reshape(G, QPG, P).transpose(0, 2, 1)

    def expert(wg, wu, wd):
        n = wg.shape[0]
        up = [w.reshape(n, I, C, P).transpose(0, 3, 2, 1).reshape(n, P, C * I) for w in (wg, wu)]
        return np.concatenate([*up, wd.transpose(0, 2, 1)], axis=2)

    shared = expert(a["L1_ffn_sw_gate"][None], a["L1_ffn_sw_up"][None], a["L1_ffn_sw_down"][None])
    out = {
        "x": a["x"].reshape(B * S, D),
        "ctxT": a["ctx_512"].reshape(B * S, L).T,
        "wqkvT": a["L0_attn_Wqkv"].T,
        "bqk": a["L0_attn_bqkv"][:2 * D].reshape(4, P).T,
        "bv": a["L0_attn_bqkv"][2 * D:],
        "woutT": a["L0_attn_Wout"].T,
        "bout": a["L0_attn_bout"],
        "wkT": a["L0_xattn_W_k"].T,
        "bk": a["L0_xattn_b_k"],
        "gamma": a["L0_xattn_ln_gamma"],
        "beta": a["L0_xattn_ln_beta"],
        "wgT": a["L0_ffn_W_g"].T,
        "wuT": a["L0_ffn_W_u"].T,
        "wdT": a["L0_ffn_W_d"].T,
        "wwide": np.concatenate([wq, wkv, wo], axis=2),
        "bwide": np.concatenate([bq, bkv[:, 0, :, None], np.zeros((G, P, 3), np.float32)], axis=2),
        "bvwide": bkv[:, 1, :],
        "pe": position_table(),
        "xqT": a["L1_xattn_Wq"].T,
        "xkvT": a["L1_xattn_Wkv_expand"].T,
        "xoT": a["L1_xattn_Wout"].T,
        "gateT": a["L1_ffn_gate_w"].T,
        "ebias": a["L1_ffn_expert_bias"],
        "wexp": np.concatenate([expert(a["L1_ffn_w_gate"], a["L1_ffn_w_up"], a["L1_ffn_w_down"]), shared]),
    }
    return {k: np.ascontiguousarray(v) for k, v in out.items()}


def kernel(**inputs):
    from concourse import bacc
    from concourse.bass_utils import run_bass_kernel_spmd as run

    arrays = layouts({k: np.asarray(v) for k, v in inputs.items()})
    nc = bacc.Bacc("TRN2", target_bir_lowering=False, num_devices=1)
    t = {k: nc.dram_tensor(f"in_{k}", v.shape, mybir.dt.from_np(v.dtype), kind="ExternalInput").ap()
         for k, v in arrays.items()}
    t["out"] = nc.dram_tensor("out", (B * S, D), F32, kind="ExternalOutput").ap()
    build(nc, t)
    res = run(nc, [{f"in_{k}": v for k, v in arrays.items()}], core_ids=[0])
    return res.results[0]["out"].reshape(B, S, D)
```

```python
from contextlib import ExitStack

import numpy as np
import concourse.bass as bass
from concourse import mybir

F32 = mybir.dt.float32
F32R = mybir.dt.float32r
BF16 = mybir.dt.bfloat16
U32 = mybir.dt.uint32
ACT = mybir.ActivationFunctionType
ALU = mybir.AluOpType
AX = mybir.AxisListType

P = 128
B, S, D = 4, 256, 256
TILES = B * S // P
C = D // P
NH, HD = 16, 16
G, QPG, DW = 4, 4, 128
L = 64
FF = 1024
E, I, TOPK = 16, 128, 4
EPS_LN, EPS_X, EPS_F = 1e-5, 1e-6, 1e-8
NEG = -1e30
ROUND = 1.5 * 2.0 ** 23
AHEAD = 4
START = 1

UN = 12
UW = 12
N_P, N_PT = 4, 3


class Steps:

    def __init__(self, sem):
        self.sem = sem

    def done(self, u):
        return u + (1 + AHEAD)

    def free(self, u, ring):
        return u + (1 + AHEAD - ring)


class BankUses:

    def __init__(self):
        self.count = [START, START, START]
        self.turn = 0
        self.of = {}

    def take(self, key):
        n = self.turn
        self.of[key] = (n, self.count[n])
        self.count[n] += 1
        self.turn = (n + 1) % 3
        return self.of[key]


def build(nc, t, stop=6):
    ctx = ExitStack()
    with ctx:
        def sb(name, shape, dt=F32):
            return ctx.enter_context(nc.sbuf_tensor(name, shape, dt))

        def sem(name):
            return ctx.enter_context(nc.semaphore(name))

        X = sb("X", [P, TILES, D])
        XT = sb("XT", [P, C, B * S])
        ident = sb("ident", [P, P])
        identb = sb("identb", [P, P], BF16)
        tri = sb("tri", [P, 4, P], BF16)
        stat = sb("stat", [P, B, 2, 6])
        mv = sb("mv", [P, B, 2, 2])
        veps = sb("veps", [P, B, 2])
        rstd = sb("rstd", [P, B, 2])
        mhalf = sb("mhalf", [P, 8])
        wqkv = sb("wqkv", [P, C, 3 * D])
        wout = sb("wout", [P, C, D])
        bqk = sb("bqk", [P, 4])
        bqs = sb("bqs", [P, 2])
        bv = sb("bv", [P, D])
        bout = sb("bout", [P, D])
        qf = sb("qf", [P, C, S])
        kf = sb("kf", [P, C, S])
        qr = sb("qr", [P, 2, 2, C, S], F32R)
        kr = sb("kr", [P, 2, C, S], F32R)
        kbd = sb("kbd", [P, 2, C, 8, S], F32R)
        vn = sb("vn", [P, 2, 2, NH, 32])
        an = sb("an", [P, 2, C, S])
        prob = sb("prob", [P, N_P, 512])
        probT = sb("probT", [P, N_PT, 512])
        nmax = sb("nmax", [P, N_P, 4])
        rsum = sb("rsum", [P, N_P, 4])
        rinv = sb("rinv", [P, N_P, 4])
        cx = sb("cx", [L, B * S])
        wk = sb("wk", [L, L])
        bk = sb("bk", [L, 1])
        bkb = sb("bkb", [P, L])
        gam = sb("gam", [P, D])
        bet = sb("bet", [P, D])
        kvT = sb("kvT", [L, S])
        kv = sb("kv", [P, 2, L])
        oT = sb("oT", [L, S])
        z = sb("z", [P, 2, D])
        xst = sb("xst", [P, 2, 6])
        xmv = sb("xmv", [P, 2, 2])
        xve = sb("xve", [P, 2])
        xrs = sb("xrs", [P, 2])
        xnm = sb("xnm", [P, 2])
        xsm = sb("xsm", [P, 2])
        xri = sb("xri", [P, 2])
        sgu = sb("sgu", [P, 2, C, FF], BF16)
        wd = sb("wd", [P, FF // P, D], F32R)
        qT = sb("qT", [P, C, S], BF16)
        xn = sb("xn", [P, 2, D])
        fst = sb("fst", [P, 2, 6])
        fmv = sb("fmv", [P, 2, 2])
        fve = sb("fve", [P, 2])
        frs = sb("frs", [P, 2])
        amax = sb("amax", [P, 2])
        fsc = sb("fsc", [P, 2])
        finv = sb("finv", [P, 2])
        sg = sb("sg", [P, 2, 512])
        pr = sb("pr", [P, 2, 512])
        prT = sb("prT", [P, 2, 2, 512], F32R)
        bw = sb("bw", [P, 8])
        bws = sb("bws", [P, 8])
        bvw = sb("bvw", [P, P])
        xq = sb("xq", [P, C, D])
        xkv = sb("xkv", [L, 2 * D])
        xo = sb("xo", [P, C, D])
        gw = sb("gw", [P, C, E])
        eb = sb("eb", [P, E])
        we = wqkv[:, :, :]
        top = sb("top", [P, TILES, 8])
        topi = sb("topi", [P, TILES, 8], U32)
        topf = sb("topf", [P, TILES, 8])
        iota = sb("iota", [P, E])
        csum = sb("csum", [P, TILES])
        cinv = sb("cinv", [P, TILES])
        cw = sb("cw", [P, TILES, E + 1])
        cwe = sb("cwe", [P, 2, TILES])
        with ExitStack() as early:
            def sb_early(name, shape, dt=F32):
                return early.enter_context(nc.sbuf_tensor(name, shape, dt))

            ww = sb_early("ww", [P, 2560])
            pes = sb_early("pes", [P, 2, S])
            peb = sb_early("peb", [P, 5, S])
            qw = sb_early("qw", [P, QPG, B * S])
            kw = sb_early("kw", [P, B * S])
            vw = sb_early("vw", [P, TILES, DW])
            aw = sb_early("aw", [P, 2, QPG, S], F32R)
        XTr = sb("XTr", [P, 2, C, B * S], F32R)
        hid = sb("hid", [P, 4, 2, 512], F32R)
        wr = sb("wr", [P, 2, 2, 3 * D], F32R)
        sc_ = sb("sc_", [P, TILES, E])
        sel = sb("sel", [P, TILES, E])
        eq = sb("eq", [P, TILES, TOPK, E])
        pick = sb("pick", [P, TILES, E])
        cws = sb("cws", [P, TILES, E])
        kbd_flat = kbd[:, :, :, :, :].rearrange("p a c g s -> p (a c g s)")
        wo_parts_ = kbd_flat[:, 0:2 * QPG * D].rearrange("p (a n) -> p a n", a=2)
        aw_low = kbd_flat[:, 2 * QPG * D:4 * QPG * D].rearrange("p (b h s) -> p b h s", b=2, h=QPG)
        xt_wide = kbd_flat[:, 4 * QPG * D:].rearrange("p (a c n) -> p a c n", a=2, c=C)
        wq_parts = qr[:, :, :, :, :].rearrange("p b a c s -> p (b a c s)").rearrange("p (a c n) -> p a c n", a=2, c=C)
        wk_parts = kr[:, :, :, 0:P]
        wd_raw = (kw[:, :].rearrange("p (w d) -> p w d", d=D), vw[:, :, :].rearrange("p t (h d) -> p (t h d)", h=1)
                  .rearrange("p (w d) -> p w d", d=D))
        raw = qw[:, :, :].rearrange("p (u c) n -> p u c n", u=2)

        def bank(name):
            return ctx.enter_context(nc.psum_tensor(name, [P, 512], F32))

        pS = [bank("pS0"), bank("pS1")]
        pT = bank("pT")
        pO = [bank("pO0"), bank("pO1")]
        pG = [bank("pG0"), bank("pG1"), bank("pG2")]

        ld = {k: sem("loaded_" + k) for k in ("x0", "x", "k", "q", "v", "bqk", "bv", "a0", "x1", "ctx", "f", "w", "x2", "e",
                                              "wqk", "wv", "wo", "exp0", "exp1")}
        consts = sem("consts")
        kbd_zeroed = sem("keys_zeroed")
        vn_zeroed = sem("values_zeroed")
        gfull = [sem(f"general{n}_full") for n in range(3)]
        gread = [sem(f"general{n}_read") for n in range(3)]
        qk_low = sem("qk_low")
        k_spread = [sem(f"keys{hg}_spread") for hg in range(4)]
        passed = {e: sem("passed_" + e) for e in ("dve", "pe", "pool", "sp")}
        score = Steps(sem("score_done"))
        maxed = Steps(sem("max_done"))
        exped = Steps(sem("exp_done"))
        recip = Steps(sem("recip_done"))
        normed = Steps(sem("norm_done"))
        transp = Steps(sem("transpose_done"))
        copied = Steps(sem("probT_done"))
        pved = Steps(sem("pv_done"))
        oread = Steps(sem("out_read"))
        bias_q = sem("bias_q")
        ln_step = [sem(f"ln{q}_step") for q in range(6)]
        ln_rstd = [sem(f"ln{q}_rstd") for q in range(6)]
        x_done = [sem(f"x{q}_done") for q in range(6)]
        x1_step = sem("x1_step")
        x1_rstd = sem("x1_rstd")
        x1_exp = sem("x1_exp")
        signs = sem("signs")
        f_hi = sem("f_product_high")
        f_step = sem("f_step")
        f_rstd = sem("f_rstd")
        w_bias = sem("w_bias")
        w_used = sem("group_projected")
        xt_hi = {sub: sem(f"xt{sub}_high") for sub in (0, 4)}
        xt_lo = {sub: sem(f"xt{sub}_low") for sub in (0, 4)}
        w_hi = sem("wq_wk_high")
        w_lo = sem("wq_wk_low")
        wo_hi = sem("wo_high")
        wo_lo = sem("wo_low")
        aw_hi = Steps(sem("wide_out_high"))
        low_zeroed = sem("keys_low_zeroed")
        e_step = sem("e_step")
        e_gu = Steps(sem("e_gate_up"))
        e_silu = Steps(sem("e_silu"))
        e_h = Steps(sem("e_hidden"))
        e_hi = Steps(sem("e_hidden_high"))
        e_lo = Steps(sem("e_hidden_low"))
        e_cw = sem("e_cw")
        gu_parts = sem("gate_up_parts")
        down_parts = sem("down_parts")
        stored = sem("stored")

        uses = BankUses()
        LOOP_USES = {3: (0, 16, G - 2), 5: (2, 4, E + 1)}
        base = {}

        def loop_uses(sub):
            first, per, count = LOOP_USES[sub]
            base[sub] = list(uses.count)
            for n in range(2):
                uses.count[n] += (first + per * count) // 2

        def gk(sub, i, n):
            first, per, _ = LOOP_USES[sub]
            before = per // 2 if sub == 3 else 0
            return i * (per // 2) + (base[sub][n % 2] + (first + n) // 2 - before)

        def down_k(v, n=1):
            return v + (base[5][n] + 1)

        def g_take(pe, k, n):
            pe.wait_ge(gread[n], k)
            return pG[n]

        def g_wait(eng, k, n):
            eng.wait_ge(gfull[n], k + 1)
            return pG[n]

        def g_result(eng, k, n):
            eng.wait_ge(gread[n], k + 1)

        def full(eng, *key):
            n, k = uses.of[key]
            return g_wait(eng, k, n), n

        def result(eng, *key):
            n, k = uses.of[key]
            g_result(eng, k, n)

        KINDS = (("first", 0), ("second", 0), ("second", 2))
        narrow_units = [(4 * hg + o, kind) for hg in range(4) for kind, o in KINDS]
        wide_units = [(o, kind) for b in range(B) for kind, o in KINDS]
        UNITS_AT = {0: 0, 3: B * UN, 4: B * UN + G * UW}
        OUTS_AT = {0: 0, 3: B * 2, 4: B * 2 + G * 8}

        def by_head(ap, kind):
            return ap.rearrange("p (h k) -> p h k", h=4 if kind == "first" else 2)

        FIRST_STEP = -13
        WIDE_AT = 67
        WIDE_FROM = 83
        WIDE_READY = 89
        STEPS_END = {0: WIDE_FROM + 34 if stop > 3 else WIDE_READY, 4: (B - 1) * UN + 23}
        FRONT_STEPS = 24
        LAST_AT = {0: 50, 4: 20}
        BATCHES_AT = {0: 0, 4: B}

        def tasks(sub, s):
            return [(b, s - UN * b) for b in range(B)]

        def unit(sub, s):
            if 0 <= s < B * UN:
                return s // UN, s % UN, UNITS_AT[sub] + s
            return None

        def f_unit(o, at):
            return (o - at) // 2 if 0 <= o - at < 8 and (o - at) % 2 == 0 else None

        PASSES = [(0, 0), (1, 0), (0, 1)]
        W_PIECES = ([(ww[:, c * 512 + m * 256:c * 512 + m * 256 + 256], wq_parts[:, :, c, m * 256:m * 256 + 256])
                     for c in range(C) for m in range(2)]
                    + [(ww[:, 1024:1536].rearrange("p (c n) -> p c n", c=C)[:, :, 0:P], wk_parts)])
        WO_PIECES = [(ww[:, 1536 + D * h:1536 + D * (h + 1)], wo_parts_[:, :, D * h:D * (h + 1)]) for h in range(QPG)]

        SECOND_AT = {"first": WIDE_READY - WIDE_FROM, "middle": 0, "last": 0}
        DELAY = {"first": SECOND_AT["first"] - 1, "middle": 0, "last": 0}
        WIDE_STEPS = {phase: UW + 9 + delay for phase, delay in DELAY.items()}

        def wide_unit(phase, k):
            if 0 <= k < UW // 2:
                return k
            k -= DELAY[phase]
            return k if UW // 2 <= k < UW else None

        def wide_projection(phase, k):
            k -= SECOND_AT[phase]
            own = [m for m in range(QPG + 2) if k == max(m - 1, 0)]
            return [("second", m) for m in own] + [("first", m) for m in range(QPG + 2) if k == 11 + m and phase != "last"]

        def wide_out(phase, k):
            for b in range(B):
                if k == 3 * b + 9 + (DELAY[phase] if b >= 2 else 0):
                    return b
            return None

        WIDE_N = {}
        for k in range(WIDE_STEPS["middle"]):
            if wide_out("middle", k) is not None:
                WIDE_N["out", wide_out("middle", k)] = len(WIDE_N)
            for use in wide_projection("middle", k):
                WIDE_N[use] = len(WIDE_N)

        def wide_use(phase, g, what, m):
            if phase != "middle":
                return uses.of["wide", phase, what, m]
            n = WIDE_N[what, m]
            return n % 2, gk(3, g, n)

        def wide_full(eng, phase, g, what, m):
            n, k = wide_use(phase, g, what, m)
            return g_wait(eng, k, n), n

        def wide_read(eng, phase, g, what, m):
            n, k = wide_use(phase, g, what, m)
            g_result(eng, k, n)

        def after_last_group(eng, sems, phase, g, what, m):
            if phase != "first":
                n = WIDE_N[what, m]
                eng.wait_ge(sems[n % 2], gk(3, g, n) - 7)

        LN_STEPS = [4, 3, 3, 3, 3, 3]

        block = ctx.enter_context(nc.Block())

        @block.tensor
        def _(pe):
            for st in (score, transp, pved, e_gu):
                pe.sem_inc(st.sem, AHEAD)
            for st in gfull:
                pe.sem_inc(st, START)

            def take(*key):
                n, k = uses.take(key)
                return g_take(pe, k, n), n

            def score_unit(sub, u0, u, b, h0, kind):
                pe.wait_ge(exped.sem, exped.free(u0 + u, 2))
                bank = pS[u % 2]
                v = by_head(bank[:, :], kind)
                if kind == "first":
                    pe.matmul(v, identb[:, :], tri[:, :, :], start=True, stop=False, skip_group_check=True)
                    q0, nk, nh = 0, P, 4
                else:
                    pe.matmul(v[:, :, P:S], identb[:, :], tri[:, 0:2, :], start=True, stop=False, skip_group_check=True)
                    q0, nk, nh = P, S, 2
                if sub == 3:
                    for h in range(nh):
                        a = pe.matmul(v[:, h, :], qw[:, h0 + h, b * S + q0:b * S + q0 + P], kw[:, b * S:b * S + nk],
                                      start=False, stop=True, skip_group_check=True)
                else:
                    tl, g = h0 // 8, h0 % 8
                    for pq, pk in PASSES:
                        a = pe.matmul(v, qr[:, b % 2, pq, tl, q0:q0 + P], kbd[:, pk, tl, g:g + nh, 0:nk],
                                      start=False, stop=(pq, pk) == PASSES[-1], skip_group_check=True)
                a.then_inc(score.sem, 1)

            def transpose_unit(u0, u):
                pe.wait_ge(normed.sem, normed.done(u0 + u))
                pe.wait_ge(copied.sem, copied.free(u0 + u, 1))
                for q in range(4):
                    a = pe.transpose(pT[:, q * P:(q + 1) * P], prob[:, u % N_P, q * P:(q + 1) * P], ident[:, :])
                a.then_inc(transp.sem, 1)

            def value_unit(sub, u0, o, o0, u, first, b, h0, kind):
                if first:
                    pe.wait_ge(oread.sem, oread.free(o0 + o, 2))
                pe.wait_ge(copied.sem, copied.done(u0 + u))
                bank = pO[o % 2]
                for q in range(4):
                    h, kt = (h0 + q, 0) if kind == "first" else (h0 + q // 2, q % 2)
                    src = probT[:, u % N_PT, q * P:(q + 1) * P]
                    if sub == 3:
                        a = pe.matmul(bank[:, h * P:(h + 1) * P], vw[:, 2 * b + kt, :], src, start=kt == 0,
                                      stop=kind == "first" or kt == 1, skip_group_check=True)
                    else:
                        r, q0 = (h % 8) // 2, 0 if kind == "first" else P
                        a = pe.matmul(bank[32 * r:32 * r + 32, q0:q0 + P], vn[:, b % 2, kt, h, :], src,
                                      start=kind == "first" and h % 2 == 0,
                                      stop=h % 2 == 1 and (kind == "first" or kt == 1), skip_group_check=True)
                a.then_inc(pved.sem, 1)

            def transpose_batch(src, *key):
                bank, n = take(*key)
                for c in range(C):
                    for q in range(2):
                        a = pe.transpose(bank[:, c * S + q * P:c * S + (q + 1) * P], src[:, q, c * P:(c + 1) * P], ident[:, :])
                a.then_inc(gfull[n], 1)

            def project(sub, b, what):
                if what == "k":
                    result(pe, "xT", sub, b)
                if sub == 4 and b == 0:
                    pe.wait_ge(ld["x2"], 48)
                if sub == 0 and b == 0:
                    pe.wait_ge(ld[what], 16)
                bank, n = take(what, sub, b)
                for m in range(2):
                    if sub == 4 and what == "k":
                        a = pe.matmul(bank[:, m * S:(m + 1) * S], xkv[:, m * P:(m + 1) * P], cx[:, b * S:(b + 1) * S],
                                      start=True, stop=True)
                        continue
                    w, w0 = (wqkv, (m if what == "q" else 2 + m) * P) if sub == 0 else (xq, m * P)
                    for c in range(C):
                        a = pe.matmul(bank[:, m * S:(m + 1) * S], w[:, c, w0:w0 + P], XT[:, c, b * S:(b + 1) * S],
                                      start=c == 0, stop=c == 1)
                a.then_inc(gfull[n], 1)

            def project_values(sub, b):
                if sub == 0 and b == 0:
                    pe.wait_ge(ld["v"], 16)
                bank, n = take("v", sub, b)
                for q in range(2):
                    tok = b * S + q * P
                    if sub == 4:
                        a = pe.matmul(bank[:, q * D:(q + 1) * D], cx[:, tok:tok + P], xkv[:, D:2 * D], start=True, stop=True)
                    else:
                        for c in range(C):
                            a = pe.matmul(bank[:, q * D:(q + 1) * D], XT[:, c, tok:tok + P], wqkv[:, c, 2 * D:3 * D],
                                          start=c == 0, stop=c == 1)
                a.then_inc(gfull[n], 1)

            def out_projection(sub, b, wo):
                if sub == 0 and b == 0:
                    pe.wait_ge(ld["a0"], 64)
                pe.wait_ge(oread.sem, oread.done(OUTS_AT[sub] + 2 * b + 1))
                bank, n = take("out", sub, b)
                for q in range(2):
                    for c in range(C):
                        a = pe.matmul(bank[:, q * D:(q + 1) * D], an[:, b % 2, c, q * P:(q + 1) * P], wo[:, c, :],
                                      start=c == 0, stop=c == 1)
                a.then_inc(gfull[n], 1)

            def gated_softmax(b, o):
                bs = slice(b * S, (b + 1) * S)
                if o == 18:
                    if b == 0:
                        pe.wait_ge(ld["ctx"], 16)
                    bank, n = take("kvT", b)
                    pe.matmul(bank[0:L, 0:S], wk[:, :], cx[:, bs], start=True, stop=True).then_inc(gfull[n], 1)
                    bank, n = take("kv", b)
                    for q in range(2):
                        a = pe.matmul(bank[:, q * L:(q + 1) * L], cx[:, b * S + q * P:b * S + (q + 1) * P], wk[:, :],
                                      start=True, stop=True)
                    a.then_inc(gfull[n], 1)
                if o == 20:
                    pe.wait_ge(x_done[0], b + 1)
                    transpose_batch(X[:, 2 * b:2 * b + 2, :], "x1T", b)
                if o == 22:
                    result(pe, "x1T", b)
                    result(pe, "kv", b)
                    bank, n = take("ctx", b)
                    for c in range(C):
                        a = pe.matmul(bank[0:L, 0:S], kv[:, c, :], XT[:, c, bs], start=c == 0, stop=c == 1)
                    a.then_inc(gfull[n], 1)
                if o == 24:
                    result(pe, "ctx", b)
                    result(pe, "kvT", b)
                    bank, n = take("sim", b)
                    for q in range(2):
                        a = pe.matmul(bank[:, q * D:(q + 1) * D], oT[:, q * P:(q + 1) * P], kvT[:, :], start=True, stop=True)
                    a.then_inc(gfull[n], 1)

            def feed_forward(b, o):
                if o == 34:
                    pe.wait_ge(f_step, 11 * b + 11)
                    transpose_batch(xn, "qT", b)
                for at, which in ((36, "gate"), (37, "up")):
                    k = f_unit(o, at)
                    if k is not None:
                        if k == 0:
                            result(pe, "qT", b)
                        if b == 0 and k == 0:
                            pe.wait_ge(signs, 4)
                        bank, n = take(which, b, k)
                        for c in range(C):
                            a = pe.matmul(bank[:, :], qT[:, c, (k // 2) * P:(k // 2 + 1) * P],
                                          sgu[:, 0 if which == "gate" else 1, c, (k % 2) * 512:(k % 2 + 1) * 512],
                                          start=c == 0, stop=c == 1)
                        a.then_inc(gfull[n], 1)
                k = f_unit(o, 39)
                if k is not None:
                    result(pe, "up", b, k)
                    bank, n = take("prT", b, k)
                    for w in range(4):
                        a = pe.transpose(bank[:, w * P:(w + 1) * P], pr[:, k % 2, w * P:(w + 1) * P], ident[:, :])
                    a.then_inc(gfull[n], 1)
                if o in (43, 47):
                    q = (o - 43) // 4
                    pe.wait_ge(signs, 6)
                    for k in (2 * q, 2 * q + 1):
                        result(pe, "prT", b, k)
                    bank, n = take("down", b, q)
                    for w in range(8):
                        for part in range(2):
                            a = pe.matmul(bank[:, 0:D], prT[:, w // 4, part, (w % 4) * P:(w % 4 + 1) * P], wd[:, w, :],
                                          start=w + part == 0, stop=w == 7 and part == 1)
                    a.then_inc(gfull[n], 1)

            def gate_up(v, q):
                s, half = (q // 2) % 2, q % 2
                pe.wait_ge(e_silu.sem, e_silu.free(v, 2))
                pe.wait_ge(e_h.sem, e_h.free(v, 2))
                for u, bank in ((0, pS[half]), (1, (pT, pG[2])[half])):
                    for m, (pw, px) in enumerate(PASSES * C):
                        c = m // 3
                        o = u * D + c * P
                        a = pe.matmul(bank[:, :], wr[:, s, pw, o:o + P], XTr[:, px, c, half * 512:(half + 1) * 512],
                                      start=m == 0, stop=m == 3 * C - 1)
                a.then_inc(e_gu.sem, 1)

            def background(sub, s):
                for b, o in tasks(sub, s):
                    if o == -11:
                        if sub == 0:
                            pe.wait_ge(ld["x" if b else "x0"], 16)
                        else:
                            pe.wait_ge(x_done[3], b + 1)
                        transpose_batch(X[:, 2 * b:2 * b + 2, :], "xT", sub, b)
                    if o == -10:
                        project(sub, b, "k")
                    if o == -9:
                        project(sub, b, "q")
                    if o == -8:
                        project_values(sub, b)
                    if o == 17:
                        out_projection(sub, b, wout if sub == 0 else xo)
                    if sub == 0 and stop > 1:
                        gated_softmax(b, o)
                    if sub == 0 and stop > 2:
                        feed_forward(b, o)
                    if o == LAST_AT[sub] and stop > (3 if sub == 0 else 5):
                        pe.wait_ge(x_done[2 if sub == 0 else 4], b + 1)
                        transpose_batch(X[:, 2 * b:2 * b + 2, :], "last", sub, b)
                if sub == 4 and stop > 5 and s == 54:
                    pe.wait_ge(xt_lo[4], 2)
                    pe.wait_ge(gu_parts, 2)
                    gate_up(0, 0)
                if sub == 0 and stop > 3 and WIDE_AT <= s < WIDE_AT + QPG + 2:
                    n = s - WIDE_AT
                    if n == 0:
                        for b in range(2):
                            result(pe, "last", 0, b)
                        pe.wait_ge(xt_lo[0], 2)
                        pe.wait_ge(w_lo, 5)
                        pe.wait_ge(ld["wv"], 48)
                    bank, g = take("wide", n)
                    project_wide(bank, 0, n).then_inc(gfull[g], 1)

            def stream(sub, start):
                for s in range(start, STEPS_END[sub]):
                    at = unit(sub, s)
                    if at is not None:
                        b, k, _ = at
                        if k == 0:
                            pe.wait_ge(qk_low, 2 * (BATCHES_AT[sub] + b) + 2)
                            result(pe, "v", sub, b)
                        if k % 3 == 0:
                            pe.wait_ge(k_spread[k // 3], 4 * 16 * (BATCHES_AT[sub] + b + 1))
                        if sub == 0 and s == 0:
                            pe.wait_ge(consts, 7)
                        score_unit(sub, UNITS_AT[sub], s, b, *narrow_units[k])
                    if unit(sub, s - 3) is not None:
                        transpose_unit(UNITS_AT[sub], s - 3)
                    at = unit(sub, s - 4)
                    if at is not None:
                        b, k, _ = at
                        value_unit(sub, UNITS_AT[sub], 2 * b + k // 6, OUTS_AT[sub], s - 4, k % 6 == 0, b, *narrow_units[k])
                    if sub == 0 and stop > 3 and s >= WIDE_FROM:
                        wide_step("first", 0, s - WIDE_FROM)
                    background(sub, s)

            def wide_step(phase, g, k):
                u0, o0 = g * UW + UNITS_AT[3], g * 8 + OUTS_AT[3]
                if k == 0:
                    for m in range(QPG + 2):
                        if phase == "first":
                            result(pe, "wide", m)
                        elif m >= QPG:
                            after_last_group(pe, gread, phase, g, "first", m)
                u = wide_unit(phase, k)
                if u is not None:
                    if u == UW // 2:
                        for m in (QPG - 1, QPG):
                            wide_read(pe, phase, g, "second", m)
                    score_unit(3, u0, u, u // 3, *wide_units[u])
                u = wide_unit(phase, k - 3)
                if u is not None:
                    transpose_unit(u0, u)
                u = wide_unit(phase, k - 4)
                if u is not None:
                    if u == UW // 2:
                        wide_read(pe, phase, g, "second", QPG + 1)
                    value_unit(3, u0, 2 * (u // 3) + (u % 3 > 0), o0, u, u % 3 < 2, u // 3, *wide_units[u])

                def take_wide(what, m):
                    if phase != "middle":
                        return take("wide", phase, what, m)
                    n, count = wide_use(phase, g, what, m)
                    return g_take(pe, count, n), n

                b = wide_out(phase, k)
                if b is not None:
                    pe.wait_ge(oread.sem, oread.done(o0 + (2 * b + 1)))
                    pe.wait_ge(wo_lo, g * 4 + 4)
                    bank, n = take_wide("out", b)
                    for q in range(2):
                        for m, (pa, pw) in enumerate(PASSES * QPG):
                            c = m // 3
                            x = (aw_low if pa else aw)[:, b % 2, c, q * P:(q + 1) * P]
                            a = pe.matmul(bank[:, q * D:(q + 1) * D], x, wo_parts_[:, pw, c * D:(c + 1) * D],
                                          start=m == 0, stop=m == 3 * QPG - 1)
                    a.then_inc(gfull[n], 1)
                for what, m in wide_projection(phase, k):
                    if (what, m) == ("second", 0) and phase == "first":
                        for b in range(B):
                            result(pe, "last", 0, b)
                        pe.wait_ge(xt_lo[0], B)
                    if (what, m) == ("first", 0):
                        pe.wait_ge(w_lo, g * 5 + 10)
                    if m == QPG + 1:
                        pe.wait_ge(ld["wv"], g * 48 + (48 if what == "second" else 96))
                    bank, n = take_wide(what, m)
                    project_wide(bank, 1 if what == "second" else 0, m).then_inc(gfull[n], 1)

            def project_wide(bank, half, n):
                if n <= QPG:
                    for m, (pw, px) in enumerate(PASSES * C):
                        c = m // 3
                        w = wq_parts[:, pw, c, n * P:(n + 1) * P] if n < QPG else wk_parts[:, pw, c, :]
                        a = pe.matmul(bank[:, :], w, xt_wide[:, px, c, half * 512:(half + 1) * 512],
                                      start=m == 0, stop=m == 3 * C - 1)
                else:
                    for q in range(4):
                        tok = (4 * half + q) * P
                        for c in range(C):
                            a = pe.matmul(bank[:, q * P:(q + 1) * P], XT[:, c, tok:tok + P],
                                          ww[:, 1024 + c * 256 + P:1024 + (c + 1) * 256], start=c == 0, stop=c == 1)
                return a

            pe.wait_ge(consts, 2)
            stream(0, FIRST_STEP)
            if stop > 3:
                loop_uses(3)
                for m in (QPG, QPG + 1):
                    wide_read(pe, "first", 0, "first", m)
                with pe.Fori(1, G - 1) as g:
                    for k in range(WIDE_STEPS["middle"]):
                        wide_step("middle", g, k)
                for k in range(WIDE_STEPS["last"]):
                    wide_step("last", G - 1, k)
                    if k >= FRONT_STEPS + FIRST_STEP and stop > 4:
                        background(4, k - FRONT_STEPS)
            if stop > 4:
                stream(4, WIDE_STEPS["last"] - FRONT_STEPS)
            if stop > 5:
                pe.wait_ge(ld["e"], 32)
                loop_uses(5)
                for b in range(B):
                    result(pe, "last", 4, b)
                for n in (0, 1):
                    bank = g_take(pe, base[5][n], n)
                    for q in range(4):
                        for c in range(C):
                            tile = 4 * n + q
                            a = pe.matmul(bank[:, q * E:(q + 1) * E], XT[:, c, tile * P:(tile + 1) * P], gw[:, c, :],
                                          start=c == 0, stop=c == 1)
                    a.then_inc(gfull[n % 2], 1)

                def down(v, q):
                    pe.wait_ge(e_lo.sem, e_lo.done(v))
                    for n in range(2):
                        bank = g_take(pe, down_k(v, n), n)
                        for w in range(2):
                            o = (2 * n + w) * P
                            for m, (ph, pw) in enumerate(PASSES):
                                a = pe.matmul(bank[:, w * D:(w + 1) * D], hid[:, q % 4, ph, o:o + P],
                                              wr[:, (q // 2) % 2, pw, 2 * D:3 * D], start=m == 0, stop=m == 2)
                        a.then_inc(gfull[n], 1)

                pe.wait_ge(xt_lo[4], B)
                gate_up(1, 1)
                with pe.Fori(0, E // 2) as i:
                    for q in range(4):
                        if q % 2 == 0:
                            pe.wait_ge(gu_parts, i * 4 + (q + 4))
                        gate_up(i * 4 + (q + 2), q + 2)
                        if q % 2 == 0:
                            pe.wait_ge(down_parts, i * 4 + (q + 2))
                        down(i * 4 + q, q)
                pe.wait_ge(down_parts, 2 * E + 2)
                for q in range(2):
                    down(2 * E + q, q)

        @block.sync
        def _(sp):
            def load(dst, src, key):
                sp.dma_start(dst, src).then_inc(ld[key], 16)

            def spread_keys(sub, b):
                n = BATCHES_AT[sub] + b
                sp.wait_ge(qk_low, 2 * n + 1)
                for hg in range(4):
                    if b == 0 and hg % 2 == 0:
                        sp.wait_ge(kbd_zeroed, BATCHES_AT[sub] // 2 + 1 + hg // 2)
                        if sub == 4:
                            sp.wait_ge(low_zeroed, 1)
                    if n > 0:
                        sp.wait_ge(score.sem, score.done(UNITS_AT[sub] + (b - 1) * UN + 3 * hg + 2 if b > 0
                                                         else (B - 1) * UN + 3 * hg + 2))
                    for g in range(4 * (hg % 2), 4 * (hg % 2) + 4):
                        sp.dma_start(kbd[16 * g:16 * g + 16, :, hg // 2, g, :].bitcast(F32),
                                     kr[16 * g:16 * g + 16, :, hg // 2, :].bitcast(F32)).then_inc(k_spread[hg], 16)

            def load_group_qk(g):
                load(ww[:, 0:1024], t["wwide"][g, :, 0:1024].rearrange("o p n -> p (o n)"), "wqk")
                load(ww[:, 1024:1536].rearrange("p (c n) -> p c n", c=C)[:, :, 0:P],
                     t["wwide"][g, :, 1024:1536].rearrange("o p (c n) -> p (o c) n", c=C)[:, :, 0:P], "wqk")

            def load_group_v(g):
                load(ww[:, 1024:1536].rearrange("p (c n) -> p c n", c=C)[:, :, P:2 * P],
                     t["wwide"][g, :, 1024:1536].rearrange("o p (c n) -> p (o c) n", c=C)[:, :, P:2 * P], "wv")
                load(bw[:, :], t["bwide"][g, :, :].rearrange("o p n -> p (o n)"), "wv")
                load(bvw[:, :], t["bvwide"][g, :].rearrange("o n -> (o n)").partition_broadcast(P), "wv")

            def load_group_out(g):
                load(ww[:, 1536:2560], t["wwide"][g, :, 1536:2560].rearrange("o p n -> p (o n)"), "wo")

            x = t["x"].rearrange("(t p) d -> p t d", p=P)
            load(X[:, 0:2, :], x[:, 0:2, :], "x0")
            w = t["wqkvT"].rearrange("(c p) n -> p c n", p=P)
            load(wqkv[:, :, D:2 * D], w[:, :, D:2 * D], "k")
            load(bqk[:, :], t["bqk"], "bqk")
            load(wqkv[:, :, 0:D], w[:, :, 0:D], "q")
            load(wqkv[:, :, 2 * D:3 * D], w[:, :, 2 * D:3 * D], "v")
            load(bv[:, :], t["bv"].partition_broadcast(P), "bv")
            load(X[:, 2:TILES, :], x[:, 2:TILES, :], "x")
            load(cx[:, :], t["ctxT"], "ctx")
            spread_keys(0, 0)
            load(bout[:, :], t["bout"].partition_broadcast(P), "a0")
            load(wout[:, :, :], t["woutT"].rearrange("(c p) n -> p c n", p=P), "a0")
            load(wk[:, :], t["wkT"], "a0")
            load(bk[:, :], t["bk"].rearrange("(l o) -> l o", o=1), "a0")
            load(bkb[:, :], t["bk"].partition_broadcast(P), "x1")
            load(gam[:, :], t["gamma"].partition_broadcast(P), "x1")
            load(bet[:, :], t["beta"].partition_broadcast(P), "x1")
            load(raw[:, 0, :, :], t["wgT"].rearrange("(c p) n -> p c n", p=P), "f")
            load(raw[:, 1, :, :], t["wuT"].rearrange("(c p) n -> p c n", p=P), "f")
            for part in range(2):
                load(wd_raw[part], t["wdT"].rearrange("(c p) n -> p c n", p=P)[:, 4 * part:4 * part + 4, :], "f")
            spread_keys(0, 1)
            load(pes[:, :, :], t["pe"], "w")
            load(xq[:, :, :], t["xqT"].rearrange("(c p) n -> p c n", p=P), "x2")
            load(xkv[:, :], t["xkvT"], "x2")
            load(xo[:, :, :], t["xoT"].rearrange("(c p) n -> p c n", p=P), "x2")
            load(gw[:, :, :], t["gateT"].rearrange("(c p) n -> p c n", p=P), "e")
            load(eb[:, :], t["ebias"].partition_broadcast(P), "e")
            load_group_qk(slice(0, 1))
            load_group_v(slice(0, 1))
            load_group_out(slice(0, 1))
            for b in range(2, B):
                spread_keys(0, b)
            if stop > 3:
                with sp.Fori(1, G) as g:
                    sp.wait_ge(w_lo, g * 5)
                    sp.sem_inc(passed["sp"], 1)
                    load_group_qk(bass.ds(g, 1))
                    sp.wait_ge(wo_lo, g * 4)
                    sp.sem_inc(passed["sp"], 1)
                    load_group_out(bass.ds(g, 1))
                    sp.wait_ge(w_used, g)
                    sp.wait_ge(w_bias, g * 2 + START)
                    sp.sem_inc(passed["sp"], 1)
                    load_group_v(bass.ds(g, 1))
            if stop > 5:
                for s in range(2):
                    load(we[:, s, :], t["wexp"][s, :, :], f"exp{s}")
            if stop > 4:
                for b in range(B):
                    spread_keys(4, b)
            if stop > 5:
                with sp.Fori(1, E // 2) as i:
                    for s in range(2):
                        sp.wait_ge(gu_parts, i * 4 + (2 * s - 2))
                        sp.wait_ge(down_parts, i * 4 + (2 * s - 2))
                        sp.sem_inc(passed["sp"], 1)
                        load(we[:, s, :], t["wexp"][bass.ds(i * 2 + s, 1), :, :].rearrange("o p n -> p (o n)"), f"exp{s}")
                sp.wait_ge(gu_parts, 2 * E - 2)
                sp.wait_ge(down_parts, 2 * E - 2)
                load(we[:, 0, :], t["wexp"][E, :, :], "exp0")
            out = t["out"].rearrange("(t p) d -> p t d", p=P)
            for tiles, batches in ((slice(0, 4), 2), (slice(4, 6), 3), (slice(6, 8), 4)):
                sp.wait_ge(x_done[stop - 1], batches)
                sp.dma_start(out[:, tiles, :], X[:, tiles, :]).then_inc(stored, 16)
            sp.wait_ge(stored, 48)

        @block.gpsimd
        def _(pool):
            pool.sem_inc(normed.sem, AHEAD)
            pool.memset(ident[:, :], 0.0).then_inc(consts, 1)
            pool.wait_ge(consts, 1)
            pool.affine_select(out=ident[:, :], in_=ident[:, :], compare_op=ALU.not_equal, fill=1.0,
                               base=0, pattern=[[-1, P]], channel_multiplier=1).then_inc(consts, 1)
            pool.memset(kbd[:, :, 0, :, :].bitcast(F32), 0.0).then_inc(kbd_zeroed, 1)
            pool.memset(tri[:, :, :], 0.0).then_inc(consts, 1)
            pool.memset(mhalf[:, :], -0.5).then_inc(consts, 1)
            pool.iota(iota[:, :], pattern=[[1, E]], base=0, channel_multiplier=0,
                      allow_small_or_imprecise_dtypes=True).then_inc(consts, 1)
            pool.wait_ge(consts, 3)
            pool.affine_select(out=tri[:, :, :], in_=tri[:, :, :], compare_op=ALU.is_ge, fill=NEG,
                               base=0, pattern=[[0, 4], [-1, P]], channel_multiplier=1).then_inc(consts, 1)
            pool.tensor_copy(identb[:, :], ident[:, :]).then_inc(consts, 1)

            def norm(u0, u, kind):
                pool.wait_ge(recip.sem, recip.done(u0 + u))
                v = by_head(prob[:, u % N_P, :], kind)
                n = v.shape[1]
                pool.tensor_tensor(v, v, rinv[:, u % N_P, 0:n].unsqueeze(2).broadcast_to(list(v.shape)),
                                   ALU.mult).then_inc(normed.sem, 1)

            def ln_root(sub, b):
                pool.wait_ge(ln_step[sub], (b + 1) * LN_STEPS[sub])
                pool.tensor_tensor(rstd[:, b, :], veps[:, b, :], mhalf[:, 0:2], ALU.pow).then_inc(ln_rstd[sub], 1)

            def low_piece(piece, n, high_done, low_done):
                x, dst = piece
                pool.wait_ge(high_done, n + 1)
                pool.tensor_tensor(dst[:, 1], x, dst[:, 0], ALU.subtract).then_inc(low_done, 1)

            def parts(x, dst, k, sem_):
                high, low = (dst[:, w] for w in range(2))
                pool.tensor_copy(high, x).then_inc(sem_, 1)
                pool.wait_ge(sem_, k + 1)
                pool.tensor_tensor(low, x, high, ALU.subtract).then_inc(sem_, 1)

            def low_activations(sub, b, xt):
                bs = slice(b * S, (b + 1) * S)
                low_piece((XT[:, :, bs], xt[:, :, :, bs]), b, xt_hi[sub], xt_lo[sub])

            def split(e, s, cols, done):
                pool.sem_inc(passed["pool"], 1)
                parts(we[:, s, cols], wr[:, s, :, cols], 2 * e, done)

            GU, DOWN = slice(0, 2 * D), slice(2 * D, 3 * D)

            def low_part(low, x, high, which, sub, b):
                result(pool, which, sub, b)
                pool.tensor_tensor(low, x[:, :, :], high, ALU.subtract).then_inc(qk_low, 1)

            def background(sub, s):
                for b, o in tasks(sub, s):
                    if sub == 4 and o == -13:
                        ln_root(3, b)
                    if sub == 4 and b == 0 and o == -4:
                        for batch in range(B):
                            wide_full(pool, "last", G - 1, "out", batch)
                        for c in range(C):
                            pool.memset(kbd[:, 0, c, :, :].bitcast(F32), 0.0).then_inc(kbd_zeroed, 1)
                    if sub == 0 and o == 52 and stop > 3:
                        low_activations(0, b, xt_wide)
                    if o == -8:
                        low_part(kr[:, 1], kf, kr[:, 0], "k", sub, b)
                    if o == -7:
                        low_part(qr[:, b % 2, 1], qf, qr[:, b % 2, 0], "q", sub, b)
                        if sub == 0 and b == 0:
                            pool.memset(kbd[:, :, 1, :, :].bitcast(F32), 0.0).then_inc(kbd_zeroed, 1)
                    if o == 18:
                        ln_root(sub, b)
                    if sub == 4 and o == 22 and stop > 5:
                        low_activations(4, b, XTr)
                    if sub == 0 and stop > 1:
                        if o == 26:
                            pool.wait_ge(x1_step, 9 * b + 3)
                            pool.tensor_tensor(xrs[:, :], xve[:, :], mhalf[:, 0:2], ALU.pow).then_inc(x1_rstd, 1)
                        if o == 29:
                            ln_root(1, b)
                    if sub == 0 and stop > 2:
                        if o == 31:
                            pool.wait_ge(f_step, 11 * b + 3)
                            pool.tensor_tensor(frs[:, :], fve[:, :], mhalf[:, 0:2], ALU.pow).then_inc(f_rstd, 1)
                        if o == 48:
                            ln_root(2, b)
                if sub == 0 and stop > 3 and 54 <= s < 59:
                    low_piece(W_PIECES[s - 54], s - 54, w_hi, w_lo)
                if sub == 4 and stop > 5 and s in (16, 22, 28, 34):
                    k = (s - 16) // 6
                    if k % 2 == 0:
                        pool.wait_ge(ld[f"exp{k // 2}"], 16)
                    split(k // 2, k // 2, *((GU, gu_parts), (DOWN, down_parts))[k % 2])

            def stream(sub, start):
                for s in range(start, STEPS_END[sub]):
                    background(sub, s)
                    at = unit(sub, s - 1)
                    if at is not None:
                        norm(UNITS_AT[sub], s - 1, narrow_units[at[1]][1])
                    if sub == 0 and stop > 3 and s >= WIDE_FROM:
                        wide_step("first", 0, s - WIDE_FROM)

            def wide_step(phase, g, k):
                u = wide_unit(phase, k - 1)
                if u is not None:
                    norm(g * UW + UNITS_AT[3], u, wide_units[u][1])
                if 1 <= k < 5:
                    low_piece(WO_PIECES[k - 1], g * 4 + (k - 1), wo_hi, wo_lo)
                k -= SECOND_AT[phase] + 6
                if 0 <= k < 5 and phase != "last":
                    low_piece(W_PIECES[k], g * 5 + (5 + k), w_hi, w_lo)
                if k == 0 and phase == "last":
                    pool.wait_ge(w_used, G)
                    pool.memset(kbd[:, 1, :, :, :].bitcast(F32), 0.0).then_inc(low_zeroed, 1)

            stream(0, FIRST_STEP)
            if stop > 3:
                with pool.Fori(1, G - 1) as g:
                    for k in range(WIDE_STEPS["middle"]):
                        wide_step("middle", g, k)
                for k in range(WIDE_STEPS["last"]):
                    wide_step("last", G - 1, k)
                    if k >= FRONT_STEPS + FIRST_STEP and stop > 4:
                        background(4, k - FRONT_STEPS)
            if stop == 4:
                for b in range(B):
                    ln_root(3, b)
            if stop > 4:
                stream(4, WIDE_STEPS["last"] - FRONT_STEPS)
            if stop > 5:
                def split_gu(e, s):
                    pool.wait_ge(ld[f"exp{s}"], e * 8 + (16 - 8 * s))
                    pool.wait_ge(e_gu.sem, e_gu.done(e * 2 - 3))
                    split(e, s, GU, gu_parts)

                def split_down(e, s):
                    pool.wait_ge(gfull[1], down_k(e * 2 - 3) + 1)
                    split(e, s, DOWN, down_parts)

                with pool.Fori(1, E // 2) as i:
                    split_gu(i * 2, 0)
                    split_down(i * 2, 0)
                    split_gu(i * 2 + 1, 1)
                    split_down(i * 2 + 1, 1)
                split_gu(E, 0)
                split_down(E, 0)
                for b in range(B):
                    ln_root(5, b)

        @block.scalar
        def _(act):
            act.sem_inc(exped.sem, AHEAD)
            act.sem_inc(oread.sem, AHEAD)
            act.sem_inc(e_silu.sem, AHEAD)
            act.sem_inc(aw_hi.sem, AHEAD)
            act.sem_inc(e_hi.sem, AHEAD)
            act.sem_inc(w_bias, START)

            def exp_unit(u0, u, kind):
                act.wait_ge(maxed.sem, maxed.done(u0 + u))
                act.wait_ge(transp.sem, transp.free(u0 + u, N_P))
                src, dst = by_head(pS[u % 2][:, :], kind), by_head(prob[:, u % N_P, :], kind)
                for h in range(src.shape[1]):
                    e = act.activation(dst[:, h, :], src[:, h, :], ACT.Exp, bias=nmax[:, u % N_P, h:h + 1],
                                       accum_out=rsum[:, u % N_P, h:h + 1])
                e.then_inc(exped.sem, 1)

            def evacuate_out(sub, s):
                at = unit(sub, s)
                if at is None or at[1] % 6 != 5:
                    return
                b, k, u = at
                act.wait_ge(pved.sem, pved.done(u))
                if b >= 2:
                    full(act, "out", sub, b - 2)
                elif sub == 4:
                    full(act, "out", 0, b + 2)
                act.activation(an[:, b % 2, k // 6, :], pO[k // 6][:, 0:S], ACT.Copy).then_inc(oread.sem, 1)

            def queries_or_keys(sub, b, which):
                n = BATCHES_AT[sub] + b
                if sub == 4 and b < 2:
                    act.wait_ge(w_used, G)
                if which == "q":
                    if b >= 2:
                        act.wait_ge(score.sem, score.done(UNITS_AT[sub] + (b - 1) * UN - 1))
                    elif sub == 4:
                        act.wait_ge(score.sem, score.done(B * UN - 1))
                elif n > 0:
                    for hg in range(4):
                        act.wait_ge(k_spread[hg], 4 * 16 * n)
                if n > 0:
                    act.wait_ge(qk_low, 2 * n - (1 if which == "k" else 0))
                bank, g = full(act, which, sub, b)
                scale = HD ** -0.5 if which == "q" else 1.0
                for dst in (qf, qr[:, b % 2, 0]) if which == "q" else (kf, kr[:, 0]):
                    if sub == 0:
                        for m in range(2):
                            bias = bqs[:, m:m + 1] if which == "q" else bqk[:, 2 + m:3 + m]
                            a = act.activation(dst[:, m, :], bank[:, m * S:(m + 1) * S], ACT.Identity, bias=bias, scale=scale)
                    else:
                        a = act.activation(dst[:, :, :], bank[:, :].rearrange("p (m s) -> p m s", m=2), ACT.Copy, scale=scale)
                a.then_inc(gread[g], 1)

            def copy_xT(b, *key):
                bank, n = full(act, *key)
                act.activation(XT[:, :, b * S:(b + 1) * S], bank[:, :].rearrange("p (c s) -> p c s", c=C),
                               ACT.Copy).then_inc(gread[n], 1)

            def gated_softmax(b, o):
                if o == 19:
                    if b == 0:
                        act.wait_ge(ld["a0"], 64)
                    if b > 0:
                        full(act, "sim", b - 1)
                    bank, n = full(act, "kvT", b)
                    act.activation(kvT[:, :], bank[0:L, 0:S], ACT.Identity, bias=bk[:, 0:1]).then_inc(gread[n], 1)
                if o == 23:
                    bank, n = full(act, "ctx", b)
                    act.activation(oT[:, :], bank[0:L, 0:S], ACT.Copy, scale=D ** -0.5).then_inc(gread[n], 1)
                if o == 25:
                    if b > 0:
                        act.wait_ge(x1_step, 9 * b)
                    bank, n = full(act, "sim", b)
                    act.activation(z[:, :, :], bank[:, :].rearrange("p (t d) -> p t d", t=2), ACT.Copy).then_inc(gread[n], 1)
                if o == 28:
                    act.wait_ge(x1_step, 9 * b + 7)
                    for q in range(2):
                        e = act.activation(z[:, q, :], z[:, q, :], ACT.Exp, bias=xnm[:, q:q + 1],
                                           accum_out=xsm[:, q:q + 1])
                    e.then_inc(x1_exp, 1)

            def feed_forward(b, o):
                k = f_unit(o, 37)
                if k is not None:
                    v = 4 * b + k
                    if v >= 2:
                        result(act, "up", (v - 2) // 4, (v - 2) % 4)
                    bank, n = full(act, "gate", b, k)
                    act.activation(sg[:, k % 2, :], bank[:, :], ACT.Silu,
                                   scale=finv[:, k // 2:k // 2 + 1]).then_inc(gread[n], 1)
                k = f_unit(o, 40)
                if k is not None:
                    if k >= 2 or b > 0:
                        full(act, "down", *((b, 0) if k >= 2 else (b - 1, 1)))
                    bank, n = full(act, "prT", b, k)
                    act.activation(prT[:, k % 2, 0, :], bank[:, :], ACT.Copy).then_inc(f_hi, 1)

            def sign_weights(s):
                if s == 0:
                    act.wait_ge(ld["f"], 64)
                if s < 4:
                    act.activation(sgu[:, s // 2, s % 2, :], raw[:, s // 2, s % 2, :], ACT.Sign).then_inc(signs, 1)
                else:
                    part = slice(4 * (s - 4), 4 * (s - 3))
                    act.activation(wd[:, part, :], wd_raw[s - 4], ACT.Sign).then_inc(signs, 1)

            def silu_half(v, q):
                act.wait_ge(e_gu.sem, e_gu.done(v))
                act.wait_ge(e_h.sem, e_h.free(v, 2))
                act.activation(sg[:, q % 2, :], pS[q % 2][:, :], ACT.Silu).then_inc(e_silu.sem, 1)

            def hidden_high(v, q):
                act.wait_ge(e_h.sem, e_h.done(v))
                act.wait_ge(gfull[1], down_k(v - 4) + 1)
                act.activation(hid[:, q % 4, 0, :], pr[:, q % 2, :], ACT.Copy).then_inc(e_hi.sem, 1)

            def background(sub, s):
                for b, o in tasks(sub, s):
                    if o == -9:
                        queries_or_keys(sub, b, "k")
                    if o == -8:
                        queries_or_keys(sub, b, "q")
                    if sub == 0 and stop > 1:
                        gated_softmax(b, o)
                    if sub == 0 and stop > 2:
                        feed_forward(b, o)
                    if o == LAST_AT[sub] + 1 and stop > (3 if sub == 0 else 5):
                        copy_xT(b, "last", sub, b)
                    if o == LAST_AT[sub] + 2 and stop > (3 if sub == 0 else 5):
                        if sub == 0 and b == 0:
                            for hg in range(4):
                                act.wait_ge(k_spread[hg], 4 * 16 * B)
                        result(act, "last", sub, b)
                        bs = slice(b * S, (b + 1) * S)
                        act.activation((xt_wide if sub == 0 else XTr)[:, 0, :, bs], XT[:, :, bs],
                                       ACT.Copy).then_inc(xt_hi[sub], 1)
                if sub == 4 and stop > 5 and s == 55:
                    silu_half(0, 0)
                if sub == 4 and stop > 5 and s == 57:
                    hidden_high(0, 0)
                if sub == 0 and stop > 2 and 12 <= s < 18:
                    sign_weights(s - 12)
                if sub == 0 and stop > 3 and 53 <= s < 58:
                    if s == 53:
                        act.wait_ge(ld["wqk"], 32)
                    high_piece(W_PIECES[s - 53], w_hi)
                if sub == 0 and stop > 3 and s == 60:
                    act.wait_ge(ld["w"], 16)
                    bias_tables(0)

            def stream(sub, start):
                for s in range(start, STEPS_END[sub]):
                    background(sub, s)
                    at = unit(sub, s)
                    if at is not None:
                        exp_unit(UNITS_AT[sub], s, narrow_units[at[1]][1])
                    evacuate_out(sub, s - 5)
                    if sub == 0 and stop > 3 and s >= WIDE_FROM:
                        wide_step("first", 0, s - WIDE_FROM)

            def bias_tables(g):
                act.wait_ge(ld["wv"], g * 48 + 48)
                if not (isinstance(g, int) and g == 0):
                    act.wait_ge(w_used, g)
                act.activation(bws[:, :], bw[:, :], ACT.Copy, scale=DW ** -0.5).then_inc(w_bias, 1)
                act.wait_ge(w_bias, g * 2 + (START + 1))
                for h in range(QPG + 1):
                    bias = bws[:, h:h + 1] if h < QPG else bw[:, h:h + 1]
                    a = act.activation(peb[:, h, :], pes[:, h // QPG, :], ACT.Identity, bias=bias)
                a.then_inc(w_bias, 1)

            def high_piece(piece, done):
                x, dst = piece
                act.activation(dst[:, 0], x, ACT.Copy).then_inc(done, 1)

            def wide_step(phase, g, k):
                u0 = g * UW + UNITS_AT[3]
                if 1 <= k < 5:
                    if k == 1:
                        act.wait_ge(ld["wo"], g * 16 + 16)
                        for b in (B - 2, B - 1):
                            after_last_group(act, gfull, phase, g, "out", b)
                    high_piece(WO_PIECES[k - 1], wo_hi)
                p = k - SECOND_AT[phase] - 6
                if 0 <= p < 5 and phase != "last":
                    if p == 0:
                        act.wait_ge(ld["wqk"], g * 32 + 64)
                        act.wait_ge(w_used, g + 1)
                    high_piece(W_PIECES[p], w_hi)
                    if p == 3:
                        bias_tables(g + 1)
                u = wide_unit(phase, k)
                if u is not None:
                    exp_unit(u0, u, wide_units[u][1])
                u = wide_unit(phase, k - 5)
                if u is not None and u % 3 != 1:
                    act.wait_ge(pved.sem, pved.done(u0 + u))
                    b, half = u // 3, int(u % 3 > 0)
                    if b >= 2:
                        wide_full(act, phase, g, "out", b - 2)
                    else:
                        after_last_group(act, gfull, phase, g, "out", b + 2)
                    act.activation(aw[:, b % 2, :, half * P:half * P + P],
                                   pO[half][:, :].rearrange("p (h q) -> p h q", h=QPG),
                                   ACT.Copy).then_inc(aw_hi.sem, 1)

            act.wait_ge(ld["bqk"], 16)
            act.activation(bqs[:, :], bqk[:, 0:2], ACT.Copy, scale=HD ** -0.5).then_inc(bias_q, 1)
            act.wait_ge(bias_q, 1)
            stream(0, FIRST_STEP)
            if stop > 3:
                for b in (B - 2, B - 1):
                    wide_full(act, "first", 0, "out", b)
                with act.Fori(1, G - 1) as g:
                    for k in range(WIDE_STEPS["middle"]):
                        wide_step("middle", g, k)
                for k in range(WIDE_STEPS["last"]):
                    if k >= FRONT_STEPS + FIRST_STEP and stop > 4:
                        background(4, k - FRONT_STEPS)
                    wide_step("last", G - 1, k)
            if stop > 4:
                stream(4, WIDE_STEPS["last"] - FRONT_STEPS)
            if stop > 5:
                for n in (0, 1):
                    bank = g_wait(act, base[5][n], n)
                    act.activation(sc_[:, 4 * n:4 * (n + 1), :], bank[:, 0:4 * E].rearrange("p (t e) -> p t e", e=E),
                                   ACT.Sigmoid).then_inc(gread[n % 2], 1)

                silu_half(1, 1)
                with act.Fori(0, E // 2) as i:
                    for q in range(4):
                        silu_half(i * 4 + (q + 2), q + 2)
                        hidden_high(i * 4 + (q + 1), q + 1)
                hidden_high(2 * E + 1, 1)

        @block.vector
        def _(dve):
            for st in (maxed, recip, copied, e_h, e_lo):
                dve.sem_inc(st.sem, AHEAD)
            for st in gread:
                dve.sem_inc(st, START)
            dve.memset(vn[:, :, :, :, :], 0.0).then_inc(vn_zeroed, 1)

            def max_unit(u0, u, kind):
                dve.wait_ge(score.sem, score.done(u0 + u))
                v = by_head(pS[u % 2][:, :], kind)
                dve.reduce_max(nmax[:, u % N_P, 0:v.shape[1]], v, AX.X, negate=True).then_inc(maxed.sem, 1)

            def recip_unit(u0, u, kind):
                dve.wait_ge(exped.sem, exped.done(u0 + u))
                dve.wait_ge(normed.sem, normed.free(u0 + u, N_P))
                n = 4 if kind == "first" else 2
                dve.reciprocal(rinv[:, u % N_P, 0:n], rsum[:, u % N_P, 0:n]).then_inc(recip.sem, 1)

            def copy_unit(u0, u):
                dve.wait_ge(transp.sem, transp.done(u0 + u))
                dve.wait_ge(pved.sem, pved.free(u0 + u, N_PT))
                dve.tensor_copy(probT[:, u % N_PT, :], pT[:, :]).then_inc(copied.sem, 1)

            def ln_stats(sub, b):
                at = b * LN_STEPS[sub] + LN_STEPS[sub] - 3
                if sub > 0:
                    dve.wait_ge(x_done[sub - 1], b + 1)
                if at > 0:
                    dve.wait_ge(ln_step[sub], at)
                for q in range(2):
                    a = dve.bn_stats(stat[:, b, q, :], X[:, 2 * b + q, :])
                a.then_inc(ln_step[sub], 1)
                dve.wait_ge(ln_step[sub], at + 1)
                for q in range(2):
                    a = dve.bn_aggr(mv[:, b, q, :], stat[:, b, q, :])
                a.then_inc(ln_step[sub], 1)
                dve.wait_ge(ln_step[sub], at + 2)
                dve.tensor_scalar(veps[:, b, :], mv[:, b, :, 1], EPS_LN, None, ALU.add).then_inc(ln_step[sub], 1)

            def ln_apply(sub, b):
                dve.wait_ge(ln_rstd[sub], b + 1)
                for q in range(2):
                    a = dve.tensor_scalar(X[:, 2 * b + q, :], X[:, 2 * b + q, :], mv[:, b, q, 0:1], rstd[:, b, q:q + 1],
                                          ALU.subtract, ALU.mult)
                a.then_inc(x_done[sub], 1)

            def add_out(sub, b):
                if sub == 0 and b == 0:
                    dve.wait_ge(ld["a0"], 64)
                    dve.wait_ge(ld["x1"], 48)
                bank, n = full(dve, "out", sub, b)
                xb = X[:, 2 * b:2 * b + 2, :]
                dve.tensor_tensor(xb, bank[:, :].rearrange("p (t d) -> p t d", t=2), xb, ALU.add).then_inc(gread[n], 1)
                result(dve, "out", sub, b)
                if sub == 0:
                    dve.tensor_tensor(xb, xb, bout[:, :].unsqueeze(1).broadcast_to([P, 2, D]),
                                      ALU.add).then_inc(ln_step[0], 1)
                ln_stats(sub, b)

            def copy_xT(b, *key):
                bank, n = full(dve, *key)
                dve.tensor_copy(XT[:, :, b * S:(b + 1) * S],
                                bank[:, :].rearrange("p (c s) -> p c s", c=C)).then_inc(gread[n], 1)

            def values(sub, b):
                if b >= 2:
                    dve.wait_ge(pved.sem, pved.done(UNITS_AT[sub] + (b - 1) * UN - 1))
                elif sub == 4:
                    dve.wait_ge(pved.sem, pved.done(B * UN - 1))
                dve.wait_ge(vn_zeroed, 1)
                if sub == 0 and b == 0:
                    dve.wait_ge(ld["bv"], 16)
                bank, n = full(dve, "v", sub, b)
                src = bank[:, :].rearrange("p (t s e d) -> p t s e d", t=2, e=2, d=HD)
                for q in range(2):
                    for e in range(2):
                        dst = vn[:, b % 2, q, e::2, e * HD:(e + 1) * HD]
                        if sub == 0:
                            bias = bv[:, :].rearrange("p (s e d) -> p s e d", e=2, d=HD)[:, :, e, :]
                            a = dve.tensor_tensor(dst, src[:, q, :, e, :], bias, ALU.add)
                        else:
                            a = dve.tensor_copy(dst, src[:, q, :, e, :])
                a.then_inc(gread[n], 1)

            def gated_softmax(b, o):
                at = 9 * b
                if o == 19:
                    if b > 0:
                        full(dve, "ctx", b - 1)
                    bank, n = full(dve, "kv", b)
                    dve.tensor_tensor(kv[:, :, :], bank[:, 0:2 * L].rearrange("p (t d) -> p t d", d=L),
                                      bkb[:, :].unsqueeze(1).broadcast_to([P, 2, L]), ALU.add).then_inc(gread[n], 1)
                if o == 21:
                    copy_xT(b, "x1T", b)
                if o == 26:
                    result(dve, "sim", b)
                    if b > 0:
                        dve.wait_ge(x1_step, at)
                    for q in range(2):
                        a = dve.bn_stats(xst[:, q, :], z[:, q, :])
                    a.then_inc(x1_step, 1)
                    dve.wait_ge(x1_step, at + 1)
                    for q in range(2):
                        a = dve.bn_aggr(xmv[:, q, :], xst[:, q, :])
                    a.then_inc(x1_step, 1)
                    dve.wait_ge(x1_step, at + 2)
                    dve.tensor_scalar(xve[:, :], xmv[:, :, 1], EPS_X, None, ALU.add).then_inc(x1_step, 1)
                if o == 27:
                    dve.wait_ge(x1_rstd, b + 1)
                    for q in range(2):
                        a = dve.tensor_scalar(z[:, q, :], z[:, q, :], xmv[:, q, 0:1], xrs[:, q:q + 1],
                                              ALU.subtract, ALU.mult)
                    a.then_inc(x1_step, 1)
                    dve.wait_ge(x1_step, at + 4)
                    dve.tensor_tensor(z[:, :, :], z[:, :, :], gam[:, :].unsqueeze(1).broadcast_to([P, 2, D]),
                                      ALU.mult).then_inc(x1_step, 1)
                    dve.wait_ge(x1_step, at + 5)
                    dve.tensor_tensor(z[:, :, :], z[:, :, :], bet[:, :].unsqueeze(1).broadcast_to([P, 2, D]),
                                      ALU.add).then_inc(x1_step, 1)
                    dve.wait_ge(x1_step, at + 6)
                    dve.reduce_max(xnm[:, :], z[:, :, :], AX.X, negate=True).then_inc(x1_step, 1)
                if o == 29:
                    dve.wait_ge(x1_exp, b + 1)
                    dve.reciprocal(xri[:, :], xsm[:, :]).then_inc(x1_step, 1)
                    dve.wait_ge(x1_step, at + 8)
                    for q in range(2):
                        a = dve.scalar_tensor_tensor(X[:, 2 * b + q, :], z[:, q, :], xri[:, q:q + 1],
                                                     X[:, 2 * b + q, :], ALU.mult, ALU.add)
                    a.then_inc(x1_step, 1)
                    dve.wait_ge(x1_step, at + 9)
                    ln_stats(1, b)
                if o == 30:
                    ln_apply(1, b)

            def feed_forward(b, o):
                at = 11 * b
                if o == 31:
                    dve.wait_ge(x_done[1], b + 1)
                    if b > 0:
                        dve.wait_ge(f_step, at)
                    for q in range(2):
                        a = dve.bn_stats(fst[:, q, :], X[:, 2 * b + q, :])
                    a.then_inc(f_step, 1)
                    dve.wait_ge(f_step, at + 1)
                    for q in range(2):
                        a = dve.bn_aggr(fmv[:, q, :], fst[:, q, :])
                    a.then_inc(f_step, 1)
                    dve.wait_ge(f_step, at + 2)
                    dve.tensor_scalar(fve[:, :], fmv[:, :, 1], EPS_F, None, ALU.add).then_inc(f_step, 1)
                if o == 32:
                    dve.wait_ge(f_rstd, b + 1)
                    for q in range(2):
                        a = dve.tensor_scalar(xn[:, q, :], X[:, 2 * b + q, :], fmv[:, q, 0:1], frs[:, q:q + 1],
                                              ALU.subtract, ALU.mult)
                    a.then_inc(f_step, 1)
                    dve.wait_ge(f_step, at + 4)
                    dve.reduce_max(amax[:, :], xn[:, :, :], AX.X, apply_absolute_value=True).then_inc(f_step, 1)
                    dve.wait_ge(f_step, at + 5)
                    dve.reciprocal(fsc[:, :], amax[:, :]).then_inc(f_step, 1)
                    if b > 0:
                        result(dve, "up", b - 1, 3)
                    dve.tensor_scalar(finv[:, :], amax[:, :], 1.0 / 127.0, None, ALU.mult).then_inc(f_step, 1)
                    dve.wait_ge(f_step, at + 7)
                    dve.tensor_scalar(fsc[:, :], fsc[:, :], 127.0, None, ALU.mult).then_inc(f_step, 1)
                if o == 33:
                    dve.wait_ge(f_step, at + 8)
                    for q in range(2):
                        a = dve.tensor_scalar(xn[:, q, :], xn[:, q, :], fsc[:, q:q + 1], ROUND, ALU.mult, ALU.add)
                    a.then_inc(f_step, 1)
                    dve.wait_ge(f_step, at + 9)
                    dve.tensor_scalar(xn[:, :, :], xn[:, :, :], ROUND, 127.0, ALU.subtract, ALU.min).then_inc(f_step, 1)
                    dve.wait_ge(f_step, at + 10)
                    dve.tensor_scalar(xn[:, :, :], xn[:, :, :], -128.0, None, ALU.max).then_inc(f_step, 1)
                if o == 35:
                    bank, n = full(dve, "qT", b)
                    dve.tensor_copy(qT[:, :, :], bank[:, :].rearrange("p (c s) -> p c s", c=C)).then_inc(gread[n], 1)
                k = f_unit(o, 38)
                if k is not None:
                    v = 4 * b + k
                    result(dve, "gate", b, k)
                    if v >= 2:
                        full(dve, "prT", (v - 2) // 4, (v - 2) % 4)
                    bank, n = full(dve, "up", b, k)
                    dve.scalar_tensor_tensor(pr[:, k % 2, :], bank[:, :], finv[:, k // 2:k // 2 + 1],
                                             sg[:, k % 2, :], ALU.mult, ALU.mult).then_inc(gread[n], 1)
                k = f_unit(o, 41)
                if k is not None:
                    bank, n = full(dve, "prT", b, k)
                    dve.wait_ge(f_hi, 4 * b + k + 1)
                    dve.tensor_tensor(prT[:, k % 2, 1, :], bank[:, :], prT[:, k % 2, 0, :],
                                      ALU.subtract).then_inc(gread[n], 1)
                if o in (44, 48):
                    q = (o - 44) // 4
                    bank, n = full(dve, "down", b, q)
                    dve.tensor_tensor(X[:, 2 * b + q, :], bank[:, 0:D], X[:, 2 * b + q, :], ALU.add).then_inc(gread[n], 1)
                    if q == 1:
                        for w in range(2):
                            result(dve, "down", b, w)
                        ln_stats(2, b)
                if o == 49:
                    ln_apply(2, b)

            def hidden(v, q):
                dve.wait_ge(e_silu.sem, e_silu.done(v))
                dve.wait_ge(e_hi.sem, e_hi.free(v, 2))
                dve.wait_ge(e_lo.sem, e_lo.free(v, 2))
                dve.tensor_tensor(pr[:, q % 2, :], (pT, pG[2])[q % 2][:, :], sg[:, q % 2, :], ALU.mult).then_inc(e_h.sem, 1)

            def hidden_low(v, q):
                dve.wait_ge(e_h.sem, e_h.done(v))
                dve.wait_ge(e_hi.sem, e_hi.done(v))
                dve.tensor_tensor(hid[:, q % 4, 1, :], pr[:, q % 2, :], hid[:, q % 4, 0, :], ALU.subtract).then_inc(e_lo.sem, 1)

            def background(sub, s):
                for b, o in tasks(sub, s):
                    if sub == 4 and o == -13:
                        wide_read(dve, "last", G - 1, "out", b)
                        ln_stats(3, b)
                    if sub == 4 and o == -12:
                        ln_apply(3, b)
                    if o == -10:
                        copy_xT(b, "xT", sub, b)
                    if o == -7:
                        values(sub, b)
                    if o == 18:
                        add_out(sub, b)
                    if o == 19:
                        ln_apply(sub, b)
                    if sub == 0 and stop > 1:
                        gated_softmax(b, o)
                    if sub == 0 and stop > 2:
                        feed_forward(b, o)
                if sub == 4 and stop > 5 and s == 56:
                    hidden(0, 0)
                if sub == 4 and stop > 5 and s == 58:
                    hidden_low(0, 0)
                if sub == 0 and stop > 3 and WIDE_AT < s <= WIDE_AT + QPG + 2:
                    n = s - 1 - WIDE_AT
                    if n == 0:
                        dve.wait_ge(w_bias, START + 2)
                        dve.wait_ge(signs, 6)
                    bank, g = full(dve, "wide", n)
                    wide_result(bank, 0, n).then_inc(gread[g], 1)

            def stream(sub, start):
                for s in range(start, STEPS_END[sub]):
                    background(sub, s)
                    at = unit(sub, s)
                    if at is not None:
                        max_unit(UNITS_AT[sub], s, narrow_units[at[1]][1])
                    at = unit(sub, s - 1)
                    if at is not None:
                        recip_unit(UNITS_AT[sub], s - 1, narrow_units[at[1]][1])
                    if unit(sub, s - 3) is not None:
                        copy_unit(UNITS_AT[sub], s - 3)
                    if sub == 0 and stop > 3 and s >= WIDE_FROM:
                        wide_step("first", 0, s - WIDE_FROM)

            def wide_step(phase, g, k):
                u0, o0 = g * UW + UNITS_AT[3], g * 8 + OUTS_AT[3]
                if k == 0 and phase == "last":
                    for n in range(2):
                        dve.wait_ge(gread[n], gk(3, g, n))

                def results(wanted):
                    for what, m in wide_projection(phase, k - 1):
                        if what != wanted:
                            continue
                        if (what, m) == ("second", 0) and phase != "first":
                            dve.wait_ge(score.sem, score.done(u0 - 1))
                            dve.wait_ge(pved.sem, pved.done(u0 - 1))
                        if (what, m) == ("first", 0):
                            dve.wait_ge(w_bias, g * 2 + (START + 4))
                            dve.wait_ge(score.sem, score.done(u0 + (UW // 2 - 1)))
                            dve.wait_ge(pved.sem, pved.done(u0 + (UW // 2 - 1)))
                        bank, n = wide_full(dve, phase, g, what, m)
                        wide_result(bank, 1 if what == "second" else 0, m).then_inc(gread[n], 1)

                results("second")
                if k == SECOND_AT[phase] + 6:
                    for m in range(QPG + 2):
                        wide_read(dve, phase, g, "second", m)
                    dve.sem_inc(w_used, 1)
                u = wide_unit(phase, k - 6)
                if u is not None and u % 3 != 1:
                    b, half = u // 3, int(u % 3 > 0)
                    dve.wait_ge(aw_hi.sem, aw_hi.done(g * 8 + (2 * b + half)))
                    cols = slice(half * P, (half + 1) * P)
                    dve.tensor_tensor(aw_low[:, b % 2, :, cols], pO[half][:, :].rearrange("p (h q) -> p h q", h=QPG),
                                      aw[:, b % 2, :, cols], ALU.subtract).then_inc(oread.sem, 1)
                u = wide_unit(phase, k)
                if u is not None:
                    max_unit(u0, u, wide_units[u][1])
                u = wide_unit(phase, k - 1)
                if u is not None:
                    recip_unit(u0, u, wide_units[u][1])
                u = wide_unit(phase, k - 3)
                if u is not None:
                    copy_unit(u0, u)
                results("first")
                b = wide_out(phase, k - 1)
                if b is not None:
                    bank, n = wide_full(dve, phase, g, "out", b)
                    if phase == "middle":
                        dve.wait_ge(gread[n], wide_use(phase, g, "out", b)[1])
                    xb = X[:, 2 * b:2 * b + 2, :]
                    dve.tensor_tensor(xb, bank[:, :].rearrange("p (t d) -> p t d", t=2), xb, ALU.add).then_inc(gread[n], 1)

            def wide_result(bank, half, n):
                b512 = bank[:, :].rearrange("p (b s) -> p b s", b=2)
                cols = slice(half * 512, (half + 1) * 512)
                if n < QPG:
                    return dve.scalar_tensor_tensor(qw[:, n, cols].rearrange("p (b s) -> p b s", b=2), b512, DW ** -0.5,
                                                    peb[:, n, :].unsqueeze(1).broadcast_to([P, 2, S]), ALU.mult, ALU.add)
                if n == QPG:
                    return dve.tensor_tensor(kw[:, cols].rearrange("p (b s) -> p b s", b=2), b512,
                                             peb[:, QPG, :].unsqueeze(1).broadcast_to([P, 2, S]), ALU.add)
                return dve.tensor_tensor(vw[:, 4 * half:4 * half + 4, :], bank[:, :].rearrange("p (t d) -> p t d", t=4),
                                         bvw[:, :].unsqueeze(1).broadcast_to([P, 4, DW]), ALU.add)

            stream(0, FIRST_STEP)
            if stop > 3:
                for b in range(B):
                    wide_read(dve, "first", 0, "out", b)
                with dve.Fori(1, G - 1) as g:
                    for k in range(WIDE_STEPS["middle"]):
                        wide_step("middle", g, k)
                for k in range(WIDE_STEPS["last"]):
                    if k >= FRONT_STEPS + FIRST_STEP and stop > 4:
                        background(4, k - FRONT_STEPS)
                    wide_step("last", G - 1, k)
            if stop == 4:
                for b in range(B):
                    wide_read(dve, "last", G - 1, "out", b)
                    ln_stats(3, b)
                    ln_apply(3, b)
            if stop > 4:
                stream(4, WIDE_STEPS["last"] - FRONT_STEPS)
            if stop > 5:
                dve.wait_ge(ld["e"], 32)
                for n in (0, 1):
                    g_result(dve, base[5][n], n)
                wide = [P, TILES, E]
                dve.tensor_tensor(sel[:, :, :], sc_[:, :, :], eb[:, :].unsqueeze(1).broadcast_to(wide), ALU.add).then_inc(e_step, 1)
                dve.wait_ge(e_step, 1)
                for q in range(TILES):
                    a = dve.max(top[:, q, :], sel[:, q, :])
                a.then_inc(e_step, 1)
                dve.wait_ge(e_step, 2)
                for q in range(TILES):
                    a = dve.max_index(topi[:, q, :], top[:, q, :], sel[:, q, :])
                a.then_inc(e_step, 1)
                dve.wait_ge(e_step, 3)
                dve.tensor_copy(topf[:, :, :], topi[:, :, :]).then_inc(e_step, 1)
                dve.wait_ge(e_step, 4)
                dve.wait_ge(consts, 7)
                for q in range(TOPK):
                    a = dve.tensor_tensor(eq[:, :, q, :], iota[:, :].unsqueeze(1).broadcast_to(wide),
                                          topf[:, :, q:q + 1].broadcast_to(wide), ALU.is_equal)
                a.then_inc(e_step, 1)
                dve.wait_ge(e_step, 5)
                dve.tensor_reduce(pick[:, :, :], eq[:, :, :, :].rearrange("p t k e -> p t e k"), AX.X, ALU.add).then_inc(e_step, 1)
                dve.wait_ge(e_step, 6)
                dve.tensor_tensor(cws[:, :, :], pick[:, :, :], sc_[:, :, :], ALU.mult).then_inc(e_step, 1)
                dve.wait_ge(e_step, 7)
                dve.tensor_reduce(csum[:, :], cws[:, :, :], AX.X, ALU.add).then_inc(e_step, 1)
                dve.wait_ge(e_step, 8)
                dve.reciprocal(cinv[:, :], csum[:, :]).then_inc(e_step, 1)
                dve.wait_ge(e_step, 9)
                dve.tensor_tensor(cw[:, :, 0:E], cws[:, :, :], cinv[:, :].unsqueeze(2).broadcast_to(wide), ALU.mult).then_inc(e_step, 1)
                dve.memset(cw[:, :, E:E + 1], 1.0).then_inc(e_step, 1)
                dve.wait_ge(e_step, 11)

                def combine(v, q):
                    for n in range(2):
                        bank = g_wait(dve, down_k(v, n), n)
                        dve.wait_ge(gread[n], down_k(v, n))
                        for w in range(2):
                            tile = 4 * (q % 2) + 2 * n + w
                            a = dve.scalar_tensor_tensor(X[:, tile, :], bank[:, w * D:(w + 1) * D],
                                                         cwe[:, (q // 2) % 2, tile:tile + 1], X[:, tile, :],
                                                         ALU.mult, ALU.add)
                        a.then_inc(gread[n], 1)

                def expert_weights(e, s):
                    return dve.tensor_copy(cwe[:, s, :], cw[:, :, e].rearrange("p t o -> p (t o)"))

                hidden(1, 1)
                with dve.Fori(0, E // 2) as i:
                    dve.wait_ge(gread[1], down_k(i * 4))
                    for s in range(2):
                        a = expert_weights(bass.ds(i * 2 + s, 1), s)
                    a.then_inc(e_cw, 1)
                    dve.wait_ge(e_cw, i + 1)
                    for q in range(4):
                        hidden(i * 4 + (q + 2), q + 2)
                        hidden_low(i * 4 + (q + 1), q + 1)
                        combine(i * 4 + q, q)
                hidden_low(2 * E + 1, 1)
                dve.wait_ge(gread[1], down_k(2 * E))
                expert_weights(slice(E, E + 1), 0).then_inc(e_cw, 1)
                dve.wait_ge(e_cw, E // 2 + 1)
                for q in range(2):
                    combine(2 * E + q, q)
                    for n in range(2):
                        g_result(dve, down_k(2 * E + q, n), n)
                    for b in (2 * q, 2 * q + 1):
                        ln_stats(5, b)
                    for b in (2 * q, 2 * q + 1):
                        ln_apply(5, b)


def position_table():
    pos = np.arange(S, dtype=np.float32)[:, None]
    i = np.arange(0, DW, 2, dtype=np.float32)
    ang = pos * np.exp(-(np.log(np.float32(10000.0)) * i / np.float32(DW))).astype(np.float32)
    pe = np.zeros((S, DW), np.float32)
    pe[:, 0::2] = np.sin(ang)
    pe[:, 1::2] = np.cos(ang)
    return np.ascontiguousarray(np.stack([pe.T * np.float32(DW ** -0.5), pe.T], axis=1))


def layouts(a):
    wq = a["L1_attn_wq"].reshape(C, P, G, 512).transpose(2, 1, 0, 3).reshape(G, P, 1024)
    wkv = a["L1_attn_wkv"].reshape(C, P, G, 256).transpose(2, 1, 0, 3).reshape(G, P, 512)
    wo = a["L1_attn_wo"].reshape(G, QPG, P, D).transpose(0, 2, 1, 3).reshape(G, P, 1024)
    bkv = a["L1_attn_bkv"].reshape(G, 2, P)
    bq = a["L1_attn_bq"].reshape(G, QPG, P).transpose(0, 2, 1)

    def expert(wg, wu, wd):
        n = wg.shape[0]
        up = [w.reshape(n, I, C, P).transpose(0, 3, 2, 1).reshape(n, P, C * I) for w in (wg, wu)]
        return np.concatenate([*up, wd.transpose(0, 2, 1)], axis=2)

    shared = expert(a["L1_ffn_sw_gate"][None], a["L1_ffn_sw_up"][None], a["L1_ffn_sw_down"][None])
    out = {
        "x": a["x"].reshape(B * S, D),
        "ctxT": a["ctx_512"].reshape(B * S, L).T,
        "wqkvT": a["L0_attn_Wqkv"].T,
        "bqk": a["L0_attn_bqkv"][:2 * D].reshape(4, P).T,
        "bv": a["L0_attn_bqkv"][2 * D:],
        "woutT": a["L0_attn_Wout"].T,
        "bout": a["L0_attn_bout"],
        "wkT": a["L0_xattn_W_k"].T,
        "bk": a["L0_xattn_b_k"],
        "gamma": a["L0_xattn_ln_gamma"],
        "beta": a["L0_xattn_ln_beta"],
        "wgT": a["L0_ffn_W_g"].T,
        "wuT": a["L0_ffn_W_u"].T,
        "wdT": a["L0_ffn_W_d"].T,
        "wwide": np.concatenate([wq, wkv, wo], axis=2),
        "bwide": np.concatenate([bq, bkv[:, 0, :, None], np.zeros((G, P, 3), np.float32)], axis=2),
        "bvwide": bkv[:, 1, :],
        "pe": position_table(),
        "xqT": a["L1_xattn_Wq"].T,
        "xkvT": a["L1_xattn_Wkv_expand"].T,
        "xoT": a["L1_xattn_Wout"].T,
        "gateT": a["L1_ffn_gate_w"].T,
        "ebias": a["L1_ffn_expert_bias"],
        "wexp": np.concatenate([expert(a["L1_ffn_w_gate"], a["L1_ffn_w_up"], a["L1_ffn_w_down"]), shared]),
    }
    return {k: np.ascontiguousarray(v) for k, v in out.items()}


def kernel(**inputs):
    from concourse import bacc
    from concourse.bass_utils import run_bass_kernel_spmd as run

    arrays = layouts({k: np.asarray(v) for k, v in inputs.items()})
    nc = bacc.Bacc("TRN2", target_bir_lowering=False, num_devices=1)
    t = {k: nc.dram_tensor(f"in_{k}", v.shape, mybir.dt.from_np(v.dtype), kind="ExternalInput").ap()
         for k, v in arrays.items()}
    t["out"] = nc.dram_tensor("out", (B * S, D), F32, kind="ExternalOutput").ap()
    build(nc, t)
    res = run(nc, [{f"in_{k}": v for k, v in arrays.items()}], core_ids=[0])
    return res.results[0]["out"].reshape(B, S, D)
```
